# Optimizing a Trainium2 kernel written in Bass

```python
import numpy as np
import jax
import jax.numpy as jnp

def _softmax(x, axis=-1):
    return jax.nn.softmax(x, axis=axis)

def _gelu(x):
    return jax.nn.gelu(x, approximate=True)

def _silu(x):
    return jax.nn.silu(x)

def _sigmoid(x):
    return jax.nn.sigmoid(x)

def _layernorm(x, axis=-1, eps=1e-05):
    m = jnp.mean(x, axis=axis, keepdims=True)
    v = jnp.var(x, axis=axis, keepdims=True)
    return (x - m) / jnp.sqrt(v + eps)

def _scatter_add(tgt, idx, src, axis=0):
    return tgt.at[idx].add(src)

def _segment_sum(src, seg, n):
    return jax.ops.segment_sum(src, seg, n)
kernel_name = 'mk_gnn_resnorm_d4_gnn_r16_7f1e6d'

def setup_inputs(seed: int=0):
    np.random.seed(seed)
    _w = jnp.asarray

    def _rec_inputs():
        import jax
        import jax.numpy as jnp
        _gk = jax.random.key(seed)
        x = -0.0003713 + 1 * jax.random.normal(jax.random.fold_in(_gk, 1), (3125, 256), jnp.float32)
        _s = jax.random.randint(jax.random.fold_in(_gk, 2), (50000,), 0, 3125, jnp.int32)
        _d = jax.random.randint(jax.random.fold_in(_gk, 3), (50000,), 0, 3125, jnp.int32)
        _loop = jnp.arange(3125, dtype=jnp.int32)
        src = jnp.concatenate([_s, _d, _loop])
        dst = jnp.concatenate([_d, _s, _loop])
        _o = jnp.argsort(dst, stable=True)
        src = src[_o]
        dst = dst[_o]
        edge_type_32 = jax.random.randint(jax.random.fold_in(_gk, 13), (103125,), 0, 32, jnp.int32)
        edge_weight = jax.random.uniform(jax.random.fold_in(_gk, 14), (103125,), jnp.float32, 0.0, 0.999998)
        edge_weight1 = jax.random.uniform(jax.random.fold_in(_gk, 15), (103125, 1), jnp.float32, 0.0, 0.999998)
        node_vec = jax.random.uniform(jax.random.fold_in(_gk, 16), (3125,), jnp.float32, 0.0, 0.999833)
        return (x, src, dst, edge_type_32, edge_weight, edge_weight1, node_vec)
    x, src, dst, edge_type_32, edge_weight, edge_weight1, node_vec = _rec_inputs()

    def _L0_gnn_setup():
        import jax, jax.numpy as jnp
        import numpy as np
        N, HID, HEADS = (3125, 256, 8)
        D = HID // HEADS
        E = 50000

        def _gnn_layer(x, edge_index, Wq, bq, Wk, bk, Wv, bv, Wskip, bskip, gamma, beta):
            n = x.shape[0]
            src, dst = (edge_index[0], edge_index[1])
            q = (x @ Wq + bq).reshape(n, HEADS, D)
            k = (x @ Wk + bk).reshape(n, HEADS, D)
            v = (x @ Wv + bv).reshape(n, HEADS, D)
            logits = jnp.einsum('ehd,ehd->eh', q[dst], k[src]) / jnp.sqrt(jnp.float32(D))
            seg_max = jax.ops.segment_max(logits, dst, num_segments=n)
            expv = jnp.exp(logits - seg_max[dst])
            denom = jax.ops.segment_sum(expv, dst, num_segments=n)
            attn = expv / denom[dst]
            agg = jax.ops.segment_sum(attn[:, :, None] * v[src], dst, num_segments=n)
            out = agg.reshape(n, HID) + (x @ Wskip + bskip)
            h = jax.nn.gelu(out, approximate=False)
            y = x + h
            mu = jnp.mean(y, axis=-1, keepdims=True)
            var = jnp.var(y, axis=-1, keepdims=True)
            return (y - mu) / jnp.sqrt(var + 1e-05) * gamma + beta
        key = jax.random.key(seed)
        ks = jax.random.split(key, 12)
        s = 0.02
        x = jax.random.normal(ks[0], (N, HID), dtype=jnp.float32)
        edge_index = jax.random.randint(ks[1], (2, E), 0, N, dtype=jnp.int64)
        Wq = jax.random.normal(ks[2], (HID, HID), dtype=jnp.float32) * s
        bq = jnp.zeros((HID,), dtype=jnp.float32)
        Wk = jax.random.normal(ks[3], (HID, HID), dtype=jnp.float32) * s
        bk = jnp.zeros((HID,), dtype=jnp.float32)
        Wv = jax.random.normal(ks[4], (HID, HID), dtype=jnp.float32) * s
        bv = jnp.zeros((HID,), dtype=jnp.float32)
        Wskip = jax.random.normal(ks[5], (HID, HID), dtype=jnp.float32) * s
        bskip = jnp.zeros((HID,), dtype=jnp.float32)
        gamma = jnp.ones((HID,), dtype=jnp.float32)
        beta = jnp.zeros((HID,), dtype=jnp.float32)
        return {'x': x, 'edge_index': edge_index, 'Wq': Wq, 'bq': bq, 'Wk': Wk, 'bk': bk, 'Wv': Wv, 'bv': bv, 'Wskip': Wskip, 'bskip': bskip, 'gamma': gamma, 'beta': beta}
    _L0_gnn_all = _L0_gnn_setup()
    _L0_gnn_in = {k: v for k, v in _L0_gnn_all.items() if k in ('Wq', 'bq', 'Wk', 'bk', 'Wv', 'bv', 'Wskip', 'bskip', 'gamma', 'beta')}
    del _L0_gnn_all

    def _L1_gnn_setup():
        import jax, jax.numpy as jnp
        import numpy as np
        N_NODES = 1250
        N_EDGES = 20000
        IN_DIM = 256
        OUT_DIM = 256
        NUM_RELS = 32
        NUM_BASES = 8
        key = jax.random.key(seed)
        k1, k2, k3, k4, k5, k6, k7 = jax.random.split(key, 7)
        h = jax.random.normal(k1, (N_NODES, IN_DIM), dtype=jnp.float32)
        src = jax.random.randint(k2, (N_EDGES,), 0, N_NODES, dtype=jnp.int32)
        dst = jax.random.randint(k3, (N_EDGES,), 0, N_NODES, dtype=jnp.int32)
        rel_type = jax.random.randint(k4, (N_EDGES,), 0, NUM_RELS, dtype=jnp.int32)
        norm = jax.random.uniform(k5, (N_EDGES, 1), dtype=jnp.float32)
        scale_w = np.sqrt(2.0) * np.sqrt(6.0 / (IN_DIM + OUT_DIM))
        bases = jax.random.uniform(k6, (NUM_BASES, IN_DIM, OUT_DIM), dtype=jnp.float32, minval=-scale_w, maxval=scale_w)
        scale_c = np.sqrt(2.0) * np.sqrt(6.0 / (NUM_RELS + NUM_BASES))
        w_comp = jax.random.uniform(k7, (NUM_RELS, NUM_BASES), dtype=jnp.float32, minval=-scale_c, maxval=scale_c)
        return {'h': h, 'src': src, 'dst': dst, 'rel_type': rel_type, 'norm': norm, 'bases': bases, 'w_comp': w_comp}
    _L1_gnn_all = _L1_gnn_setup()
    _L1_gnn_in = {k: v for k, v in _L1_gnn_all.items() if k in ('bases', 'w_comp')}
    del _L1_gnn_all

    def _L2_gnn_setup():
        import jax, jax.numpy as jnp
        import numpy as np
        N = 1250
        E = 20000
        IN = 256
        HID = 256
        OUT = 256
        H1 = 8
        D1 = HID // H1
        H2 = 1

        def gat_conv(h, src, dst, fc_w, attn_l, attn_r, bias, heads, out_feats):
            n = h.shape[0]
            feat = (h @ fc_w.T).reshape(n, heads, out_feats)
            el = jnp.sum(feat * attn_l, axis=-1)
            er = jnp.sum(feat * attn_r, axis=-1)
            e = jax.nn.leaky_relu(el[src] + er[dst], 0.2)
            m = jax.ops.segment_max(e, dst, num_segments=n)
            m = jnp.where(jnp.isfinite(m), m, 0.0)
            ex = jnp.exp(e - m[dst])
            ssum = jax.ops.segment_sum(ex, dst, num_segments=n)
            a = ex / ssum[dst]
            rst = jax.ops.segment_sum(feat[src] * a[..., None], dst, num_segments=n)
            return rst + bias.reshape(heads, out_feats)
        key = jax.random.key(seed)
        ks = jax.random.split(key, 16)
        s = 0.05
        inputs = jax.random.normal(ks[0], (N, IN), jnp.float32)
        src = jax.random.randint(ks[1], (E,), 0, N, jnp.int32)
        dst = jax.random.randint(ks[2], (E,), 0, N, jnp.int32)
        return {'inputs': inputs, 'src': src, 'dst': dst, 'fc1_w': jax.random.normal(ks[3], (H1 * D1, IN), jnp.float32) * s, 'attn_l1': jax.random.normal(ks[4], (H1, D1), jnp.float32) * s, 'attn_r1': jax.random.normal(ks[5], (H1, D1), jnp.float32) * s, 'bias1': jax.random.normal(ks[6], (H1 * D1,), jnp.float32) * s, 'fc2_w': jax.random.normal(ks[7], (H2 * OUT, HID), jnp.float32) * s, 'attn_l2': jax.random.normal(ks[8], (H2, OUT), jnp.float32) * s, 'attn_r2': jax.random.normal(ks[9], (H2, OUT), jnp.float32) * s, 'bias2': jax.random.normal(ks[10], (H2 * OUT,), jnp.float32) * s, 'wb0': jax.random.normal(ks[11], (HID, IN), jnp.float32) * s, 'bb0': jax.random.normal(ks[12], (HID,), jnp.float32) * s, 'wb1': jax.random.normal(ks[13], (OUT, IN + HID), jnp.float32) * s, 'bb1': jax.random.normal(ks[14], (OUT,), jnp.float32) * s}
    _L2_gnn_all = _L2_gnn_setup()
    _L2_gnn_in = {k: v for k, v in _L2_gnn_all.items() if k in ('fc1_w', 'attn_l1', 'attn_r1', 'bias1', 'fc2_w', 'attn_l2', 'attn_r2', 'bias2', 'wb0', 'bb0', 'wb1', 'bb1')}
    del _L2_gnn_all

    def _L3_gnn_setup():
        import jax, jax.numpy as jnp
        import numpy as np
        from jax import lax
        N, E, D = (512, 16384, 256)
        NH, FOUT = (4, 64)
        D_STATE, D_CONV, DT_RANK = (16, 4, 16)

        def _layer_norm(x, g, b, eps=1e-05):
            mu = jnp.mean(x, -1, keepdims=True)
            var = jnp.var(x, -1, keepdims=True)
            return (x - mu) * lax.rsqrt(var + eps) * g + b

        def _mamba(xs, in_proj_w, conv_w, conv_b, x_proj_w, dt_proj_w, dt_proj_b, A_log, D_param, out_proj_w):
            n = xs.shape[0]
            xz = xs @ in_proj_w.T
            xc, z = jnp.split(xz, 2, axis=-1)
            K = conv_w.shape[1]
            xp = jnp.pad(xc, ((K - 1, 0), (0, 0)))
            xc = sum((xp[k:k + n] * conv_w[:, k] for k in range(K))) + conv_b
            xc = jax.nn.silu(xc)
            dbc = xc @ x_proj_w.T
            dt = jax.nn.softplus(dbc[:, :DT_RANK] @ dt_proj_w.T + dt_proj_b)
            Bm = dbc[:, DT_RANK:DT_RANK + D_STATE]
            Cm = dbc[:, DT_RANK + D_STATE:]
            A = -jnp.exp(A_log)
            dA = jnp.exp(dt[:, :, None] * A)
            dBx = (dt * xc)[:, :, None] * Bm[:, None, :]

            def step(h, t):
                dA_t, dBx_t, C_t = t
                h = dA_t * h + dBx_t
                return (h, h @ C_t)
            _, y = lax.scan(step, jnp.zeros((xc.shape[1], D_STATE), xs.dtype), (dA, dBx, Cm))
            y = y + xc * D_param
            y = y * jax.nn.silu(z)
            return y @ out_proj_w.T

        def _forward(x, edge_index, deg_noise, gat_w, gat_a_src, gat_a_tgt, gat_b, ln_local_g, ln_local_b, ln_global_g, ln_global_b, ln2_g, ln2_b, in_proj_w, conv_w, conv_b, x_proj_w, dt_proj_w, dt_proj_b, A_log, D_param, out_proj_w, wl, wg, ff1_w, ff1_b, ff2_w, ff2_b):
            n = x.shape[0]
            src, tgt = (edge_index[0], edge_index[1])
            proj = (x @ gat_w.T).reshape(n, NH, FOUT)
            s_src = jnp.sum(proj * gat_a_src, -1)
            s_tgt = jnp.sum(proj * gat_a_tgt, -1)
            e = jax.nn.leaky_relu(s_src[src] + s_tgt[tgt], 0.2)
            exp_e = jnp.exp(e - jnp.max(e))
            denom = jax.ops.segment_sum(exp_e, tgt, num_segments=n)
            attn = exp_e / (denom[tgt] + 1e-16)
            agg = jax.ops.segment_sum(proj[src] * attn[:, :, None], tgt, num_segments=n)
            h_local = jax.nn.elu((agg + x.reshape(n, NH, FOUT)).reshape(n, NH * FOUT) + gat_b)
            h_local = _layer_norm(h_local, ln_local_g, ln_local_b)
            deg = jax.ops.segment_sum(jnp.ones((src.shape[0],), x.dtype), src, num_segments=n)
            perm = jnp.argsort(deg + deg_noise, stable=True)
            inv = jnp.argsort(perm)
            y = _mamba(x[perm], in_proj_w, conv_w, conv_b, x_proj_w, dt_proj_w, dt_proj_b, A_log, D_param, out_proj_w)
            h_attn = _layer_norm(x + y[inv], ln_global_g, ln_global_b)
            gate = jax.nn.sigmoid(h_local @ wl.T + h_attn @ wg.T)
            h = gate * h_local + (1.0 - gate) * h_attn
            ff = jax.nn.relu(h @ ff1_w.T + ff1_b) @ ff2_w.T + ff2_b
            return _layer_norm(h + ff, ln2_g, ln2_b)
        key = jax.random.key(seed)
        ks = jax.random.split(key, 24)
        w = lambda i, shape, s=0.05: jax.random.normal(ks[i], shape, dtype=jnp.float32) * s
        return {'x': jax.random.normal(ks[0], (N, D), dtype=jnp.float32), 'edge_index': jax.random.randint(ks[1], (2, E), 0, N, dtype=jnp.int32), 'edge_prob': jax.random.uniform(ks[2], (E,), dtype=jnp.float32), 'deg_noise': jax.random.uniform(ks[3], (N,), dtype=jnp.float32), 'gat_w': w(4, (NH * FOUT, D)), 'gat_a_src': w(5, (NH, FOUT)), 'gat_a_tgt': w(6, (NH, FOUT)), 'gat_b': jnp.zeros((NH * FOUT,), jnp.float32), 'ln_local_g': jnp.ones((D,), jnp.float32), 'ln_local_b': jnp.zeros((D,), jnp.float32), 'ln_global_g': jnp.ones((D,), jnp.float32), 'ln_global_b': jnp.zeros((D,), jnp.float32), 'ln2_g': jnp.ones((D,), jnp.float32), 'ln2_b': jnp.zeros((D,), jnp.float32), 'in_proj_w': w(7, (2 * D, D)), 'conv_w': w(8, (D, D_CONV), 0.2), 'conv_b': jnp.zeros((D,), jnp.float32), 'x_proj_w': w(9, (DT_RANK + 2 * D_STATE, D)), 'dt_proj_w': w(10, (D, DT_RANK)), 'dt_proj_b': w(11, (D,), 0.1) - 4.0, 'A_log': jnp.log(jnp.tile(jnp.arange(1, D_STATE + 1, dtype=jnp.float32), (D, 1))), 'D_param': jnp.ones((D,), jnp.float32), 'out_proj_w': w(12, (D, D)), 'wl': w(13, (D, D)), 'wg': w(14, (D, D)), 'ff1_w': w(15, (2 * D, D)), 'ff1_b': jnp.zeros((2 * D,), jnp.float32), 'ff2_w': w(16, (D, 2 * D)), 'ff2_b': jnp.zeros((D,), jnp.float32)}
    _L3_gnn_all = _L3_gnn_setup()
    _L3_gnn_in = {k: v for k, v in _L3_gnn_all.items() if k in ('gat_w', 'gat_a_src', 'gat_a_tgt', 'gat_b', 'ln_local_g', 'ln_local_b', 'ln_global_g', 'ln_global_b', 'ln2_g', 'ln2_b', 'in_proj_w', 'conv_w', 'conv_b', 'x_proj_w', 'dt_proj_w', 'dt_proj_b', 'A_log', 'D_param', 'out_proj_w', 'wl', 'wg', 'ff1_w', 'ff1_b', 'ff2_w', 'ff2_b')}
    del _L3_gnn_all
    return {'x': x, 'src': src, 'dst': dst, 'edge_type_32': edge_type_32, 'edge_weight': edge_weight, 'edge_weight1': edge_weight1, 'node_vec': node_vec, 'L0_gnn_Wq': _L0_gnn_in['Wq'], 'L0_gnn_bq': _L0_gnn_in['bq'], 'L0_gnn_Wk': _L0_gnn_in['Wk'], 'L0_gnn_bk': _L0_gnn_in['bk'], 'L0_gnn_Wv': _L0_gnn_in['Wv'], 'L0_gnn_bv': _L0_gnn_in['bv'], 'L0_gnn_Wskip': _L0_gnn_in['Wskip'], 'L0_gnn_bskip': _L0_gnn_in['bskip'], 'L0_gnn_gamma': _L0_gnn_in['gamma'], 'L0_gnn_beta': _L0_gnn_in['beta'], 'L1_gnn_bases': _L1_gnn_in['bases'], 'L1_gnn_w_comp': _L1_gnn_in['w_comp'], 'L2_gnn_fc1_w': _L2_gnn_in['fc1_w'], 'L2_gnn_attn_l1': _L2_gnn_in['attn_l1'], 'L2_gnn_attn_r1': _L2_gnn_in['attn_r1'], 'L2_gnn_bias1': _L2_gnn_in['bias1'], 'L2_gnn_fc2_w': _L2_gnn_in['fc2_w'], 'L2_gnn_attn_l2': _L2_gnn_in['attn_l2'], 'L2_gnn_attn_r2': _L2_gnn_in['attn_r2'], 'L2_gnn_bias2': _L2_gnn_in['bias2'], 'L2_gnn_wb0': _L2_gnn_in['wb0'], 'L2_gnn_bb0': _L2_gnn_in['bb0'], 'L2_gnn_wb1': _L2_gnn_in['wb1'], 'L2_gnn_bb1': _L2_gnn_in['bb1'], 'L3_gnn_gat_w': _L3_gnn_in['gat_w'], 'L3_gnn_gat_a_src': _L3_gnn_in['gat_a_src'], 'L3_gnn_gat_a_tgt': _L3_gnn_in['gat_a_tgt'], 'L3_gnn_gat_b': _L3_gnn_in['gat_b'], 'L3_gnn_ln_local_g': _L3_gnn_in['ln_local_g'], 'L3_gnn_ln_local_b': _L3_gnn_in['ln_local_b'], 'L3_gnn_ln_global_g': _L3_gnn_in['ln_global_g'], 'L3_gnn_ln_global_b': _L3_gnn_in['ln_global_b'], 'L3_gnn_ln2_g': _L3_gnn_in['ln2_g'], 'L3_gnn_ln2_b': _L3_gnn_in['ln2_b'], 'L3_gnn_in_proj_w': _L3_gnn_in['in_proj_w'], 'L3_gnn_conv_w': _L3_gnn_in['conv_w'], 'L3_gnn_conv_b': _L3_gnn_in['conv_b'], 'L3_gnn_x_proj_w': _L3_gnn_in['x_proj_w'], 'L3_gnn_dt_proj_w': _L3_gnn_in['dt_proj_w'], 'L3_gnn_dt_proj_b': _L3_gnn_in['dt_proj_b'], 'L3_gnn_A_log': _L3_gnn_in['A_log'], 'L3_gnn_D_param': _L3_gnn_in['D_param'], 'L3_gnn_out_proj_w': _L3_gnn_in['out_proj_w'], 'L3_gnn_wl': _L3_gnn_in['wl'], 'L3_gnn_wg': _L3_gnn_in['wg'], 'L3_gnn_ff1_w': _L3_gnn_in['ff1_w'], 'L3_gnn_ff1_b': _L3_gnn_in['ff1_b'], 'L3_gnn_ff2_w': _L3_gnn_in['ff2_w'], 'L3_gnn_ff2_b': _L3_gnn_in['ff2_b']}

def reference(x, src, dst, edge_type_32, edge_weight, edge_weight1, node_vec, L0_gnn_Wq, L0_gnn_bq, L0_gnn_Wk, L0_gnn_bk, L0_gnn_Wv, L0_gnn_bv, L0_gnn_Wskip, L0_gnn_bskip, L0_gnn_gamma, L0_gnn_beta, L1_gnn_bases, L1_gnn_w_comp, L2_gnn_fc1_w, L2_gnn_attn_l1, L2_gnn_attn_r1, L2_gnn_bias1, L2_gnn_fc2_w, L2_gnn_attn_l2, L2_gnn_attn_r2, L2_gnn_bias2, L2_gnn_wb0, L2_gnn_bb0, L2_gnn_wb1, L2_gnn_bb1, L3_gnn_gat_w, L3_gnn_gat_a_src, L3_gnn_gat_a_tgt, L3_gnn_gat_b, L3_gnn_ln_local_g, L3_gnn_ln_local_b, L3_gnn_ln_global_g, L3_gnn_ln_global_b, L3_gnn_ln2_g, L3_gnn_ln2_b, L3_gnn_in_proj_w, L3_gnn_conv_w, L3_gnn_conv_b, L3_gnn_x_proj_w, L3_gnn_dt_proj_w, L3_gnn_dt_proj_b, L3_gnn_A_log, L3_gnn_D_param, L3_gnn_out_proj_w, L3_gnn_wl, L3_gnn_wg, L3_gnn_ff1_w, L3_gnn_ff1_b, L3_gnn_ff2_w, L3_gnn_ff2_b):
    import jax
    import jax.numpy as jnp

    def _L0_gnn_ref(x, edge_index, Wq, bq, Wk, bk, Wv, bv, Wskip, bskip, gamma, beta):
        import jax, jax.numpy as jnp
        import numpy as np
        N, HID, HEADS = (3125, 256, 8)
        D = HID // HEADS
        E = 50000

        def _gnn_layer(x, edge_index, Wq, bq, Wk, bk, Wv, bv, Wskip, bskip, gamma, beta):
            n = x.shape[0]
            src, dst = (edge_index[0], edge_index[1])
            q = (x @ Wq + bq).reshape(n, HEADS, D)
            k = (x @ Wk + bk).reshape(n, HEADS, D)
            v = (x @ Wv + bv).reshape(n, HEADS, D)
            logits = jnp.einsum('ehd,ehd->eh', q[dst], k[src]) / jnp.sqrt(jnp.float32(D))
            seg_max = jax.ops.segment_max(logits, dst, num_segments=n)
            expv = jnp.exp(logits - seg_max[dst])
            denom = jax.ops.segment_sum(expv, dst, num_segments=n)
            attn = expv / denom[dst]
            agg = jax.ops.segment_sum(attn[:, :, None] * v[src], dst, num_segments=n)
            out = agg.reshape(n, HID) + (x @ Wskip + bskip)
            h = jax.nn.gelu(out, approximate=False)
            y = x + h
            mu = jnp.mean(y, axis=-1, keepdims=True)
            var = jnp.var(y, axis=-1, keepdims=True)
            return (y - mu) / jnp.sqrt(var + 1e-05) * gamma + beta
        return _gnn_layer(x, edge_index, Wq, bq, Wk, bk, Wv, bv, Wskip, bskip, gamma, beta)

    def _L1_gnn_ref(h, src, dst, rel_type, norm, bases, w_comp):
        import jax, jax.numpy as jnp
        import numpy as np
        N_NODES = 1250
        N_EDGES = 20000
        IN_DIM = 256
        OUT_DIM = 256
        NUM_RELS = 32
        NUM_BASES = 8
        weight = jnp.einsum('rb,bio->rio', w_comp, bases)
        xw = jnp.einsum('ni,rio->nro', h, weight)
        msg = xw[src, rel_type] * norm
        out = jax.ops.segment_sum(msg, dst, num_segments=h.shape[0])
        return jax.nn.relu(out)

    def _L2_gnn_ref(inputs, src, dst, fc1_w, attn_l1, attn_r1, bias1, fc2_w, attn_l2, attn_r2, bias2, wb0, bb0, wb1, bb1):
        import jax, jax.numpy as jnp
        import numpy as np
        N = 1250
        E = 20000
        IN = 256
        HID = 256
        OUT = 256
        H1 = 8
        D1 = HID // H1
        H2 = 1

        def gat_conv(h, src, dst, fc_w, attn_l, attn_r, bias, heads, out_feats):
            n = h.shape[0]
            feat = (h @ fc_w.T).reshape(n, heads, out_feats)
            el = jnp.sum(feat * attn_l, axis=-1)
            er = jnp.sum(feat * attn_r, axis=-1)
            e = jax.nn.leaky_relu(el[src] + er[dst], 0.2)
            m = jax.ops.segment_max(e, dst, num_segments=n)
            m = jnp.where(jnp.isfinite(m), m, 0.0)
            ex = jnp.exp(e - m[dst])
            ssum = jax.ops.segment_sum(ex, dst, num_segments=n)
            a = ex / ssum[dst]
            rst = jax.ops.segment_sum(feat[src] * a[..., None], dst, num_segments=n)
            return rst + bias.reshape(heads, out_feats)
        n = inputs.shape[0]
        deg = jax.ops.segment_sum(jnp.ones_like(dst, jnp.float32), dst, num_segments=n)
        norm = (1.0 / jnp.clip(deg, 1.0, None))[:, None]
        h0 = gat_conv(inputs, src, dst, fc1_w, attn_l1, attn_r1, bias1, H1, D1)
        h0 = h0.reshape(n, H1 * D1)
        h1 = jax.nn.relu(h0 + norm * (inputs @ wb0.T + bb0))
        h2 = gat_conv(h1, src, dst, fc2_w, attn_l2, attn_r2, bias2, H2, OUT)
        h2 = h2.mean(axis=1)
        cat = jnp.concatenate([inputs, h1], axis=-1)
        return h2 + norm * (cat @ wb1.T + bb1)

    def _L3_gnn_ref(x, edge_index, edge_prob, deg_noise, gat_w, gat_a_src, gat_a_tgt, gat_b, ln_local_g, ln_local_b, ln_global_g, ln_global_b, ln2_g, ln2_b, in_proj_w, conv_w, conv_b, x_proj_w, dt_proj_w, dt_proj_b, A_log, D_param, out_proj_w, wl, wg, ff1_w, ff1_b, ff2_w, ff2_b):
        import jax, jax.numpy as jnp
        import numpy as np
        from jax import lax
        N, E, D = (512, 16384, 256)
        NH, FOUT = (4, 64)
        D_STATE, D_CONV, DT_RANK = (16, 4, 16)

        def _layer_norm(x, g, b, eps=1e-05):
            mu = jnp.mean(x, -1, keepdims=True)
            var = jnp.var(x, -1, keepdims=True)
            return (x - mu) * lax.rsqrt(var + eps) * g + b

        def _mamba(xs, in_proj_w, conv_w, conv_b, x_proj_w, dt_proj_w, dt_proj_b, A_log, D_param, out_proj_w):
            n = xs.shape[0]
            xz = xs @ in_proj_w.T
            xc, z = jnp.split(xz, 2, axis=-1)
            K = conv_w.shape[1]
            xp = jnp.pad(xc, ((K - 1, 0), (0, 0)))
            xc = sum((xp[k:k + n] * conv_w[:, k] for k in range(K))) + conv_b
            xc = jax.nn.silu(xc)
            dbc = xc @ x_proj_w.T
            dt = jax.nn.softplus(dbc[:, :DT_RANK] @ dt_proj_w.T + dt_proj_b)
            Bm = dbc[:, DT_RANK:DT_RANK + D_STATE]
            Cm = dbc[:, DT_RANK + D_STATE:]
            A = -jnp.exp(A_log)
            dA = jnp.exp(dt[:, :, None] * A)
            dBx = (dt * xc)[:, :, None] * Bm[:, None, :]

            def step(h, t):
                dA_t, dBx_t, C_t = t
                h = dA_t * h + dBx_t
                return (h, h @ C_t)
            _, y = lax.scan(step, jnp.zeros((xc.shape[1], D_STATE), xs.dtype), (dA, dBx, Cm))
            y = y + xc * D_param
            y = y * jax.nn.silu(z)
            return y @ out_proj_w.T

        def _forward(x, edge_index, deg_noise, gat_w, gat_a_src, gat_a_tgt, gat_b, ln_local_g, ln_local_b, ln_global_g, ln_global_b, ln2_g, ln2_b, in_proj_w, conv_w, conv_b, x_proj_w, dt_proj_w, dt_proj_b, A_log, D_param, out_proj_w, wl, wg, ff1_w, ff1_b, ff2_w, ff2_b):
            n = x.shape[0]
            src, tgt = (edge_index[0], edge_index[1])
            proj = (x @ gat_w.T).reshape(n, NH, FOUT)
            s_src = jnp.sum(proj * gat_a_src, -1)
            s_tgt = jnp.sum(proj * gat_a_tgt, -1)
            e = jax.nn.leaky_relu(s_src[src] + s_tgt[tgt], 0.2)
            exp_e = jnp.exp(e - jnp.max(e))
            denom = jax.ops.segment_sum(exp_e, tgt, num_segments=n)
            attn = exp_e / (denom[tgt] + 1e-16)
            agg = jax.ops.segment_sum(proj[src] * attn[:, :, None], tgt, num_segments=n)
            h_local = jax.nn.elu((agg + x.reshape(n, NH, FOUT)).reshape(n, NH * FOUT) + gat_b)
            h_local = _layer_norm(h_local, ln_local_g, ln_local_b)
            deg = jax.ops.segment_sum(jnp.ones((src.shape[0],), x.dtype), src, num_segments=n)
            perm = jnp.argsort(deg + deg_noise, stable=True)
            inv = jnp.argsort(perm)
            y = _mamba(x[perm], in_proj_w, conv_w, conv_b, x_proj_w, dt_proj_w, dt_proj_b, A_log, D_param, out_proj_w)
            h_attn = _layer_norm(x + y[inv], ln_global_g, ln_global_b)
            gate = jax.nn.sigmoid(h_local @ wl.T + h_attn @ wg.T)
            h = gate * h_local + (1.0 - gate) * h_attn
            ff = jax.nn.relu(h @ ff1_w.T + ff1_b) @ ff2_w.T + ff2_b
            return _layer_norm(h + ff, ln2_g, ln2_b)
        return _forward(x, edge_index, deg_noise, gat_w, gat_a_src, gat_a_tgt, gat_b, ln_local_g, ln_local_b, ln_global_g, ln_global_b, ln2_g, ln2_b, in_proj_w, conv_w, conv_b, x_proj_w, dt_proj_w, dt_proj_b, A_log, D_param, out_proj_w, wl, wg, ff1_w, ff1_b, ff2_w, ff2_b)
    edge_index = jnp.stack([src, dst])
    x = _layernorm(x + _L0_gnn_ref(x, edge_index, L0_gnn_Wq, L0_gnn_bq, L0_gnn_Wk, L0_gnn_bk, L0_gnn_Wv, L0_gnn_bv, L0_gnn_Wskip, L0_gnn_bskip, L0_gnn_gamma, L0_gnn_beta), axis=-1)
    x = _layernorm(x + _L1_gnn_ref(x, src, dst, edge_type_32, edge_weight1, L1_gnn_bases, L1_gnn_w_comp), axis=-1)
    x = _layernorm(x + _L2_gnn_ref(x, src, dst, L2_gnn_fc1_w, L2_gnn_attn_l1, L2_gnn_attn_r1, L2_gnn_bias1, L2_gnn_fc2_w, L2_gnn_attn_l2, L2_gnn_attn_r2, L2_gnn_bias2, L2_gnn_wb0, L2_gnn_bb0, L2_gnn_wb1, L2_gnn_bb1), axis=-1)
    x = _layernorm(x + _L3_gnn_ref(x, edge_index, edge_weight, node_vec, L3_gnn_gat_w, L3_gnn_gat_a_src, L3_gnn_gat_a_tgt, L3_gnn_gat_b, L3_gnn_ln_local_g, L3_gnn_ln_local_b, L3_gnn_ln_global_g, L3_gnn_ln_global_b, L3_gnn_ln2_g, L3_gnn_ln2_b, L3_gnn_in_proj_w, L3_gnn_conv_w, L3_gnn_conv_b, L3_gnn_x_proj_w, L3_gnn_dt_proj_w, L3_gnn_dt_proj_b, L3_gnn_A_log, L3_gnn_D_param, L3_gnn_out_proj_w, L3_gnn_wl, L3_gnn_wg, L3_gnn_ff1_w, L3_gnn_ff1_b, L3_gnn_ff2_w, L3_gnn_ff2_b), axis=-1)
    return x

_drawn_inputs = setup_inputs


def setup_inputs(seed=0):
    import zlib

    import numpy as np

    out = dict(_drawn_inputs(seed))
    spreads = {'L0_gnn_bq': (0.0, 0.8),
     'L0_gnn_bk': (0.0, 2.0),
     'L0_gnn_bv': (0.0, 0.1),
     'L0_gnn_bskip': (0.0, 0.1),
     'L0_gnn_gamma': (1.0, 0.2),
     'L0_gnn_beta': (0.0, 0.1),
     'L3_gnn_gat_b': (0.0, 0.335),
     'L3_gnn_ln_local_g': (1.0, 0.2),
     'L3_gnn_ln_local_b': (0.0, 0.268),
     'L3_gnn_ln_global_g': (1.0, 0.2),
     'L3_gnn_ln_global_b': (0.0, 0.269),
     'L3_gnn_ln2_g': (1.0, 0.2),
     'L3_gnn_ln2_b': (0.0, 0.1),
     'L3_gnn_conv_b': (0.0, 0.8),
     'L3_gnn_D_param': (1.0, 0.6),
     'L3_gnn_ff1_b': (0.0, 0.1),
     'L3_gnn_ff2_b': (0.0, 0.1)}
    factors = {'node_vec': 3.686,
     'L0_gnn_Wq': 8.0,
     'L0_gnn_Wk': 8.0,
     'L0_gnn_Wv': 2.996,
     'L2_gnn_attn_l1': 6.605,
     'L2_gnn_attn_r1': 8.0,
     'L2_gnn_bias1': 2.843,
     'L2_gnn_attn_l2': 8.0,
     'L2_gnn_attn_r2': 8.0,
     'L2_gnn_wb0': 8.0,
     'L2_gnn_bb0': 28.584,
     'L2_gnn_bb1': 8.0,
     'L3_gnn_gat_a_src': 5.35,
     'L3_gnn_gat_a_tgt': 8.0,
     'L3_gnn_in_proj_w': 2.923,
     'L3_gnn_conv_w': 3.244,
     'L3_gnn_x_proj_w': 8.0,
     'L3_gnn_dt_proj_w': 8.0,
     'L3_gnn_dt_proj_b': 8.0,
     'L3_gnn_A_log': 8.0,
     'L3_gnn_out_proj_w': 2.942}
    for name, (base, spread) in spreads.items():
        noise = np.random.default_rng([zlib.crc32(name.encode()), seed]).standard_normal(out[name].shape)
        drawn = base * np.exp(spread * noise) if base else spread * noise
        out[name] = jnp.asarray(drawn.astype(out[name].dtype))
    for name, factor in factors.items():
        out[name] = (out[name] * factor).astype(out[name].dtype)
    return out
```

```python
from contextlib import ExitStack

import concourse.bass as bass
from concourse import mybir

F32 = mybir.dt.float32
I32 = mybir.dt.int32
BF16 = mybir.dt.bfloat16
ALU = mybir.AluOpType
ACT = mybir.ActivationFunctionType
X = mybir.AxisListType.X

P = 128
N = 3125
E = 103125
F = 256
T = (N + P - 1) // P
NP = T * P
RELS = 32
BASES = 8
EP = 125
EC = E // EP
HIST_HI, HIST_LO = 49, 64
HB = 32
EC_PAD = 832
S = 8
RUN = 16
MB = 4
NB = S // MB
META = 4 * S
CHUNKS_MAX = 2 * ((E + E // P + P) // RUN + T + 2)
FAR = 1.0e6
LOW = -1.0e30
EPS = 1e-5
assert E == EP * EC and HIST_HI * HIST_LO >= N and EC_PAD % (2 * HB) == 0


class Steps:

    def __init__(self, eng, sem, base=0):
        self.eng, self.sem, self.base, self.n = eng, sem, base, 0

    def add(self, ins):
        ins.then_inc(self.sem, 1)
        self.n += 1

    def wait(self):
        self.eng.wait_ge(self.sem, self.base + self.n)

    def do(self, ins):
        self.add(ins)
        self.wait()


def over_slots(ap, n):
    return ap.unsqueeze(1).to_broadcast([ap.shape[0], n, ap.shape[1]])


def over_dims(ap, n):
    return ap.unsqueeze(len(ap.shape)).to_broadcast(list(ap.shape) + [n])


def rows_of(vec):
    return vec.rearrange("(a f) -> a f", a=1)


def on_all(vec, n=P):
    return rows_of(vec).to_broadcast([n, vec.shape[0]])


def prime(pool, dr, spare, sem):
    pool.dma_start(spare[:], dr["info"][0:1, :]).then_inc(sem, 16)


def finish(nc, sems):
    nc.clear_and_free_semaphores(sems)
    nc.all_engine_barrier()


def count_edges(nc, io, dr):
    with ExitStack() as ctx:
        def sb(name, shape, dt=F32):
            return ctx.enter_context(nc.sbuf_tensor(name, shape, dt))
        names = ["e_pads", "e_loaded", "e_iota", "e_steps", "e_casts", "e_hot0", "e_hot1", "e_summed0", "e_summed1",
                 "e_zeroed", "e_hist", "e_counts", "e_packed", "e_runs", "e_actruns", "e_stored"]
        sems = {n[2:]: nc.alloc_semaphore(n) for n in names}
        hot, summed = [sems["hot0"], sems["hot1"]], [sems["summed0"], sems["summed1"]]
        W = EC + RUN
        dst = sb("e_dst", [EP, EC_PAD], I32)
        src = sb("e_src", [EP, W], I32)
        rel = sb("e_rel", [EP, W], I32)
        nrm = sb("e_nrm", [EP, W])
        packed = sb("e_pack", [EP, W], I32)
        part_i = sb("e_parti", [EP, EC_PAD], I32)
        parts = {k: sb("e_part" + k, [EP, EC_PAD], BF16) for k in ("dh", "dl", "sh", "sl")}
        iota_i = sb("e_ioi", [EP, HIST_LO], I32)
        iota = sb("e_io", [EP, HIST_LO], BF16)
        ones_at = {k: [sb(f"e_hot{k}{b}", [EP, HB, HIST_HI if k[1] == "h" else HIST_LO], BF16) for b in range(2)]
                   for k in parts}
        runs = sb("e_runs_sb", [EP, EC, 2 * RUN], I32)
        zero = sb("e_zero", [EP, HIST_LO], BF16)
        counts = sb("e_counts_sb", [HIST_HI, 2, HIST_LO])
        zrow = sb("e_zrow", [1, 64])
        ps = ctx.enter_context(nc.psum_tensor("e_ps", [HIST_HI, 2, 512], F32))
        block = ctx.enter_context(nc.Block())

        @block.sync
        def _(sp):
            sp.wait_ge(sems["pads"], 3)
            sp.dma_start(dst[:, 0:EC], io["dst"].rearrange("(p c) -> p c", p=EP)).then_inc(sems["loaded"], 16)
            for tile, name in ((src, "src"), (rel, "edge_type_32"), (nrm, "edge_weight1")):
                flat = io[name] if name != "edge_weight1" else io[name].rearrange("e a -> (e a)")
                rows = flat.rearrange("(p c) -> p c", p=EP)
                sp.dma_start(tile[:, 0:EC], rows).then_inc(sems["loaded"], 16)
                sp.dma_start(tile[0:EP - 1, EC:W], rows[1:EP, 0:RUN]).then_inc(sems["loaded"], 16)
            sp.wait_ge(sems["counts"], 2)
            for k, name in enumerate(("indeg", "outdeg")):
                sp.dma_start(dr[name][0:HIST_HI * HIST_LO].rearrange("(h l) -> h l", h=HIST_HI),
                             counts[:, k, :]).then_inc(sems["stored"], 16)
                sp.dma_start(rows_of(dr[name][HIST_HI * HIST_LO:NP]), zrow[:, :]).then_inc(sems["stored"], 16)
            sp.wait_ge(sems["runs"], RUN)
            sp.wait_ge(sems["actruns"], RUN)
            sp.dma_start(dr["runs"].rearrange("(p c) w -> p c w", p=EP), runs[:]).then_inc(sems["stored"], 16)
            sp.wait_ge(sems["stored"], 16 * 5)

        @block.gpsimd
        def _(pool):
            nc.gpsimd.memset(src[:, EC:W], 0).then_inc(sems["pads"], 1)
            nc.gpsimd.memset(rel[:, EC:W], 0).then_inc(sems["pads"], 1)
            nc.gpsimd.memset(nrm[:, EC:W], 0.0).then_inc(sems["pads"], 1)
            nc.gpsimd.iota(iota_i[:], [[1, HIST_LO]], base=0, channel_multiplier=0).then_inc(sems["iota"], 1)

        @block.vector
        def _(v):
            st = Steps(v, sems["steps"])
            st.add(nc.vector.memset(zero[:], 0.0))
            st.add(nc.vector.memset(zrow[:], 0.0))
            for k in parts:
                st.add(nc.vector.memset(parts[k][:, EC:EC_PAD], 16384.0))
            v.wait_ge(sems["iota"], 1)
            st.do(nc.vector.tensor_copy(iota[:], iota_i[:]))
            v.wait_ge(sems["loaded"], 16 * 7)
            for k, tile in (("d", dst), ("s", src)):
                st.do(nc.vector.tensor_scalar(part_i[:, 0:EC], tile[:, 0:EC], 6, None, ALU.logical_shift_right))
                st.do(nc.vector.tensor_copy(parts[k + "h"][:, 0:EC], part_i[:, 0:EC]))
                st.do(nc.vector.tensor_scalar(part_i[:, 0:EC], tile[:, 0:EC], 63, None, ALU.bitwise_and))
                st.do(nc.vector.tensor_copy(parts[k + "l"][:, 0:EC], part_i[:, 0:EC]))
            nc.vector.scalar_tensor_tensor(packed[:], src[:], float(RELS), rel[:], ALU.mult,
                                           ALU.add).then_inc(sems["packed"], 1)
            with v.Fori(0, EC_PAD // HB // 2) as i:
                for b in range(2):
                    v.wait_ge(summed[b], i + 1)
                    for k in ("dh", "dl", "sh", "sl"):
                        w = HIST_HI if k[1] == "h" else HIST_LO
                        cols = parts[k][:, bass.ds((2 * i + b) * HB, HB)]
                        ins = nc.vector.tensor_tensor(ones_at[k][b][:], over_dims(cols, w),
                                                      over_slots(iota[:, 0:w], HB), ALU.is_equal)
                    ins.then_inc(hot[b], 1)
            v.wait_ge(sems["packed"], 1)
            for s in range(RUN):
                nc.vector.tensor_copy(runs[:, :, s], packed[:, s:s + EC]).then_inc(sems["runs"], 1)
            v.wait_ge(sems["hist"], 1)
            for k in range(2):
                nc.vector.tensor_copy(counts[:, k, :], ps[:, k, 0:HIST_LO]).then_inc(sems["counts"], 1)

        @block.scalar
        def _(act):
            act.wait_ge(sems["loaded"], 16 * 7)
            for s in range(RUN):
                nc.scalar.activation(runs[:, :, RUN + s].bitcast(F32), nrm[:, s:s + EC],
                                     ACT.Copy).then_inc(sems["actruns"], 1)

        @block.tensor
        def _(pe):
            pe.sem_inc(summed[0], 1)
            pe.sem_inc(summed[1], 1)
            pe.wait_ge(sems["steps"], 1)
            for k in range(2):
                nc.tensor.matmul(ps[:, k, 0:HIST_LO], zero[:, 0:HIST_HI], zero[:, :], start=True, stop=False)
            with pe.Fori(0, EC_PAD // HB // 2) as i:
                for b in range(2):
                    pe.wait_ge(hot[b], i + 1)
                    for c in range(HB):
                        for k, (h, l) in enumerate((("dh", "dl"), ("sh", "sl"))):
                            ins = nc.tensor.matmul(ps[:, k, 0:HIST_LO], ones_at[h][b][:, c, :], ones_at[l][b][:, c, :],
                                                   start=False, stop=False, skip_group_check=True)
                    ins.then_inc(summed[b], 1)
            for k in range(2):
                ins = nc.tensor.matmul(ps[:, k, 0:HIST_LO], zero[:, 0:HIST_HI], zero[:, :], start=False, stop=True)
            ins.then_inc(sems["hist"], 1)
    finish(nc, list(sems.values()))


def rank(v, st, out, keys_all, keys_own, before, upto_own, tri, junk, cnt):
    for t in range(T):
        own = keys_own[:, t:t + 1]
        lo, hi = t * P, (t + 1) * P
        if t:
            st.add(v.tensor_scalar(junk[:, 0:lo], keys_all[:, 0:lo], own, 0.0, upto_own, ALU.add,
                                         accum_out=cnt[:, 0:1]))
        else:
            st.add(v.memset(cnt[:, 0:1], 0.0))
        if t < T - 1:
            st.add(v.tensor_scalar(junk[:, hi:NP], keys_all[:, hi:NP], own, 0.0, before, ALU.add,
                                         accum_out=cnt[:, 1:2]))
        else:
            st.add(v.memset(cnt[:, 1:2], 0.0))
        st.add(v.tensor_scalar(junk[:, lo:hi], keys_all[:, lo:hi], own, 0.0, before, ALU.add,
                                     accum_out=cnt[:, 2:3]))
        st.wait()
        st.do(v.scalar_tensor_tensor(junk[:, lo:hi], keys_all[:, lo:hi], own, tri, ALU.is_equal, ALU.mult,
                                           accum_out=cnt[:, 3:4]))
        st.do(v.tensor_reduce(out[:, t:t + 1], cnt[:, 0:4], X, ALU.add))


def order_nodes(nc, io, dr):
    with ExitStack() as ctx:
        def sb(name, shape, dt=F32):
            return ctx.enter_context(nc.sbuf_tensor(name, shape, dt))
        names = ["n_pad", "n_loaded", "n_iota", "n_steps", "n_starts", "n_stored", "n_reloaded", "n_keys",
                 "n_info", "n_scattered"]
        sems = {n[2:]: nc.alloc_semaphore(n) for n in names}
        deg_all = sb("n_degall", [P, NP])
        key_all = sb("n_keyall", [P, NP])
        junk = sb("n_junk", [P, NP], BF16)
        row = sb("n_row", [1, NP])
        cum = sb("n_cum", [1, NP])
        zero = sb("n_zero", [1, NP])
        deg, start, key, nv = (sb("n_" + k, [P, T]) for k in ("deg", "start", "key", "nv"))
        node_i = sb("n_nodei", [P, T], I32)
        by_deg, by_key = sb("n_bydeg", [P, T]), sb("n_bykey", [P, T])
        place = sb("n_place", [P, T], I32)
        info = sb("n_infosb", [P, T, 4], I32)
        cnt = sb("n_cnt", [P, 4])
        lane_i, col_i = sb("n_lanei", [P, 1], I32), sb("n_coli", [P, P], I32)
        lane, col, tri = sb("n_lane", [P, 1]), sb("n_col", [P, P]), sb("n_tri", [P, P])
        block = ctx.enter_context(nc.Block())
        by_col = "(t p) -> p t"
        whole = (T - 1) * P

        @block.sync
        def _(sp):
            with nc.allow_non_contiguous_dma(reason="one word per node"):
                sp.dma_start(deg_all[:], on_all(dr["indeg"])).then_inc(sems["loaded"], 16)
                sp.dma_start(row[:], rows_of(dr["indeg"])).then_inc(sems["loaded"], 16)
                sp.dma_start(deg[:], dr["indeg"].rearrange(by_col, p=P)).then_inc(sems["loaded"], 16)
                sp.dma_start(key[:], dr["outdeg"].rearrange(by_col, p=P)).then_inc(sems["loaded"], 16)
                sp.wait_ge(sems["pad"], 1)
                sp.dma_start(nv[:, 0:T - 1], io["node_vec"][0:whole].rearrange(by_col, p=P)).then_inc(sems["loaded"], 16)
                sp.dma_start(nv[0:N - whole, T - 1:T],
                             io["node_vec"][whole:N].rearrange("(p a) -> p a", a=1)).then_inc(sems["loaded"], 16)
                sp.wait_ge(sems["starts"], 1)
                sp.dma_start(rows_of(dr["starts"]), cum[:]).then_inc(sems["stored"], 16)
                sp.wait_ge(sems["keys"], 1)
                sp.dma_start(dr["keys"].rearrange(by_col, p=P), key[:]).then_inc(sems["stored"], 16)
                sp.wait_ge(sems["stored"], 32)
                sp.dma_start(start[:], dr["starts"].rearrange(by_col, p=P)).then_inc(sems["reloaded"], 16)
                sp.dma_start(key_all[:], on_all(dr["keys"])).then_inc(sems["reloaded"], 16)

        @block.gpsimd
        def _(pool):
            nc.gpsimd.memset(nv[:], 1.0e30).then_inc(sems["pad"], 1)
            nc.gpsimd.iota(lane_i[:], [[0, 1]], base=0, channel_multiplier=1).then_inc(sems["iota"], 1)
            nc.gpsimd.iota(col_i[:], [[1, P]], base=0, channel_multiplier=0).then_inc(sems["iota"], 1)
            nc.gpsimd.iota(node_i[:], [[P, T]], base=0, channel_multiplier=1).then_inc(sems["iota"], 1)
            pool.wait_ge(sems["info"], 1)
            for t in range(T):
                pool.indirect_dma_start(out=dr["info"], in_=info[:, t, :], in_offset=None,
                                        out_offset=bass.IndirectOffsetOnAxis(ap=place[:, t:t + 1], axis=0)
                                        ).then_inc(sems["scattered"], 16)
            pool.wait_ge(sems["scattered"], 16 * T)

        @block.vector
        def _(v):
            st = Steps(v, sems["steps"])
            v.wait_ge(sems["iota"], 3)
            st.add(v.tensor_copy(lane[:], lane_i[:]))
            st.add(v.tensor_copy(col[:], col_i[:]))
            st.add(v.memset(zero[:], 0.0))
            st.wait()
            st.do(v.tensor_scalar(tri[:], col[:], lane[:], None, ALU.is_lt))
            v.wait_ge(sems["loaded"], 16 * 6)
            st.do(v.tensor_tensor_scan(cum[:], row[:], zero[:], 0.0, ALU.add, ALU.add))
            v.tensor_tensor(cum[:], cum[:], row[:], ALU.subtract).then_inc(sems["starts"], 1)
            v.tensor_tensor(key[:], key[:], nv[:], ALU.add).then_inc(sems["keys"], 1)
            rank(v, st, by_deg, deg_all, deg, ALU.is_gt, ALU.is_ge, tri[:], junk, cnt)
            v.wait_ge(sems["reloaded"], 32)
            v.wait_ge(sems["keys"], 1)
            rank(v, st, by_key, key_all, key, ALU.is_lt, ALU.is_le, tri[:], junk, cnt)
            st.add(v.tensor_copy(info[:, :, 0], node_i[:]))
            st.add(v.tensor_copy(info[:, :, 1], start[:]))
            st.add(v.tensor_copy(info[:, :, 2], deg[:]))
            st.add(v.tensor_copy(info[:, :, 3], by_key[:]))
            v.tensor_copy(place[:], by_deg[:]).then_inc(sems["info"], 1)
    finish(nc, list(sems.values()))


def fetch_nodes(nc, io, dr, kp):
    with ExitStack() as ctx:
        def sb(name, shape, dt=F32):
            return ctx.enter_context(nc.sbuf_tensor(name, shape, dt))
        names = ["f_loaded", "f_steps", "f_zero", "f_nodes", "f_iota"]
        sems = {n[2:]: nc.alloc_semaphore(n) for n in names}
        first = sb("f_first", [1, T], I32)
        per_i = sb("f_per", [1, 2, T], I32)
        per = sb("f_perf", [1, 2, T])
        cum = sb("f_cum", [1, 2, T])
        zero = sb("f_zero_sb", [1, T])
        deg_i = sb("f_degi", [P, T], I32)
        i1, i2, i3 = sb("f_i1", [P, P], I32), sb("f_i2", [P, 1], I32), sb("f_i3", [P, S], I32)
        f1, f2 = sb("f_f1", [P, P]), sb("f_f2", [P, 1])
        block = ctx.enter_context(nc.Block())

        @block.sync
        def _(sp):
            with nc.allow_non_contiguous_dma(reason="records of four words"):
                sp.dma_start(kp["info"][:], dr["info"].rearrange("(t p) w -> p t w", p=P)).then_inc(sems["loaded"], 16)
                sp.dma_start(first[:], dr["info"].rearrange("(t p) w -> p w t", p=P)[0:1, 2, :]
                             ).then_inc(sems["loaded"], 16)
            sp.wait_ge(sems["loaded"], 32)

        @block.gpsimd
        def _(pool):
            nc.gpsimd.iota(i1[:], [[1, P]], base=0, channel_multiplier=0).then_inc(sems["iota"], 1)
            nc.gpsimd.iota(i2[:], [[0, 1]], base=0, channel_multiplier=1).then_inc(sems["iota"], 1)
            nc.gpsimd.iota(i3[:], [[1, S]], base=0, channel_multiplier=0).then_inc(sems["iota"], 1)
            nc.gpsimd.memset(kp["x"][:], 0.0).then_inc(sems["zero"], 1)
            pool.wait_ge(sems["zero"], 1)
            pool.wait_ge(sems["loaded"], 32)
            for t in range(T):
                pool.indirect_dma_start(out=kp["x"][:, t, :], out_offset=None, in_=io["x"],
                                        in_offset=bass.IndirectOffsetOnAxis(ap=kp["info"][:, t, 0:1], axis=0),
                                        bounds_check=N - 1, oob_is_err=False).then_inc(sems["nodes"], 16)
            pool.wait_ge(sems["nodes"], 16 * T)

        @block.vector
        def _(v):
            st = Steps(v, sems["steps"])
            st.add(v.memset(zero[:], 0.0))
            st.add(v.memset(kp["sched"][:], 0))
            st.add(v.memset(kp["ones"][:], 1.0))
            v.wait_ge(sems["iota"], 3)
            st.add(v.tensor_copy(f1[:], i1[:]))
            st.add(v.tensor_copy(f2[:], i2[:]))
            st.add(v.tensor_copy(kp["slot_no"][:], i3[:]))
            st.wait()
            st.add(v.tensor_scalar(kp["ident"][:], f1[:], f2[:], None, ALU.is_equal))
            v.wait_ge(sems["loaded"], 32)
            st.do(v.tensor_copy(kp["deg"][:], kp["info"][:, :, 2]))
            st.add(v.tensor_scalar(kp["has_edges"][:], kp["deg"][:], 1.0, None, ALU.min))
            st.do(v.tensor_scalar(kp["inv_deg"][:], kp["deg"][:], 1.0, None, ALU.max))
            st.do(v.reciprocal(kp["inv_deg"][:], kp["inv_deg"][:]))
            for k, size in enumerate((S, RUN)):
                st.do(v.tensor_scalar(per[:, k, :], first[:], float(size - 1), None, ALU.add))
                st.do(v.tensor_copy(per_i[:, k, :], per[:, k, :]))
                st.do(v.tensor_scalar(per_i[:, k, :], per_i[:, k, :], size.bit_length() - 1, None,
                                      ALU.logical_shift_right))
                st.do(v.tensor_scalar(per[:, k, :], per_i[:, k, :], 1.0, None, ALU.max))
                st.do(v.tensor_tensor_scan(cum[:, k, :], per[:, k, :], zero[:], 0.0, ALU.add, ALU.add))
                st.do(v.tensor_copy(kp["sched"][:, k, 1:T + 1], cum[:, k, :]))
            st.do(v.scalar_tensor_tensor(kp["sched"][:, 2, 0:T + 1], kp["sched"][:, 1, 0:T + 1], 2.0,
                                         kp["sched"][:, 0, 0:T + 1], ALU.mult, ALU.subtract))
    finish(nc, list(sems.values()))


def bounds(eng, kp, t, row=0):
    top = CHUNKS_MAX - T if row == 0 else CHUNKS_MAX // 2
    lo = eng.value_load(kp["sched"][0:1, row, bass.ds(t, 1)], min_val=0, max_val=top)
    hi = eng.value_load(kp["sched"][0:1, row, bass.ds(t + 1, 1)], min_val=1, max_val=top)
    return lo, hi


def build_slots(nc, dr, kp):
    with ExitStack() as ctx:
        def sb(name, shape, dt=F32):
            return ctx.enter_context(nc.sbuf_tensor(name, shape, dt))
        names = ["b_zero", "b_steps", "b_index", "b_runs", "b_slots", "b_stored", "b_pace", "b_begun", "b_ended"]
        sems = {n[2:]: nc.alloc_semaphore(n) for n in names}
        edge = sb("b_edge", [P, 1])
        edge_i = sb("b_edgei", [P, 1], I32)
        left = sb("b_left", [P, 1])
        run = sb("b_run", [P, 2, RUN], I32)
        src = sb("b_src", [P, RUN], I32)
        number = sb("b_number", [P, RUN])
        off, on = sb("b_off", [P, RUN]), sb("b_on", [P, RUN])
        slot_i = sb("b_sloti", [P, RUN], I32)
        slots = sb("b_slots_sb", [P, RUN // S, 4, S])
        slots_i = slots[:].bitcast(I32)
        PRO, PER = 5, 9
        block = ctx.enter_context(nc.Block())
        two = "p (k s) -> p k s"

        @block.vector
        def _(v):
            v.memset(run[:], 0).then_inc(sems["zero"], 1)
            v.wait_ge(sems["zero"], 2)
            v.tensor_copy(number[:], slot_i[:]).then_inc(sems["zero"], 1)
            v.wait_ge(sems["zero"], 3)
            with v.Fori(0, T) as t:
                lo, hi = bounds(v, kp, t, 1)
                st = Steps(v, sems["steps"], t * 2 + lo * PER)
                st.add(v.tensor_copy(edge[:], kp["info"][:, bass.ds(t, 1), 1]))
                st.add(v.tensor_copy(left[:], kp["deg"][:, bass.ds(t, 1)]))
                st.wait()
                v.sem_inc(sems["begun"], 1)
                with v.Fori(lo, hi) as c:
                    st = Steps(v, sems["steps"], t * 2 + 2 + c * PER)
                    v.tensor_copy(edge_i[:], edge[:]).then_inc(sems["index"], 1)
                    st.do(v.tensor_scalar(on[:], number[:], left[:], None, ALU.is_lt))
                    st.do(v.tensor_scalar(off[:], on[:], -FAR, FAR, ALU.mult, ALU.add))
                    st.add(v.tensor_scalar(edge[:], edge[:], float(RUN), None, ALU.add))
                    st.add(v.tensor_scalar(left[:], left[:], float(-RUN), None, ALU.add))
                    v.wait_ge(sems["runs"], (c + 1) * 16)
                    v.wait_ge(sems["stored"], c * 16 + 16)
                    st.do(v.tensor_scalar(src[:], run[:, 0, :], 5, None, ALU.logical_shift_right))
                    st.add(v.tensor_tensor(slots_i[:, :, 0, :], src[:].rearrange(two, s=S),
                                           off[:].rearrange(two, s=S), ALU.add))
                    st.add(v.tensor_tensor(slots_i[:, :, 1, :], run[:, 0, :].rearrange(two, s=S),
                                           off[:].rearrange(two, s=S), ALU.add))
                    st.add(v.tensor_tensor(slots[:, :, 2, :], run[:, 1, :].bitcast(F32).rearrange(two, s=S),
                                           on[:].rearrange(two, s=S), ALU.mult))
                    st.add(v.tensor_scalar(slots[:, :, 3, :], off[:].rearrange(two, s=S), LOW / FAR, None, ALU.mult))
                    st.wait()
                    v.sem_inc(sems["slots"], 1)
                    assert st.n == PER

        @block.gpsimd
        def _(pool):
            nc.gpsimd.iota(slot_i[:], [[1, RUN]], base=0, channel_multiplier=0).then_inc(sems["zero"], 1)
            with pool.Fori(0, T) as t:
                lo, hi = bounds(pool, kp, t, 1)
                with pool.Fori(lo, hi) as c:
                    pool.wait_ge(sems["slots"], c + 1)
                    pool.sem_inc(sems["pace"], 1)
                    pool.wait_ge(sems["index"], c + 1)
                    pool.sem_inc(sems["pace"], 1)
                    pool.indirect_dma_start(out=run[:].rearrange("p k s -> p (k s)"), out_offset=None, in_=dr["runs"],
                                            in_offset=bass.IndirectOffsetOnAxis(ap=edge_i[:, 0:1], axis=0),
                                            bounds_check=E - 1, oob_is_err=False).then_inc(sems["runs"], 16)

        @block.sync
        def _(sp):
            sp.sem_inc(sems["stored"], 16)
            sp.sem_inc(sems["slots"], 1)
            with sp.Fori(0, T) as t:
                lo, hi = bounds(sp, kp, t, 1)
                with sp.Fori(lo, hi) as c:
                    sp.wait_ge(sems["slots"], c + 2)
                    sp.dma_start(dr["slots"][bass.ds(c * 2, 2)].rearrange("k p w -> p k w"),
                                 slots[:].rearrange("p k w s -> p k (w s)")).then_inc(sems["stored"], 16)
            last = sp.value_load(kp["sched"][0:1, 1, T:T + 1], min_val=1, max_val=CHUNKS_MAX // 2)
            sp.wait_ge(sems["stored"], last * 16 + 16)
            sp.sem_inc(sems["ended"], 1)
    finish(nc, list(sems.values()))


def transposed(pe, ps, tile, ident, parts=2):
    for k in range(parts):
        ins = pe.transpose(ps[:, k, :], tile[:, k * P:(k + 1) * P], ident)
    return ins


def product(pe, out, lhs_t, weight, bias=None, ones=None, start=True, stop=True):
    parts = lhs_t.shape[1]
    for k in range(parts):
        ins = pe.matmul(out, lhs_t[:, k, :], weight[:, k, :], start=start and k == 0,
                        stop=stop and bias is None and k == parts - 1)
    if bias is not None:
        ins = pe.matmul(out, ones, bias, start=False, stop=stop)
    return ins


def halves(w):
    return w.rearrange("(k p) o -> p k o", p=P)


def project_nodes(nc, io, dr, kp):
    with ExitStack() as ctx:
        def sb(name, shape, dt=F32):
            return ctx.enter_context(nc.sbuf_tensor(name, shape, dt))
        names = ["p_weights", "p_tile", "p_turned", "p_xt", "p_made", "p_actout", "p_dveout", "p_written", "p_index",
                 "p_pace"]
        sems = {n[2:]: nc.alloc_semaphore(n) for n in names}
        w = sb("p_w", [P, 2, 4 * F])
        b = sb("p_b", [1, 4 * F])
        tile = sb("p_tile_sb", [P, F])
        xt = sb("p_xt_sb", [P, 2, P])
        row = sb("p_row", [P, 2 * F])
        node = sb("p_node", [P, 1], I32)
        spare = sb("p_spare", [1, 4], I32)
        ps_t = ctx.enter_context(nc.psum_tensor("p_pst", [P, 4, P], F32))[:, 0:2, :]
        ps = ctx.enter_context(nc.psum_tensor("p_ps", [P, 2, 512], F32))
        block = ctx.enter_context(nc.Block())

        @block.sync
        def _(sp):
            for i, k in enumerate(("q", "skip", "k", "v")):
                sp.dma_start(w[:, :, i * F:(i + 1) * F], halves(io["L0_gnn_W" + k])).then_inc(sems["weights"], 16)
                sp.dma_start(b[:, i * F:(i + 1) * F], rows_of(io["L0_gnn_b" + k])).then_inc(sems["weights"], 16)

        @block.vector
        def _(v):
            with v.Fori(0, T) as t:
                v.wait_ge(sems["turned"], t + 1)
                v.tensor_copy(tile[:], kp["x"][:, bass.ds(t, 1), :].rearrange("p a f -> p (a f)")
                              ).then_inc(sems["tile"], 1)
                v.wait_ge(sems["written"], 16 * t + 16)
                v.tensor_copy(node[:], kp["info"][:, bass.ds(t, 1), 0]).then_inc(sems["index"], 1)
                v.wait_ge(sems["turned"], t + 2)
                v.tensor_copy(xt[:], ps_t[:]).then_inc(sems["xt"], 1)
                v.wait_ge(sems["made"], 2 * t + 1)
                v.tensor_copy(kp["a"][:, bass.ds(t, 1), :].rearrange("p a f -> p (a f)"),
                              ps[:, 0, 0:F]).then_inc(sems["dveout"], 1)
                v.tensor_copy(kp["b"][:, bass.ds(t, 1), :].rearrange("p a f -> p (a f)"),
                              ps[:, 0, F:2 * F]).then_inc(sems["dveout"], 1)

        @block.scalar
        def _(act):
            with act.Fori(0, T) as t:
                act.wait_ge(sems["made"], 2 * t + 2)
                act.wait_ge(sems["written"], 16 * t + 16)
                nc.scalar.activation(row[:], ps[:, 1, :], ACT.Copy).then_inc(sems["actout"], 1)

        @block.tensor
        def _(pe):
            pe.sem_inc(sems["turned"], 1)
            pe.wait_ge(sems["weights"], 16 * 8)
            with pe.Fori(0, T) as t:
                pe.wait_ge(sems["tile"], t + 1)
                transposed(pe, ps_t, tile, kp["ident"][:]).then_inc(sems["turned"], 1)
                pe.wait_ge(sems["xt"], t + 1)
                for g in range(2):
                    pe.wait_ge(sems["dveout" if g == 0 else "actout"], t * (2 - g) + 1)
                    product(pe, ps[:, g, :], xt, w[:, :, g * 512:(g + 1) * 512], b[:, g * 512:(g + 1) * 512],
                            kp["ones"][:, :]).then_inc(sems["made"], 1)

        @block.gpsimd
        def _(pool):
            pool.sem_inc(sems["dveout"], 1)
            pool.sem_inc(sems["actout"], 1)
            prime(pool, dr, spare, sems["written"])
            with pool.Fori(0, T) as t:
                pool.wait_ge(sems["index"], t + 1)
                pool.sem_inc(sems["pace"], 1)
                pool.wait_ge(sems["actout"], t + 2)
                pool.sem_inc(sems["pace"], 1)
                pool.indirect_dma_start(out=dr["kv"], in_=row[:], in_offset=None,
                                        out_offset=bass.IndirectOffsetOnAxis(ap=node[:, 0:1], axis=0)
                                        ).then_inc(sems["written"], 16)
            pool.wait_ge(sems["written"], 16 * T + 16)
    finish(nc, list(sems.values()))


def layer_norm(v, st, sems, small, out, src, gain=None, offset=None):
    st.do(v.bn_stats(small[:, 0:6], src))
    v.sem_inc(sems["stats"], 1)
    st.do(v.bn_aggr(small[:, 6:8], small[:, 0:6]))
    v.tensor_scalar(small[:, 8:9], small[:, 7:8], EPS, None, ALU.add).then_inc(sems["variance"], 1)
    sems["roots_asked"] += 1
    v.wait_ge(sems["root"], sems["roots_before"] + sems["roots_asked"])
    st.do(v.reciprocal(small[:, 10:11], small[:, 9:10]))
    ins = v.tensor_scalar(out, src, small[:, 6:7], small[:, 10:11], ALU.subtract, ALU.mult)
    if gain is not None:
        st.do(ins)
        st.do(v.tensor_tensor(out, out, gain, ALU.mult))
        ins = v.tensor_tensor(out, out, offset, ALU.add)
    return ins


def root_of(act, sems, small, n):
    act.wait_ge(sems["variance"], n)
    act.activation(small[:, 9:10], small[:, 8:9], ACT.Sqrt).then_inc(sems["root"], 1)


def tile_of(buf, t):
    return buf[:, bass.ds(t, 1), :].rearrange("p a f -> p (a f)")


LAYERS = {
    "conv": dict(heads=8, width=2 * F, table="kv", values=F, limit=NP - 1),
    "rel": dict(heads=0, width=F, table="messages", values=0, limit=NP * RELS - 1),
    "gat1": dict(heads=8, width=F + 8, table="gat1", values=0, limit=NP - 1),
    "gat2": dict(heads=1, width=F + 1, table="gat2", values=0, limit=NP - 1),
    "gat3": dict(heads=4, width=F + 4, table="gat3", values=0, limit=NP - 1),
}
PRODUCTS = {
    "conv": ([], []),
    "rel": (["fc1"], []),
    "gat1": (["wb0", "wb1a", "wb1b", "fc2"], ["bb0", "bb1"]),
    "gat2": (["gat"], []),
    "gat3": ([], []),
}
VECTORS = {
    "conv": ["L0_gnn_gamma", "L0_gnn_beta"],
    "rel": ["L2_gnn_attn_l1", "L2_gnn_attn_r1"],
    "gat1": ["L2_gnn_bias1", "L2_gnn_attn_l2", "L2_gnn_attn_r2"],
    "gat2": ["L2_gnn_bias2", "L3_gnn_gat_a_src", "L3_gnn_gat_a_tgt"],
    "gat3": [],
}
NEXT = {"rel": ("gat1", F + 8, 8), "gat1": ("gat2", F + 1, 1), "gat2": ("gat3", F + 4, 4)}


def edge_layer(nc, io, dr, kp, layer):
    cfg = LAYERS[layer]
    H, width, values, table = cfg["heads"], cfg["width"], cfg["values"], dr[cfg["table"]]
    D = F // H if H else 0
    nxt = NEXT.get(layer)
    weights, biases = PRODUCTS[layer]
    scans = layer == "gat2"
    with ExitStack() as ctx:
        def sb(name, shape, dt=F32):
            return ctx.enter_context(nc.sbuf_tensor(f"{layer}_{name}", shape, dt))

        def sem(name):
            s = nc.alloc_semaphore(f"{layer}_{name}")
            all_sems.append(s)
            return s
        all_sems = []
        index_in, extras_in, gathered, released = (
            [sem(f"{n}{b}") for b in range(NB)]
            for n in ("index_in", "extras_in", "gathered", "released"))
        begun, zeroed = sem("begun"), sem("zeroed")
        pace, steps, logits_ready, probs_ready = sem("pace"), sem("steps"), sem("logits_ready"), sem("probs_ready")
        loaded, rows_ready, written, xt_ready = sem("loaded"), sem("rows_ready"), sem("written"), sem("xt_ready")
        turned, made, pre_gelu, gelu_done = sem("turned"), sem("made"), sem("pre_gelu"), sem("gelu_done")
        new_x, evacuated, index_ready = sem("new_x"), sem("evacuated"), sem("index_ready")
        norm_sems = {"stats": sem("stats"), "variance": sem("variance"), "root": sem("root")}

        index = [sb(f"index{b}", [P, MB], I32) for b in range(NB)]
        extras = [sb(f"extras{b}", [P, 2, MB]) for b in range(NB)]
        rows = [sb(f"rows{b}", [P, MB, width]) for b in range(NB)]
        acc, red = sb("acc", [P, F]), sb("red", [P, F])
        work = sb("work", [P, MB, F])
        own = sb("own", [P, F if layer == "conv" else 8])
        h = max(H, 1)
        logit, logit2 = sb("logit", [P, MB + 1, h]), sb("logit2", [P, MB, h])
        prob = sb("prob", [P, MB + 1, h])
        top, new_top, den, part = (sb(n, [P, h]) for n in ("top", "newtop", "den", "part"))
        small = sb("small", [P, 12])
        out, tmp, cur = sb("out", [P, F]), sb("tmp", [P, F]), sb("cur", [P, F])
        act_out = sb("actout", [P, F])
        vec = {n: sb("v_" + n, [P, F]) for n in VECTORS[layer]}
        wt = {n: sb("w_" + n, [P, 2, F]) for n in weights}
        bias = {n: sb("b_" + n, [1, F]) for n in biases}
        xt, ht = sb("xt", [P, 2, P]), sb("ht", [P, 2, P])
        stage = sb("stage", [P, nxt[1]]) if nxt else None
        node, spare = sb("node", [P, 2], I32), sb("spare", [1, 4], I32)
        spares = [sb(f"spare{b}", [1, 4], I32) for b in range(NB)]
        banks = [ctx.enter_context(nc.psum_tensor(f"{layer}_ps{k}", [P, 512], F32)) for k in range(5)]
        ps_t, ps_h = (bank[:, 0:F].rearrange("p (k c) -> p k c", k=2) for bank in banks[0:2])
        ps = [bank[:, 0:F] for bank in banks[2:5]]
        block = ctx.enter_context(nc.Block())
        which = 1 if layer == "rel" else 0

        @block.sync
        def _(sp):
            for n in VECTORS[layer]:
                flat = io[n] if len(io[n].shape) == 1 else io[n].rearrange("a b -> (a b)")
                sp.dma_start(vec[n][:], on_all(flat)).then_inc(loaded, 16)
            for n in weights:
                sp.dma_start(wt[n][:], halves(io[n])).then_inc(loaded, 16)
            for n in biases:
                sp.dma_start(bias[n][:], rows_of(io["L2_gnn_" + n])).then_inc(loaded, 16)
            with sp.Fori(0, T) as t:
                lo, hi = bounds(sp, kp, t)
                skip = sp.value_load(kp["sched"][0:1, 2, bass.ds(t, 1)], min_val=0, max_val=T)
                with sp.Fori(lo, hi) as c:
                    record = dr["slots"][bass.ds(c + skip, 1)].rearrange("k p (w s) -> p (k w) s", s=S)
                    for b in range(NB):
                        cols = slice(b * MB, (b + 1) * MB)
                        sp.wait_ge(gathered[b], 16 + c * 16 * MB)
                        sp.dma_start(index[b][:], record[:, which, cols].bitcast(I32)).then_inc(index_in[b], 16)
                        sp.wait_ge(released[b], c + 1)
                        sp.dma_start(extras[b][:], record[:, 2:4, cols]).then_inc(extras_in[b], 16)

        @block.gpsimd
        def _(pool):
            if nxt:
                prime(pool, dr, spare, written)
            for b in range(NB):
                nc.gpsimd.memset(rows[b][:], 0.0).then_inc(zeroed, 1)
                prime(pool, dr, spares[b], gathered[b])
            pool.wait_ge(zeroed, NB)

            def gather(t):
                lo, hi = bounds(pool, kp, t)
                with pool.Fori(lo, hi) as c:
                    for b in range(NB):
                        pool.wait_ge(index_in[b], (c + 1) * 16)
                        pool.sem_inc(pace, 1)
                        pool.wait_ge(released[b], c + 1)
                        pool.sem_inc(pace, 1)
                        for s in range(MB):
                            pool.indirect_dma_start(
                                out=rows[b][:, s, :], out_offset=None, in_=table,
                                in_offset=bass.IndirectOffsetOnAxis(ap=index[b][:, s:s + 1], axis=0),
                                bounds_check=cfg["limit"], oob_is_err=False).then_inc(gathered[b], 16)

            def scatter(t):
                pool.wait_ge(rows_ready, t + 1)
                pool.sem_inc(pace, 1)
                pool.indirect_dma_start(out=dr[nxt[0]], in_=stage[:], in_offset=None,
                                        out_offset=bass.IndirectOffsetOnAxis(ap=node[:, 0:1], axis=0)
                                        ).then_inc(written, 16)
                if scans:
                    pool.indirect_dma_start(out=dr["scan_x"], in_=cur[:], in_offset=None,
                                            out_offset=bass.IndirectOffsetOnAxis(ap=node[:, 1:2], axis=0)
                                            ).then_inc(written, 16)

            gather(0)
            with pool.Fori(1, T) as t:
                gather(t)
                if nxt:
                    scatter(t - 1)
            if nxt:
                scatter(T - 1)
                pool.wait_ge(written, 16 + 16 * T * (1 + scans))

        @block.vector
        def _(v):
            per_chunk, before, after = kp["counts"][layer]
            for b in range(NB):
                v.sem_inc(released[b], 1)
            if VECTORS[layer]:
                v.wait_ge(loaded, 16 * (len(VECTORS[layer]) + len(weights) + len(biases)))
            with v.Fori(0, T) as t:
                lo, hi = bounds(v, kp, t)
                st = Steps(v, steps, t * (before + after) + lo * per_chunk)
                st.add(v.memset(acc[:], 0.0))
                if H:
                    st.add(v.memset(den[:], 0.0))
                    st.add(v.memset(top[:], LOW))
                    if layer == "conv":
                        st.add(v.tensor_copy(own[:], tile_of(kp["a"], t)))
                    else:
                        st.add(v.tensor_copy(own[:, 0:H], kp["er"][:, bass.ds(t, 1), 0:H].rearrange("p a h -> p (a h)")))
                st.wait()
                v.sem_inc(begun, 1)
                assert st.n == before, (layer, "before", st.n)
                with v.Fori(lo, hi) as c:
                    st = Steps(v, steps, t * (before + after) + before + c * per_chunk)
                    for b in range(NB):
                        v.wait_ge(gathered[b], 16 + (c + 1) * 16 * MB)
                        v.wait_ge(extras_in[b], (c + 1) * 16)
                        if not H:
                            for s in range(MB):
                                ins = v.scalar_tensor_tensor(acc[:], rows[b][:, s, :], extras[b][:, 0, s:s + 1],
                                                             acc[:], ALU.mult, ALU.add)
                                if s < MB - 1:
                                    st.do(ins)
                            ins.then_inc(released[b], 1)
                            v.wait_ge(released[b], c + 2)
                            continue
                        per_head = "p s (h d) -> p s h d"
                        lg = logit[:, 0:MB, :]
                        if layer == "conv":
                            st.do(v.tensor_tensor(work[:], rows[b][:, :, 0:F], over_slots(own[:], MB), ALU.mult))
                            st.do(v.tensor_reduce(lg, work[:].rearrange(per_head, h=H), X, ALU.add))
                        else:
                            st.do(v.tensor_tensor(logit2[:], rows[b][:, :, F:F + H], over_slots(own[:, 0:H], MB),
                                                  ALU.add))
                            st.do(v.scalar_tensor_tensor(lg, logit2[:], 0.2, logit2[:], ALU.mult, ALU.max))
                        st.do(v.tensor_tensor(lg, lg, over_dims(extras[b][:, 1, :], H), ALU.add))
                        st.do(v.tensor_reduce(new_top[:], lg.rearrange("p s h -> p h s"), X, ALU.max))
                        st.do(v.tensor_tensor(new_top[:], new_top[:], top[:], ALU.max))
                        st.add(v.tensor_tensor(lg, lg, over_slots(new_top[:], MB), ALU.subtract))
                        v.tensor_tensor(logit[:, MB, :], top[:], new_top[:], ALU.subtract).then_inc(logits_ready, 1)
                        v.wait_ge(probs_ready, c * NB + b + 1)
                        st.add(v.tensor_copy(top[:], new_top[:]))
                        st.add(v.tensor_tensor(den[:], den[:], prob[:, MB, :], ALU.mult))
                        st.add(v.tensor_reduce(part[:], prob[:, 0:MB, :].rearrange("p s h -> p h s"), X, ALU.add))
                        v.tensor_tensor(work[:].rearrange(per_head, h=H),
                                        rows[b][:, :, values:values + F].rearrange(per_head, h=H),
                                        over_dims(prob[:, 0:MB, :], D), ALU.mult).then_inc(released[b], 1)
                        st.add(v.tensor_tensor(acc[:].rearrange("p (h d) -> p h d", h=H),
                                               acc[:].rearrange("p (h d) -> p h d", h=H),
                                               over_dims(prob[:, MB, :], D), ALU.mult))
                        v.wait_ge(released[b], c + 2)
                        st.add(v.tensor_reduce(red[:], work[:].rearrange("p s f -> p f s"), X, ALU.add))
                        st.wait()
                        st.add(v.tensor_tensor(den[:], den[:], part[:], ALU.add))
                        st.add(v.tensor_tensor(acc[:], acc[:], red[:], ALU.add))
                        st.wait()
                    assert st.n == per_chunk, (layer, "per_chunk", st.n)
                st = Steps(v, steps, t * (before + after) + before + hi * per_chunk)
                sems = norm_sems
                sems["roots_asked"] = 0
                sems["roots_before"] = t * ROOTS[layer]
                x_t = tile_of(kp["x"], t)
                as_heads = "p (h d) -> p h d"
                col = bass.ds(t, 1)

                def normalise_sum():
                    st.do(v.reciprocal(part[:], den[:]))
                    st.do(v.tensor_scalar(part[:], part[:], kp["has_edges"][:, col], None, ALU.mult))
                    st.do(v.tensor_tensor(out[:].rearrange(as_heads, h=H), acc[:].rearrange(as_heads, h=H),
                                          over_dims(part[:], D), ALU.mult))

                def new_rows(src, heads, left, right):
                    d = F // heads
                    st.add(v.tensor_copy(stage[:, 0:F], src))
                    st.do(v.tensor_tensor(tmp[:], src, vec[left][:], ALU.mult))
                    st.do(v.tensor_reduce(stage[:, F:F + heads], tmp[:].rearrange(as_heads, h=heads), X, ALU.add))
                    st.do(v.tensor_tensor(tmp[:], src, vec[right][:], ALU.mult))
                    st.add(v.tensor_copy(node[:, 0:1], kp["info"][:, col, 0]))
                    st.add(v.tensor_copy(node[:, 1:2], kp["info"][:, col, 3]))
                    st.add(v.tensor_reduce(kp["er"][:, col, 0:heads].rearrange("p a h -> p (a h)"),
                                           tmp[:].rearrange(as_heads, h=heads), X, ALU.add))
                    st.wait()
                    v.sem_inc(rows_ready, 1)

                if layer == "conv":
                    normalise_sum()
                    v.tensor_tensor(out[:], out[:], tile_of(kp["b"], t), ALU.add).then_inc(pre_gelu, 1)
                    v.wait_ge(gelu_done, t + 1)
                    st.do(v.tensor_tensor(out[:], act_out[:], x_t, ALU.add))
                    st.do(layer_norm(v, st, sems, small, tmp[:], out[:], vec["L0_gnn_gamma"][:],
                                     vec["L0_gnn_beta"][:]))
                    st.do(v.tensor_tensor(out[:], tmp[:], x_t, ALU.add))
                    st.do(layer_norm(v, st, sems, small, x_t, out[:]))
                elif layer == "rel":
                    st.do(v.scalar_tensor_tensor(out[:], acc[:], 0.0, x_t, ALU.max, ALU.add))
                    st.do(layer_norm(v, st, sems, small, cur[:], out[:]))
                    v.sem_inc(new_x, 1)
                    st.add(v.tensor_copy(x_t, cur[:]))
                    v.wait_ge(turned, t + 1)
                    v.tensor_copy(xt[:], ps_t[:]).then_inc(xt_ready, 1)
                    v.wait_ge(made, t + 1)
                    v.wait_ge(written, 16 + 16 * t)
                    new_rows(ps[0][:], 8, "L2_gnn_attn_l1", "L2_gnn_attn_r1")
                elif layer == "gat1":
                    v.tensor_copy(cur[:], x_t).then_inc(new_x, 1)
                    normalise_sum()
                    st.do(v.tensor_tensor(out[:], out[:], vec["L2_gnn_bias1"][:], ALU.add))
                    v.wait_ge(turned, 2 * t + 1)
                    v.tensor_copy(xt[:], ps_t[:]).then_inc(xt_ready, 1)
                    v.wait_ge(made, 2 * t + 1)
                    st.do(v.scalar_tensor_tensor(out[:], ps[0][:], kp["inv_deg"][:, col], out[:], ALU.mult, ALU.add))
                    v.wait_ge(turned, 2 * t + 1)
                    v.tensor_scalar(cur[:], out[:], 0.0, None, ALU.max).then_inc(new_x, 1)
                    v.wait_ge(turned, 2 * t + 2)
                    v.tensor_copy(ht[:], ps_h[:]).then_inc(xt_ready, 1)
                    v.wait_ge(made, 2 * t + 2)
                    st.add(v.tensor_copy(tile_of(kp["a"], t), ps[1][:]))
                    v.wait_ge(written, 16 + 16 * t)
                    new_rows(ps[2][:], 1, "L2_gnn_attn_l2", "L2_gnn_attn_r2")
                elif layer == "gat2":
                    normalise_sum()
                    st.do(v.tensor_tensor(out[:], out[:], vec["L2_gnn_bias2"][:], ALU.add))
                    st.do(v.scalar_tensor_tensor(out[:], tile_of(kp["a"], t), kp["inv_deg"][:, col], out[:],
                                                 ALU.mult, ALU.add))
                    st.do(v.tensor_tensor(out[:], out[:], x_t, ALU.add))
                    v.wait_ge(written, 16 + 32 * t)
                    st.do(layer_norm(v, st, sems, small, cur[:], out[:]))
                    v.sem_inc(new_x, 1)
                    st.add(v.tensor_copy(x_t, cur[:]))
                    v.wait_ge(turned, t + 1)
                    v.tensor_copy(xt[:], ps_t[:]).then_inc(xt_ready, 1)
                    v.wait_ge(made, t + 1)
                    new_rows(ps[0][:], 4, "L3_gnn_gat_a_src", "L3_gnn_gat_a_tgt")
                else:
                    st.add(v.tensor_copy(tile_of(kp["a"], t), acc[:]))
                    st.add(v.tensor_copy(kp["den"][:, col, :].rearrange("p a h -> p (a h)"), den[:]))
                    st.add(v.tensor_copy(kp["top"][:, col, :].rearrange("p a h -> p (a h)"), top[:]))
                    st.wait()
                assert st.n == after, (layer, "after", st.n)

        @block.scalar
        def _(act):
            with act.Fori(0, T) as t:
                if H:
                    lo, hi = bounds(act, kp, t)
                    with act.Fori(lo, hi) as c:
                        for b in range(NB):
                            act.wait_ge(logits_ready, c * NB + b + 1)
                            act.activation(prob[:], logit[:], ACT.Exp,
                                           scale=float(D) ** -0.5 if layer == "conv" else 1.0
                                           ).then_inc(probs_ready, 1)
                if layer == "conv":
                    act.wait_ge(pre_gelu, t + 1)
                    act.activation(act_out[:], out[:], ACT.Gelu).then_inc(gelu_done, 1)
                for k in range(ROOTS[layer]):
                    root_of(act, norm_sems, small, t * ROOTS[layer] + k + 1)

        @block.tensor
        def _(pe):
            ident, ones = kp["ident"][:], kp["ones"][:, :]
            if nxt:
                pe.wait_ge(loaded, 16 * (len(VECTORS[layer]) + len(weights) + len(biases)))
                with pe.Fori(0, T) as t:
                    if layer == "gat1":
                        pe.wait_ge(new_x, 2 * t + 1)
                        transposed(pe, ps_t, cur, ident).then_inc(turned, 1)
                        pe.wait_ge(xt_ready, 2 * t + 1)
                        product(pe, ps[1][:], xt, wt["wb1a"], bias["bb1"][:], ones, stop=False)
                        product(pe, ps[0][:], xt, wt["wb0"], bias["bb0"][:], ones).then_inc(made, 1)
                        pe.wait_ge(new_x, 2 * t + 2)
                        transposed(pe, ps_h, cur, ident).then_inc(turned, 1)
                        pe.wait_ge(xt_ready, 2 * t + 2)
                        product(pe, ps[1][:], ht, wt["wb1b"], start=False)
                        product(pe, ps[2][:], ht, wt["fc2"]).then_inc(made, 1)
                    else:
                        pe.wait_ge(new_x, t + 1)
                        transposed(pe, ps_t, cur, ident).then_inc(turned, 1)
                        pe.wait_ge(xt_ready, t + 1)
                        product(pe, ps[0][:], xt, wt[weights[0]]).then_inc(made, 1)
    finish(nc, all_sems)


ROOTS = {"conv": 2, "rel": 1, "gat1": 0, "gat2": 1, "gat3": 0}


def relation_messages(nc, io, dr, kp):
    with ExitStack() as ctx:
        def sb(name, shape, dt=F32):
            return ctx.enter_context(nc.sbuf_tensor(name, shape, dt))
        names = ["r_loaded", "r_weights", "r_tile", "r_turned", "r_xt", "r_made", "r_actout", "r_dveout", "r_index",
                 "r_written0", "r_written1", "r_pace"]
        sems = {n[2:]: nc.alloc_semaphore(n) for n in names}
        bases = sb("r_bases", [P, BASES, 2, F])
        comp = sb("r_comp", [P, RELS * BASES])
        w = sb("r_w", [P, 2, RELS * F])
        stage = [sb(f"r_stage{k}", [P, RELS * F // 2]) for k in range(2)]
        tile, xt = sb("r_tile_sb", [P, F]), sb("r_xt_sb", [P, 2, P])
        node = [sb(f"r_node{k}", [P, 1], I32) for k in range(2)]
        spare = [sb(f"r_spare{k}", [1, 4], I32) for k in range(2)]
        ps_t = ctx.enter_context(nc.psum_tensor("r_pst", [P, 4, P], F32))[:, 0:2, :]
        ps = ctx.enter_context(nc.psum_tensor("r_ps", [P, 4, 512], F32))
        G = RELS * F // 512
        written = [sems["written0"], sems["written1"]]
        half_rows = dr["messages"].rearrange("(n k r) f -> (n k) (r f)", k=2, r=RELS // 2)
        block = ctx.enter_context(nc.Block())

        @block.sync
        def _(sp):
            for b in range(BASES):
                sp.dma_start(bases[:, b, :, :], halves(io["L1_gnn_bases"][b])).then_inc(sems["loaded"], 16)
            sp.dma_start(comp[:], on_all(io["L1_gnn_w_comp"].rearrange("r b -> (r b)"))).then_inc(sems["loaded"], 16)

        @block.vector
        def _(v):
            v.wait_ge(sems["loaded"], 16 * (BASES + 1))
            with v.Fori(0, RELS) as r:
                dst = w[:, :, bass.ds(r * F, F)]
                for b in range(BASES):
                    scale = comp[:, bass.ds(r * BASES + b, 1)]
                    if b == 0:
                        ins = v.tensor_scalar(dst, bases[:, 0, :, :], scale, None, ALU.mult)
                    else:
                        ins = v.scalar_tensor_tensor(dst, bases[:, b, :, :], scale, dst, ALU.mult, ALU.add)
                    ins.then_inc(sems["weights"], 1)
                    v.wait_ge(sems["weights"], r * BASES + b + 1)
            with v.Fori(0, T) as t:
                v.wait_ge(sems["turned"], t + 1)
                v.tensor_copy(tile[:], tile_of(kp["x"], t)).then_inc(sems["tile"], 1)
                v.wait_ge(sems["turned"], t + 2)
                v.tensor_copy(xt[:], ps_t).then_inc(sems["xt"], 1)
                for k in range(2):
                    v.wait_ge(written[k], 16 * t + 16)
                    v.tensor_scalar(node[k][:], kp["info"][:, bass.ds(t, 1), 0], 2.0, float(k), ALU.mult,
                                    ALU.add).then_inc(sems["index"], 1)
                    for g in range(k * G // 2 + 1, (k + 1) * G // 2, 2):
                        v.wait_ge(sems["made"], t * G + g + 1)
                        v.tensor_copy(stage[k][:, (g % (G // 2)) * 512:(g % (G // 2) + 1) * 512],
                                      ps[:, g % 4, :]).then_inc(sems["dveout"], 1)

        @block.scalar
        def _(act):
            with act.Fori(0, T) as t:
                for k in range(2):
                    act.wait_ge(written[k], 16 * t + 16)
                    for g in range(k * G // 2, (k + 1) * G // 2, 2):
                        act.wait_ge(sems["made"], t * G + g + 1)
                        act.activation(stage[k][:, (g % (G // 2)) * 512:(g % (G // 2) + 1) * 512], ps[:, g % 4, :],
                                       ACT.Copy).then_inc(sems["actout"], 1)

        @block.tensor
        def _(pe):
            pe.sem_inc(sems["turned"], 1)
            pe.sem_inc(sems["actout"], 2)
            pe.sem_inc(sems["dveout"], 2)
            pe.wait_ge(sems["weights"], RELS * BASES)
            with pe.Fori(0, T) as t:
                pe.wait_ge(sems["tile"], t + 1)
                transposed(pe, ps_t, tile, kp["ident"][:]).then_inc(sems["turned"], 1)
                pe.wait_ge(sems["xt"], t + 1)
                for g in range(G):
                    pe.wait_ge(sems["dveout" if g % 2 else "actout"], t * (G // 2) + g // 2 + 1)
                    product(pe, ps[:, g % 4, :], xt, w[:, :, g * 512:(g + 1) * 512]).then_inc(sems["made"], 1)

        @block.gpsimd
        def _(pool):
            for k in range(2):
                prime(pool, dr, spare[k], written[k])
            with pool.Fori(0, T) as t:
                for k in range(2):
                    for s, n in (("index", t * 2 + k + 1), ("actout", t * (G // 2) + (k + 1) * G // 4 + 2),
                                 ("dveout", t * (G // 2) + (k + 1) * G // 4 + 2)):
                        pool.wait_ge(sems[s], n)
                        pool.sem_inc(sems["pace"], 1)
                    pool.indirect_dma_start(out=half_rows, in_=stage[k][:], in_offset=None,
                                            out_offset=bass.IndirectOffsetOnAxis(ap=node[k][:, 0:1], axis=0)
                                            ).then_inc(written[k], 16)
            for k in range(2):
                pool.wait_ge(written[k], 16 * T + 16)
    finish(nc, list(sems.values()))


def state_scan(nc, io, dr, kp):
    NS, R = 16, 16
    with ExitStack() as ctx:
        def sb(name, shape, dt=F32):
            return ctx.enter_context(nc.sbuf_tensor("m_" + name, shape, dt))
        names = ["loaded", "steps", "rows", "turned", "xt", "xz", "neg", "exp", "xc", "dbc", "dbc_out", "spread_w",
                 "spread", "dt", "soft_a", "soft_b", "dt_ready", "decay", "z_exp", "y", "made", "yout", "stored", "alog"]
        sems = {n: nc.alloc_semaphore("m_" + n) for n in names}
        w_in, w_out, w_x = sb("win", [P, 2, 2 * F]), sb("wout", [P, 2, F]), sb("wx", [P, 2, R + 2 * NS])
        w_dt = sb("wdt", [R, F])
        cw, cb, db, dp = sb("cw", [P, 2, 4]), sb("cb", [P, 2]), sb("db", [P, 2]), sb("dp", [P, 2])
        a = sb("a", [P, 2, NS])
        xs, xst = sb("xs", [P, F]), sb("xst", [P, 2, P])
        seq = sb("seq", [P, 2, P + 3])
        cv, ex, xc, zz = sb("cv", [P, 2, P]), sb("ex", [P, 2, P]), sb("xc", [P, 2, P]), sb("zz", [P, 2, P])
        ez = sb("ez", [P, 2, P])
        dbc = sb("dbc", [R + 2 * NS, P])
        bc = sb("bc", [P, 2, NS, P])
        u, dt, dtx, e, w1, d1, ln, z0 = (sb(n, [P, 2, P]) for n in ("u", "dt", "dtx", "e", "w1", "d1", "ln", "z0"))
        da, db_x, hs = sb("da", [P, 2, NS, P]), sb("dbx", [P, 2, NS, P]), sb("hs", [P, 2, NS, P])
        last = sb("last", [P, 2, NS])
        y, yr = sb("y", [P, 2, P]), sb("yr", [P, F])
        bank = [ctx.enter_context(nc.psum_tensor(f"m_ps{k}", [P, 512], F32)) for k in range(5)]
        ps_t = bank[0][:, 0:F].rearrange("p (k c) -> p k c", k=2)
        ps_xz = bank[1][:].rearrange("p (k c) -> p k c", k=4)
        ps_d = bank[2][0:R + 2 * NS, 0:P]
        ps_dt = bank[3][:, 0:F].rearrange("p (k c) -> p k c", k=2)
        ps_o = bank[4][:, 0:F]
        block = ctx.enter_context(nc.Block())
        LOADS = 9

        def per_channel(vec):
            return vec.rearrange("(k p) -> p k", p=P)

        @block.sync
        def _(sp):
            with nc.allow_non_contiguous_dma(reason="one word per channel"):
                for dst, src in ((w_in, halves(io["in_proj"])), (w_out, halves(io["out_proj"])),
                                 (w_x, halves(io["x_proj"])), (w_dt, io["dt_proj"]),
                                 (cw, halves(io["L3_gnn_conv_w"])), (cb, per_channel(io["L3_gnn_conv_b"])),
                                 (db, per_channel(io["L3_gnn_dt_proj_b"])), (dp, per_channel(io["L3_gnn_D_param"])),
                                 (a, halves(io["L3_gnn_A_log"]))):
                    sp.dma_start(dst[:], src).then_inc(sems["loaded"], 16)
            with sp.Fori(0, T) as t:
                sp.wait_ge(sems["turned"], t + 1)
                sp.dma_start(xs[:], dr["scan_x"][bass.ds(t * P, P), :]).then_inc(sems["rows"], 16)
                sp.wait_ge(sems["dbc_out"], t + 1)
                sp.dma_start(dr["bc"], dbc[R:R + 2 * NS, :]).then_inc(sems["spread_w"], 16)
                sp.wait_ge(sems["spread_w"], 16 * t + 16)
                sp.dma_start(bc[:].rearrange("p k n c -> p (k n c)"), on_all(dr["bc"].rearrange("a c -> (a c)"))
                             ).then_inc(sems["spread"], 16)
                sp.wait_ge(sems["yout"], t + 1)
                sp.dma_start(dr["scan_y"][bass.ds(t * P, P), :], yr[:]).then_inc(sems["stored"], 16)
            sp.wait_ge(sems["stored"], 16 * T + 16)

        @block.tensor
        def _(pe):
            pe.sem_inc(sems["turned"], 1)
            pe.wait_ge(sems["loaded"], 16 * LOADS)
            with pe.Fori(0, T) as t:
                pe.wait_ge(sems["rows"], 16 * t + 16)
                transposed(pe, ps_t, xs, kp["ident"][:]).then_inc(sems["turned"], 1)
                pe.wait_ge(sems["xt"], t + 1)
                for m in range(4):
                    for k in range(2):
                        ins = pe.matmul(ps_xz[:, m, :], w_in[:, k, m * P:(m + 1) * P], xst[:, k, :], start=k == 0,
                                        stop=k == 1)
                ins.then_inc(sems["xz"], 1)
                pe.wait_ge(sems["xc"], t + 1)
                for k in range(2):
                    ins = pe.matmul(ps_d, w_x[:, k, :], xc[:, k, :], start=k == 0, stop=k == 1)
                ins.then_inc(sems["dbc"], 1)
                pe.wait_ge(sems["dbc_out"], t + 1)
                for k in range(2):
                    ins = pe.matmul(ps_dt[:, k, :], w_dt[:, k * P:(k + 1) * P], dbc[0:R, :], start=True, stop=True)
                ins.then_inc(sems["dt"], 1)
                pe.wait_ge(sems["y"], t + 1)
                for k in range(2):
                    ins = pe.matmul(ps_o, y[:, k, :], w_out[:, k, :], start=k == 0, stop=k == 1)
                ins.then_inc(sems["made"], 1)

        @block.scalar
        def _(act):
            act.wait_ge(sems["loaded"], 16 * LOADS)
            act.activation(a[:], a[:], ACT.Exp).then_inc(sems["alog"], 1)
            with act.Fori(0, T) as t:
                act.wait_ge(sems["turned"], t + 2)
                act.activation(xst[:], ps_t, ACT.Copy).then_inc(sems["xt"], 1)
                act.wait_ge(sems["neg"], t + 1)
                act.activation(ex[:], cv[:], ACT.Exp, scale=-1.0).then_inc(sems["exp"], 1)
                act.activation(ez[:], zz[:], ACT.Exp, scale=-1.0).then_inc(sems["z_exp"], 1)
                act.wait_ge(sems["soft_a"], 2 * t + 1)
                act.activation(e[:], d1[:], ACT.Exp, scale=-1.0).then_inc(sems["soft_b"], 1)
                act.wait_ge(sems["soft_a"], 2 * t + 2)
                act.activation(ln[:], w1[:], ACT.Ln).then_inc(sems["soft_b"], 1)
                act.wait_ge(sems["dt_ready"], t + 1)
                for k in range(2):
                    for n in range(NS):
                        ins = act.activation(da[:, k, n, :], dt[:, k, :], ACT.Exp, scale=a[:, k, n:n + 1])
                ins.then_inc(sems["decay"], 1)
                act.wait_ge(sems["made"], t + 1)
                act.wait_ge(sems["stored"], 16 * t + 16)
                act.activation(yr[:], ps_o, ACT.Copy).then_inc(sems["yout"], 1)

        @block.gpsimd
        def _(pool):
            pool.sem_inc(sems["stored"], 16)

        @block.vector
        def _(v):
            PER = 68
            st = Steps(v, sems["steps"])
            st.add(v.memset(seq[:], 0.0))
            st.add(v.memset(last[:], 0.0))
            v.wait_ge(sems["alog"], 1)
            st.add(v.tensor_scalar(a[:], a[:], -1.0, None, ALU.mult))
            st.wait()
            with v.Fori(0, T) as t:
                st = Steps(v, sems["steps"], 3 + t * PER)
                st.do(v.tensor_copy(seq[:, :, 0:3], seq[:, :, P:P + 3]))
                v.wait_ge(sems["xz"], t + 1)
                st.do(v.tensor_copy(seq[:, :, 3:P + 3], ps_xz[:, 0:2, :]))
                st.add(v.tensor_copy(zz[:], ps_xz[:, 2:4, :]))
                for k in range(2):
                    st.do(v.tensor_scalar(cv[:, k, :], seq[:, k, 0:P], cw[:, k, 0:1], cb[:, k:k + 1], ALU.mult, ALU.add))
                    for j in range(1, 4):
                        st.do(v.scalar_tensor_tensor(cv[:, k, :], seq[:, k, j:j + P], cw[:, k, j:j + 1], cv[:, k, :],
                                                     ALU.mult, ALU.add))
                v.sem_inc(sems["neg"], 1)
                v.wait_ge(sems["exp"], t + 1)
                st.do(v.tensor_scalar(ex[:], ex[:], 1.0, None, ALU.add))
                st.do(v.reciprocal(ex[:], ex[:]))
                v.tensor_tensor(xc[:], cv[:], ex[:], ALU.mult).then_inc(sems["xc"], 1)
                v.wait_ge(sems["xc"], t + 1)
                v.wait_ge(sems["z_exp"], t + 1)
                st.do(v.tensor_scalar(ez[:], ez[:], 1.0, None, ALU.add))
                st.do(v.reciprocal(ez[:], ez[:]))
                st.add(v.tensor_tensor(zz[:], zz[:], ez[:], ALU.mult))
                v.wait_ge(sems["dbc"], t + 1)
                v.tensor_copy(dbc[:], ps_d).then_inc(sems["dbc_out"], 1)
                v.wait_ge(sems["dt"], t + 1)
                for k in range(2):
                    st.do(v.tensor_scalar(u[:, k, :], ps_dt[:, k, :], db[:, k:k + 1], None, ALU.add))
                st.do(v.scalar_tensor_tensor(d1[:], u[:], -1.0, u[:], ALU.mult, ALU.max))
                v.sem_inc(sems["soft_a"], 1)
                v.wait_ge(sems["soft_b"], 2 * t + 1)
                v.tensor_scalar(w1[:], e[:], 1.0, None, ALU.add).then_inc(sems["soft_a"], 1)
                v.wait_ge(sems["soft_a"], 2 * t + 2)
                st.do(v.tensor_scalar(d1[:], w1[:], -1.0, None, ALU.add))
                st.do(v.tensor_scalar(z0[:], d1[:], 0.0, None, ALU.is_equal))
                st.do(v.tensor_tensor(d1[:], d1[:], z0[:], ALU.add))
                st.do(v.reciprocal(d1[:], d1[:]))
                v.wait_ge(sems["soft_b"], 2 * t + 2)
                st.do(v.tensor_tensor(d1[:], d1[:], ln[:], ALU.mult))
                st.do(v.tensor_tensor(d1[:], d1[:], z0[:], ALU.add))
                st.do(v.tensor_tensor(d1[:], d1[:], e[:], ALU.mult))
                v.scalar_tensor_tensor(dt[:], u[:], 0.0, d1[:], ALU.max, ALU.add).then_inc(sems["dt_ready"], 1)
                v.wait_ge(sems["dt_ready"], t + 1)
                st.do(v.tensor_tensor(dtx[:], dt[:], xc[:], ALU.mult))
                v.wait_ge(sems["spread"], 16 * t + 16)
                for k in range(2):
                    st.add(v.tensor_tensor(db_x[:, k, :, :], over_slots(dtx[:, k, :], NS), bc[:, 0, :, :], ALU.mult))
                st.wait()
                v.wait_ge(sems["decay"], t + 1)
                for k in range(2):
                    for n in range(NS):
                        st.add(v.tensor_tensor_scan(hs[:, k, n, :], da[:, k, n, :], db_x[:, k, n, :],
                                                    last[:, k, n:n + 1], ALU.mult, ALU.add))
                st.wait()
                st.add(v.tensor_copy(last[:], hs[:, :, :, P - 1]))
                for k in range(2):
                    st.do(v.tensor_tensor(db_x[:, k, :, :], hs[:, k, :, :], bc[:, 1, :, :], ALU.mult))
                    st.do(v.tensor_reduce(y[:, k, :], db_x[:, k, :, :].rearrange("p n c -> p c n"), X, ALU.add))
                    st.do(v.scalar_tensor_tensor(y[:, k, :], xc[:, k, :], dp[:, k:k + 1], y[:, k, :], ALU.mult,
                                                 ALU.add))
                v.tensor_tensor(y[:], y[:], zz[:], ALU.mult).then_inc(sems["y"], 1)
                v.wait_ge(sems["y"], t + 1)
                assert st.n == PER, st.n
    finish(nc, list(sems.values()))


def join(nc, io, dr, kp, result):
    with ExitStack() as ctx:
        def sb(name, shape, dt=F32):
            return ctx.enter_context(nc.sbuf_tensor("j_" + name, shape, dt))
        names = ["loaded", "steps", "gathered", "gmax_in", "gmax_turned", "gmax_row", "gmax_spread", "top_ready",
                 "top_exp", "elu_in", "elu_exp", "stats", "variance", "root", "turn", "turned", "copied", "made", "gate_in",
                 "gate_exp", "out_ready", "written", "pace"]
        sems = {n: nc.alloc_semaphore("j_" + n) for n in names}
        vectors = ["gat_b", "ln_local_g", "ln_local_b", "ln_global_g", "ln_global_b", "ln2_g", "ln2_b"]
        vec = {n: sb("v_" + n, [P, F]) for n in vectors}
        wl, wg = sb("wl", [P, 2, F]), sb("wg", [P, 2, F])
        w1, w2 = sb("w1", [P, 2, 2 * F]), sb("w2", [P, 4, F])
        b1, b2 = sb("b1", [1, 2 * F]), sb("b2", [1, F])
        fac = sb("fac", [P, T, 4])
        gm, grow, gall = sb("gm", [P, 1]), sb("grow", [1, 1]), sb("gall", [P, 1])
        small = sb("small", [P, 12])
        u, ev, hl, ha, s, g = (sb(n, [P, F]) for n in ("u", "ev", "hl", "ha", "s", "g"))
        hlt, hat, ht, ft = sb("hlt", [P, 2, P]), sb("hat", [P, 2, P]), sb("ht", [P, 2, P]), sb("ft", [P, 4, P])
        h, f, o = sb("h", [P, F]), sb("f", [P, 2 * F]), sb("o", [P, F])
        node, spare = sb("node", [P, 1], I32), sb("spare", [1, 4], I32)
        bank = [ctx.enter_context(nc.psum_tensor(f"j_ps{k}", [P, 4, P], F32)) for k in range(6)]
        block = ctx.enter_context(nc.Block())
        LOADS = len(vectors) + 6

        @block.sync
        def _(sp):
            for n in vectors:
                sp.dma_start(vec[n][:], on_all(io["L3_gnn_" + n])).then_inc(sems["loaded"], 16)
            for dst, src in ((wl, halves(io["wl"])), (wg, halves(io["wg"])), (w1, halves(io["ff1"])),
                             (w2, halves(io["ff2"])), (b1, rows_of(io["L3_gnn_ff1_b"])),
                             (b2, rows_of(io["L3_gnn_ff2_b"]))):
                sp.dma_start(dst[:], src).then_inc(sems["loaded"], 16)

        @block.gpsimd
        def _(pool):
            for t in range(T):
                pool.indirect_dma_start(out=kp["b"][:, t, :], out_offset=None, in_=dr["scan_y"],
                                        in_offset=bass.IndirectOffsetOnAxis(ap=kp["info"][:, t, 3:4], axis=0),
                                        bounds_check=NP - 1, oob_is_err=False).then_inc(sems["gathered"], 16)
            prime(pool, dr, spare, sems["written"])
            with pool.Fori(0, T) as t:
                pool.wait_ge(sems["out_ready"], t + 1)
                pool.sem_inc(sems["pace"], 1)
                pool.indirect_dma_start(out=result, in_=o[:], in_offset=None,
                                        out_offset=bass.IndirectOffsetOnAxis(ap=node[:, 0:1], axis=0),
                                        bounds_check=N - 1, oob_is_err=False).then_inc(sems["written"], 16)
            pool.wait_ge(sems["written"], 16 * T + 16)

        @block.tensor
        def _(pe):
            ident, ones = kp["ident"][:], kp["ones"][:, :]
            pe.wait_ge(sems["loaded"], 16 * LOADS)
            pe.wait_ge(sems["gmax_in"], 1)
            pe.transpose(bank[0][0:1, 0, :], gm[:], ident).then_inc(sems["gmax_turned"], 1)
            pe.wait_ge(sems["gmax_row"], 1)
            pe.matmul(bank[1][:, 0, 0:1], ones, grow[:], start=True, stop=True).then_inc(sems["gmax_spread"], 1)
            with pe.Fori(0, T) as t:
                pe.wait_ge(sems["turn"], t * 4 + 1)
                transposed(pe, bank[0], hl, ident).then_inc(sems["turned"], 1)
                pe.wait_ge(sems["turn"], t * 4 + 2)
                transposed(pe, bank[1], ha, ident).then_inc(sems["turned"], 1)
                pe.wait_ge(sems["copied"], t * 4 + 2)
                ps = bank[2][:, 0:2, :].rearrange("p k c -> p (k c)")
                product(pe, ps, hlt, wl, stop=False)
                product(pe, ps, hat, wg, start=False).then_inc(sems["made"], 1)
                pe.wait_ge(sems["turn"], t * 4 + 3)
                transposed(pe, bank[0], h, ident).then_inc(sems["turned"], 1)
                pe.wait_ge(sems["copied"], t * 4 + 3)
                product(pe, bank[3][:].rearrange("p k c -> p (k c)"), ht, w1, b1[:], ones).then_inc(sems["made"], 1)
                pe.wait_ge(sems["turn"], t * 4 + 4)
                transposed(pe, bank[4], f, ident, 4).then_inc(sems["turned"], 1)
                pe.wait_ge(sems["copied"], t * 4 + 4)
                product(pe, bank[5][:, 0:2, :].rearrange("p k c -> p (k c)"), ft, w2, b2[:], ones
                        ).then_inc(sems["made"], 1)

        @block.scalar
        def _(act):
            act.wait_ge(sems["top_ready"], 1)
            act.activation(fac[:], fac[:], ACT.Exp).then_inc(sems["top_exp"], 1)
            with act.Fori(0, T) as t:
                act.wait_ge(sems["elu_in"], t + 1)
                act.activation(ev[:], ev[:], ACT.Exp).then_inc(sems["elu_exp"], 1)
                root_of(act, sems, small, t * 4 + 1)
                root_of(act, sems, small, t * 4 + 2)
                for i, (dst, src) in enumerate(((hlt, bank[0][:, 0:2, :]), (hat, bank[1][:, 0:2, :]),
                                                (ht, bank[0][:, 0:2, :]), (ft, bank[4][:]))):
                    act.wait_ge(sems["turned"], t * 4 + i + 1)
                    act.activation(dst[:], src, ACT.Copy).then_inc(sems["copied"], 1)
                    if i == 1:
                        act.wait_ge(sems["gate_in"], t + 1)
                        act.activation(g[:], g[:], ACT.Exp, scale=-1.0).then_inc(sems["gate_exp"], 1)
                root_of(act, sems, small, t * 4 + 3)
                root_of(act, sems, small, t * 4 + 4)

        @block.vector
        def _(v):
            BEFORE, PER = 4, 33
            st = Steps(v, sems["steps"])
            v.tensor_reduce(gm[:], kp["top"][:].rearrange("p t h -> p (t h)"), X, ALU.max).then_inc(sems["gmax_in"], 1)
            v.wait_ge(sems["gmax_turned"], 1)
            v.tensor_reduce(grow[:], bank[0][0:1, 0, :], X, ALU.max).then_inc(sems["gmax_row"], 1)
            v.wait_ge(sems["gmax_spread"], 1)
            st.do(v.tensor_copy(gall[:], bank[1][:, 0, 0:1]))
            v.tensor_scalar(fac[:], kp["top"][:], gall[:], None, ALU.subtract).then_inc(sems["top_ready"], 1)
            v.wait_ge(sems["top_exp"], 1)
            st.do(v.tensor_tensor(kp["den"][:], kp["den"][:], fac[:], ALU.mult))
            st.do(v.tensor_scalar(kp["den"][:], kp["den"][:], 1e-16, None, ALU.add))
            st.do(v.reciprocal(kp["den"][:], kp["den"][:]))
            v.tensor_tensor(fac[:], fac[:], kp["den"][:], ALU.mult).then_inc(sems["top_ready"], 1)
            v.wait_ge(sems["top_ready"], 2)
            v.wait_ge(sems["loaded"], 16 * LOADS)
            v.wait_ge(sems["gathered"], 16 * T)
            with v.Fori(0, T) as t:
                st = Steps(v, sems["steps"], BEFORE + t * PER)
                sems["roots_asked"], sems["roots_before"] = 0, t * 4
                x_t = tile_of(kp["x"], t)
                st.do(v.tensor_tensor(u[:].rearrange("p (h d) -> p h d", h=4),
                                      kp["a"][:, bass.ds(t, 1), :].rearrange("p a (h d) -> p (a h) d", h=4),
                                      over_dims(fac[:, bass.ds(t, 1), :].rearrange("p a h -> p (a h)"), F // 4),
                                      ALU.mult))
                st.do(v.tensor_tensor(u[:], u[:], x_t, ALU.add))
                st.do(v.tensor_tensor(u[:], u[:], vec["gat_b"][:], ALU.add))
                v.tensor_scalar(ev[:], u[:], 0.0, None, ALU.min).then_inc(sems["elu_in"], 1)
                v.wait_ge(sems["elu_exp"], t + 1)
                st.do(v.scalar_tensor_tensor(u[:], u[:], 0.0, ev[:], ALU.max, ALU.add))
                st.do(v.tensor_scalar(u[:], u[:], -1.0, None, ALU.add))
                layer_norm(v, st, sems, small, hl[:], u[:], vec["ln_local_g"][:], vec["ln_local_b"][:]
                           ).then_inc(sems["turn"], 1)
                st.do(v.tensor_tensor(s[:], x_t, tile_of(kp["b"], t), ALU.add))
                layer_norm(v, st, sems, small, ha[:], s[:], vec["ln_global_g"][:], vec["ln_global_b"][:]
                           ).then_inc(sems["turn"], 1)
                v.wait_ge(sems["made"], t * 3 + 1)
                v.tensor_copy(g[:], bank[2][:, 0:2, :].rearrange("p k c -> p (k c)")).then_inc(sems["gate_in"], 1)
                v.wait_ge(sems["gate_exp"], t + 1)
                st.do(v.tensor_scalar(g[:], g[:], 1.0, None, ALU.add))
                st.do(v.reciprocal(g[:], g[:]))
                v.wait_ge(sems["turn"], t * 4 + 2)
                st.do(v.tensor_tensor(u[:], hl[:], ha[:], ALU.subtract))
                st.do(v.tensor_tensor(u[:], u[:], g[:], ALU.mult))
                v.tensor_tensor(h[:], u[:], ha[:], ALU.add).then_inc(sems["turn"], 1)
                v.wait_ge(sems["made"], t * 3 + 2)
                v.tensor_scalar(f[:], bank[3][:].rearrange("p k c -> p (k c)"), 0.0, None, ALU.max
                                ).then_inc(sems["turn"], 1)
                v.wait_ge(sems["made"], t * 3 + 3)
                st.do(v.tensor_tensor(u[:], h[:], bank[5][:, 0:2, :].rearrange("p k c -> p (k c)"), ALU.add))
                st.do(layer_norm(v, st, sems, small, s[:], u[:], vec["ln2_g"][:], vec["ln2_b"][:]))
                st.do(v.tensor_tensor(s[:], s[:], x_t, ALU.add))
                v.wait_ge(sems["written"], 16 * t + 16)
                st.add(v.tensor_copy(node[:], kp["info"][:, bass.ds(t, 1), 0]))
                st.do(layer_norm(v, st, sems, small, o[:], s[:]))
                v.sem_inc(sems["out_ready"], 1)
                assert st.n == PER, st.n
    finish(nc, [sems[n] for n in names])


def network(nc, io, result):
    def scratch(name, shape, dt=F32):
        return nc.dram_tensor("scratch_" + name, shape, dt).ap()
    dr = {
        "indeg": scratch("indeg", (NP,)), "outdeg": scratch("outdeg", (NP,)), "starts": scratch("starts", (NP,)),
        "keys": scratch("keys", (NP,)), "info": scratch("info", (NP, 4), I32),
        "runs": scratch("runs", (E, 2 * RUN), I32), "slots": scratch("slots", (CHUNKS_MAX, P, META)),
        "kv": scratch("kv", (NP, 2 * F)), "messages": scratch("messages", (NP * RELS, F)),
        "gat1": scratch("gat1", (NP, F + 8)), "gat2": scratch("gat2", (NP, F + 1)),
        "gat3": scratch("gat3", (NP, F + 4)), "scan_x": scratch("scan_x", (NP, F)),
        "scan_y": scratch("scan_y", (NP, F)), "bc": scratch("bc", (32, P)),
    }
    count_edges(nc, io, dr)
    order_nodes(nc, io, dr)
    with ExitStack() as ctx:
        def sb(name, shape, dt=F32):
            return ctx.enter_context(nc.sbuf_tensor("k_" + name, shape, dt))
        kp = {
            "info": sb("info", [P, T, 4], I32), "x": sb("x", [P, T, F]), "a": sb("a", [P, T, F]),
            "b": sb("b", [P, T, F]), "er": sb("er", [P, T, 8]), "den": sb("den", [P, T, 4]),
            "top": sb("top", [P, T, 4]), "deg": sb("deg", [P, T]), "has_edges": sb("has", [P, T]),
            "inv_deg": sb("inv", [P, T]), "sched": sb("sched", [1, 3, 32], I32), "ident": sb("ident", [P, P]),
            "ones": sb("ones", [1, P]), "slot_no": sb("slotno", [P, S]),
            "counts": COUNTS,
        }
        fetch_nodes(nc, io, dr, kp)
        build_slots(nc, dr, kp)
        project_nodes(nc, io, dr, kp)
        for name in ("conv", "messages", "rel", "gat1", "gat2", "gat3", "scan", "join"):
            if name == "messages":
                relation_messages(nc, io, dr, kp)
            elif name == "scan":
                state_scan(nc, io, dr, kp)
            elif name == "join":
                join(nc, io, dr, kp, result)
            else:
                edge_layer(nc, io, dr, kp, name)


COUNTS = {"conv": (26, 4, 15), "rel": (3 * NB, 1, 13), "gat1": (26, 4, 13), "gat2": (26, 4, 18),
          "gat3": (26, 4, 3)}

DIRECT = ["x", "src", "dst", "edge_type_32", "edge_weight1", "node_vec",
          "L0_gnn_Wq", "L0_gnn_bq", "L0_gnn_Wk", "L0_gnn_bk", "L0_gnn_Wv", "L0_gnn_bv", "L0_gnn_Wskip", "L0_gnn_bskip",
          "L0_gnn_gamma", "L0_gnn_beta", "L1_gnn_bases", "L1_gnn_w_comp", "L2_gnn_attn_l1", "L2_gnn_attn_r1",
          "L2_gnn_bias1", "L2_gnn_attn_l2", "L2_gnn_attn_r2", "L2_gnn_bias2", "L2_gnn_bb0", "L2_gnn_bb1",
          "L3_gnn_gat_a_src", "L3_gnn_gat_a_tgt", "L3_gnn_gat_b", "L3_gnn_ln_local_g", "L3_gnn_ln_local_b",
          "L3_gnn_ln_global_g", "L3_gnn_ln_global_b", "L3_gnn_ln2_g", "L3_gnn_ln2_b", "L3_gnn_conv_w",
          "L3_gnn_conv_b", "L3_gnn_dt_proj_b", "L3_gnn_A_log", "L3_gnn_D_param", "L3_gnn_ff1_b", "L3_gnn_ff2_b"]
TURNED = {"fc1": "L2_gnn_fc1_w", "fc2": "L2_gnn_fc2_w", "wb0": "L2_gnn_wb0", "gat": "L3_gnn_gat_w",
          "in_proj": "L3_gnn_in_proj_w", "x_proj": "L3_gnn_x_proj_w", "dt_proj": "L3_gnn_dt_proj_w",
          "out_proj": "L3_gnn_out_proj_w", "wl": "L3_gnn_wl", "wg": "L3_gnn_wg", "ff1": "L3_gnn_ff1_w",
          "ff2": "L3_gnn_ff2_w"}


def kernel(**inputs):
    import numpy as np
    import concourse.bacc as bacc
    from concourse.bass_utils import run_bass_kernel_spmd

    nc = bacc.Bacc("TRN2", target_bir_lowering=False, num_devices=1)
    arrays = {n: np.ascontiguousarray(inputs[n]) for n in DIRECT}
    arrays.update({n: np.ascontiguousarray(np.asarray(inputs[src]).T) for n, src in TURNED.items()})
    both = np.asarray(inputs["L2_gnn_wb1"]).T
    arrays["wb1a"], arrays["wb1b"] = np.ascontiguousarray(both[:F]), np.ascontiguousarray(both[F:])
    io = {n: nc.dram_tensor("in_" + n, a.shape, mybir.dt.from_np(a.dtype), kind="ExternalInput").ap()
          for n, a in arrays.items()}
    result = nc.dram_tensor("out_x", (N, F), F32, kind="ExternalOutput").ap()
    network(nc, io, result)
    r = run_bass_kernel_spmd(nc, [{"in_" + n: a for n, a in arrays.items()}], core_ids=[0])
    return r.results[0]["out_x"]
```

```python
from contextlib import ExitStack

import concourse.bass as bass
from concourse import mybir

F32 = mybir.dt.float32
I32 = mybir.dt.int32
BF16 = mybir.dt.bfloat16
ALU = mybir.AluOpType
ACT = mybir.ActivationFunctionType
X = mybir.AxisListType.X

P = 128
N = 3125
E = 103125
F = 256
T = (N + P - 1) // P
NP = T * P
RELS = 32
BASES = 8
EP = 125
EC = E // EP
HIST_HI, HIST_LO = 49, 64
HB = 32
EC_PAD = 832
S = 8
RUN = 16
MB = 4
NB = S // MB
META = 4 * S
CHUNKS_MAX = 2 * ((E + E // P + P) // RUN + 2 * T + 2)
FAR = 1.0e6
LOW = -1.0e30
EPS = 1e-5
assert E == EP * EC and HIST_HI * HIST_LO >= N and EC_PAD % (2 * HB) == 0


class Steps:

    def __init__(self, eng, sem, base=0):
        self.eng, self.sem, self.base, self.n = eng, sem, base, 0

    def add(self, ins):
        ins.then_inc(self.sem, 1)
        self.n += 1

    def wait(self):
        self.eng.wait_ge(self.sem, self.base + self.n)

    def do(self, ins):
        self.add(ins)
        self.wait()


def over_slots(ap, n):
    return ap.unsqueeze(1).to_broadcast([ap.shape[0], n, ap.shape[1]])


def over_dims(ap, n):
    return ap.unsqueeze(len(ap.shape)).to_broadcast(list(ap.shape) + [n])


def rows_of(vec):
    return vec.rearrange("(a f) -> a f", a=1)


def on_all(vec, n=P):
    return rows_of(vec).to_broadcast([n, vec.shape[0]])


def prime(pool, dr, spare, sem):
    pool.dma_start(spare[:], dr["info"][0:1, :]).then_inc(sem, 16)


def finish(nc, sems):
    nc.clear_and_free_semaphores(sems)
    nc.all_engine_barrier()


def count_edges(nc, io, dr):
    with ExitStack() as ctx:
        def sb(name, shape, dt=F32):
            return ctx.enter_context(nc.sbuf_tensor(name, shape, dt))
        names = ["e_pads", "e_loaded", "e_iota", "e_steps", "e_casts", "e_hot0", "e_hot1", "e_summed0", "e_summed1",
                 "e_zeroed", "e_hist", "e_counts", "e_packed", "e_runs", "e_actruns", "e_stored"]
        sems = {n[2:]: nc.alloc_semaphore(n) for n in names}
        hot, summed = [sems["hot0"], sems["hot1"]], [sems["summed0"], sems["summed1"]]
        W = EC + RUN
        dst = sb("e_dst", [EP, EC_PAD], I32)
        src = sb("e_src", [EP, W], I32)
        rel = sb("e_rel", [EP, W], I32)
        nrm = sb("e_nrm", [EP, W])
        packed = sb("e_pack", [EP, W], I32)
        part_i = sb("e_parti", [EP, EC_PAD], I32)
        parts = {k: sb("e_part" + k, [EP, EC_PAD], BF16) for k in ("dh", "dl", "sh", "sl")}
        iota_i = sb("e_ioi", [EP, HIST_LO], I32)
        iota = sb("e_io", [EP, HIST_LO], BF16)
        ones_at = {k: [sb(f"e_hot{k}{b}", [EP, HB, HIST_HI if k[1] == "h" else HIST_LO], BF16) for b in range(2)]
                   for k in parts}
        runs = sb("e_runs_sb", [EP, EC, 2 * RUN], I32)
        zero = sb("e_zero", [EP, HIST_LO], BF16)
        counts = sb("e_counts_sb", [HIST_HI, 2, HIST_LO])
        zrow = sb("e_zrow", [1, 64])
        ps = ctx.enter_context(nc.psum_tensor("e_ps", [HIST_HI, 2, 512], F32))
        block = ctx.enter_context(nc.Block())

        @block.sync
        def _(sp):
            sp.wait_ge(sems["pads"], 3)
            sp.dma_start(dst[:, 0:EC], io["dst"].rearrange("(p c) -> p c", p=EP)).then_inc(sems["loaded"], 16)
            for tile, name in ((src, "src"), (rel, "edge_type_32"), (nrm, "edge_weight1")):
                flat = io[name] if name != "edge_weight1" else io[name].rearrange("e a -> (e a)")
                rows = flat.rearrange("(p c) -> p c", p=EP)
                sp.dma_start(tile[:, 0:EC], rows).then_inc(sems["loaded"], 16)
                sp.dma_start(tile[0:EP - 1, EC:W], rows[1:EP, 0:RUN]).then_inc(sems["loaded"], 16)
            sp.wait_ge(sems["counts"], 2)
            for k, name in enumerate(("indeg", "outdeg")):
                sp.dma_start(dr[name][0:HIST_HI * HIST_LO].rearrange("(h l) -> h l", h=HIST_HI),
                             counts[:, k, :]).then_inc(sems["stored"], 16)
                sp.dma_start(rows_of(dr[name][HIST_HI * HIST_LO:NP]), zrow[:, :]).then_inc(sems["stored"], 16)
            sp.wait_ge(sems["runs"], RUN)
            sp.wait_ge(sems["actruns"], RUN)
            sp.dma_start(dr["runs"].rearrange("(p c) w -> p c w", p=EP), runs[:]).then_inc(sems["stored"], 16)
            sp.wait_ge(sems["stored"], 16 * 5)

        @block.gpsimd
        def _(pool):
            nc.gpsimd.memset(src[:, EC:W], 0).then_inc(sems["pads"], 1)
            nc.gpsimd.memset(rel[:, EC:W], 0).then_inc(sems["pads"], 1)
            nc.gpsimd.memset(nrm[:, EC:W], 0.0).then_inc(sems["pads"], 1)
            nc.gpsimd.iota(iota_i[:], [[1, HIST_LO]], base=0, channel_multiplier=0).then_inc(sems["iota"], 1)

        @block.vector
        def _(v):
            st = Steps(v, sems["steps"])
            st.add(nc.vector.memset(zero[:], 0.0))
            st.add(nc.vector.memset(zrow[:], 0.0))
            for k in parts:
                st.add(nc.vector.memset(parts[k][:, EC:EC_PAD], 16384.0))
            v.wait_ge(sems["iota"], 1)
            st.do(nc.vector.tensor_copy(iota[:], iota_i[:]))
            v.wait_ge(sems["loaded"], 16 * 7)
            for k, tile in (("d", dst), ("s", src)):
                st.do(nc.vector.tensor_scalar(part_i[:, 0:EC], tile[:, 0:EC], 6, None, ALU.logical_shift_right))
                st.do(nc.vector.tensor_copy(parts[k + "h"][:, 0:EC], part_i[:, 0:EC]))
                st.do(nc.vector.tensor_scalar(part_i[:, 0:EC], tile[:, 0:EC], 63, None, ALU.bitwise_and))
                st.do(nc.vector.tensor_copy(parts[k + "l"][:, 0:EC], part_i[:, 0:EC]))
            nc.vector.scalar_tensor_tensor(packed[:], src[:], float(RELS), rel[:], ALU.mult,
                                           ALU.add).then_inc(sems["packed"], 1)
            with v.Fori(0, EC_PAD // HB // 2) as i:
                for b in range(2):
                    v.wait_ge(summed[b], i + 1)
                    for k in ("dh", "dl", "sh", "sl"):
                        w = HIST_HI if k[1] == "h" else HIST_LO
                        cols = parts[k][:, bass.ds((2 * i + b) * HB, HB)]
                        ins = nc.vector.tensor_tensor(ones_at[k][b][:], over_dims(cols, w),
                                                      over_slots(iota[:, 0:w], HB), ALU.is_equal)
                    ins.then_inc(hot[b], 1)
            v.wait_ge(sems["packed"], 1)
            for s in range(RUN):
                nc.vector.tensor_copy(runs[:, :, s], packed[:, s:s + EC]).then_inc(sems["runs"], 1)
            v.wait_ge(sems["hist"], 1)
            for k in range(2):
                nc.vector.tensor_copy(counts[:, k, :], ps[:, k, 0:HIST_LO]).then_inc(sems["counts"], 1)

        @block.scalar
        def _(act):
            act.wait_ge(sems["loaded"], 16 * 7)
            for s in range(RUN):
                nc.scalar.activation(runs[:, :, RUN + s].bitcast(F32), nrm[:, s:s + EC],
                                     ACT.Copy).then_inc(sems["actruns"], 1)

        @block.tensor
        def _(pe):
            pe.sem_inc(summed[0], 1)
            pe.sem_inc(summed[1], 1)
            pe.wait_ge(sems["steps"], 1)
            for k in range(2):
                nc.tensor.matmul(ps[:, k, 0:HIST_LO], zero[:, 0:HIST_HI], zero[:, :], start=True, stop=False)
            with pe.Fori(0, EC_PAD // HB // 2) as i:
                for b in range(2):
                    pe.wait_ge(hot[b], i + 1)
                    for c in range(HB):
                        for k, (h, l) in enumerate((("dh", "dl"), ("sh", "sl"))):
                            ins = nc.tensor.matmul(ps[:, k, 0:HIST_LO], ones_at[h][b][:, c, :], ones_at[l][b][:, c, :],
                                                   start=False, stop=False, skip_group_check=True)
                    ins.then_inc(summed[b], 1)
            for k in range(2):
                ins = nc.tensor.matmul(ps[:, k, 0:HIST_LO], zero[:, 0:HIST_HI], zero[:, :], start=False, stop=True)
            ins.then_inc(sems["hist"], 1)
    finish(nc, list(sems.values()))


def rank(v, st, out, keys_all, keys_own, before, upto_own, tri, junk, cnt):
    for t in range(T):
        own = keys_own[:, t:t + 1]
        lo, hi = t * P, (t + 1) * P
        if t:
            st.add(v.tensor_scalar(junk[:, 0:lo], keys_all[:, 0:lo], own, 0.0, upto_own, ALU.add,
                                         accum_out=cnt[:, 0:1]))
        else:
            st.add(v.memset(cnt[:, 0:1], 0.0))
        if t < T - 1:
            st.add(v.tensor_scalar(junk[:, hi:NP], keys_all[:, hi:NP], own, 0.0, before, ALU.add,
                                         accum_out=cnt[:, 1:2]))
        else:
            st.add(v.memset(cnt[:, 1:2], 0.0))
        st.add(v.tensor_scalar(junk[:, lo:hi], keys_all[:, lo:hi], own, 0.0, before, ALU.add,
                                     accum_out=cnt[:, 2:3]))
        st.wait()
        st.do(v.scalar_tensor_tensor(junk[:, lo:hi], keys_all[:, lo:hi], own, tri, ALU.is_equal, ALU.mult,
                                           accum_out=cnt[:, 3:4]))
        st.do(v.tensor_reduce(out[:, t:t + 1], cnt[:, 0:4], X, ALU.add))


def order_nodes(nc, io, dr):
    with ExitStack() as ctx:
        def sb(name, shape, dt=F32):
            return ctx.enter_context(nc.sbuf_tensor(name, shape, dt))
        names = ["n_pad", "n_loaded", "n_iota", "n_steps", "n_starts", "n_stored", "n_reloaded", "n_keys",
                 "n_info", "n_scattered"]
        sems = {n[2:]: nc.alloc_semaphore(n) for n in names}
        deg_all = sb("n_degall", [P, NP])
        key_all = sb("n_keyall", [P, NP])
        junk = sb("n_junk", [P, NP], BF16)
        row = sb("n_row", [1, NP])
        cum = sb("n_cum", [1, NP])
        zero = sb("n_zero", [1, NP])
        deg, start, key, nv = (sb("n_" + k, [P, T]) for k in ("deg", "start", "key", "nv"))
        node_i = sb("n_nodei", [P, T], I32)
        by_deg, by_key = sb("n_bydeg", [P, T]), sb("n_bykey", [P, T])
        place = sb("n_place", [P, T], I32)
        info = sb("n_infosb", [P, T, 4], I32)
        cnt = sb("n_cnt", [P, 4])
        lane_i, col_i = sb("n_lanei", [P, 1], I32), sb("n_coli", [P, P], I32)
        lane, col, tri = sb("n_lane", [P, 1]), sb("n_col", [P, P]), sb("n_tri", [P, P])
        block = ctx.enter_context(nc.Block())
        by_col = "(t p) -> p t"
        whole = (T - 1) * P

        @block.sync
        def _(sp):
            with nc.allow_non_contiguous_dma(reason="one word per node"):
                sp.dma_start(deg_all[:], on_all(dr["indeg"])).then_inc(sems["loaded"], 16)
                sp.dma_start(row[:], rows_of(dr["indeg"])).then_inc(sems["loaded"], 16)
                sp.dma_start(deg[:], dr["indeg"].rearrange(by_col, p=P)).then_inc(sems["loaded"], 16)
                sp.dma_start(key[:], dr["outdeg"].rearrange(by_col, p=P)).then_inc(sems["loaded"], 16)
                sp.wait_ge(sems["pad"], 1)
                sp.dma_start(nv[:, 0:T - 1], io["node_vec"][0:whole].rearrange(by_col, p=P)).then_inc(sems["loaded"], 16)
                sp.dma_start(nv[0:N - whole, T - 1:T],
                             io["node_vec"][whole:N].rearrange("(p a) -> p a", a=1)).then_inc(sems["loaded"], 16)
                sp.wait_ge(sems["starts"], 1)
                sp.dma_start(rows_of(dr["starts"]), cum[:]).then_inc(sems["stored"], 16)
                sp.wait_ge(sems["keys"], 1)
                sp.dma_start(dr["keys"].rearrange(by_col, p=P), key[:]).then_inc(sems["stored"], 16)
                sp.wait_ge(sems["stored"], 32)
                sp.dma_start(start[:], dr["starts"].rearrange(by_col, p=P)).then_inc(sems["reloaded"], 16)
                sp.dma_start(key_all[:], on_all(dr["keys"])).then_inc(sems["reloaded"], 16)

        @block.gpsimd
        def _(pool):
            nc.gpsimd.memset(nv[:], 1.0e30).then_inc(sems["pad"], 1)
            nc.gpsimd.iota(lane_i[:], [[0, 1]], base=0, channel_multiplier=1).then_inc(sems["iota"], 1)
            nc.gpsimd.iota(col_i[:], [[1, P]], base=0, channel_multiplier=0).then_inc(sems["iota"], 1)
            nc.gpsimd.iota(node_i[:], [[P, T]], base=0, channel_multiplier=1).then_inc(sems["iota"], 1)
            pool.wait_ge(sems["info"], 1)
            for t in range(T):
                pool.indirect_dma_start(out=dr["info"], in_=info[:, t, :], in_offset=None,
                                        out_offset=bass.IndirectOffsetOnAxis(ap=place[:, t:t + 1], axis=0)
                                        ).then_inc(sems["scattered"], 16)
            pool.wait_ge(sems["scattered"], 16 * T)

        @block.vector
        def _(v):
            st = Steps(v, sems["steps"])
            v.wait_ge(sems["iota"], 3)
            st.add(v.tensor_copy(lane[:], lane_i[:]))
            st.add(v.tensor_copy(col[:], col_i[:]))
            st.add(v.memset(zero[:], 0.0))
            st.wait()
            st.do(v.tensor_scalar(tri[:], col[:], lane[:], None, ALU.is_lt))
            v.wait_ge(sems["loaded"], 16 * 6)
            st.do(v.tensor_tensor_scan(cum[:], row[:], zero[:], 0.0, ALU.add, ALU.add))
            v.tensor_tensor(cum[:], cum[:], row[:], ALU.subtract).then_inc(sems["starts"], 1)
            v.tensor_tensor(key[:], key[:], nv[:], ALU.add).then_inc(sems["keys"], 1)
            rank(v, st, by_deg, deg_all, deg, ALU.is_gt, ALU.is_ge, tri[:], junk, cnt)
            v.wait_ge(sems["reloaded"], 32)
            v.wait_ge(sems["keys"], 1)
            rank(v, st, by_key, key_all, key, ALU.is_lt, ALU.is_le, tri[:], junk, cnt)
            st.add(v.tensor_copy(info[:, :, 0], node_i[:]))
            st.add(v.tensor_copy(info[:, :, 1], start[:]))
            st.add(v.tensor_copy(info[:, :, 2], deg[:]))
            st.add(v.tensor_copy(info[:, :, 3], by_key[:]))
            v.tensor_copy(place[:], by_deg[:]).then_inc(sems["info"], 1)
    finish(nc, list(sems.values()))


def fetch_nodes(nc, io, dr, kp):
    with ExitStack() as ctx:
        def sb(name, shape, dt=F32):
            return ctx.enter_context(nc.sbuf_tensor(name, shape, dt))
        names = ["f_loaded", "f_steps", "f_zero", "f_nodes", "f_iota"]
        sems = {n[2:]: nc.alloc_semaphore(n) for n in names}
        first = sb("f_first", [1, T], I32)
        per_i = sb("f_per", [1, 3, T], I32)
        per = sb("f_perf", [1, 3, T])
        cum = sb("f_cum", [1, 3, T])
        zero = sb("f_zero_sb", [1, T])
        deg_i = sb("f_degi", [P, T], I32)
        i1, i2, i3 = sb("f_i1", [P, P], I32), sb("f_i2", [P, 1], I32), sb("f_i3", [P, S], I32)
        f1, f2 = sb("f_f1", [P, P]), sb("f_f2", [P, 1])
        block = ctx.enter_context(nc.Block())

        @block.sync
        def _(sp):
            with nc.allow_non_contiguous_dma(reason="records of four words"):
                sp.dma_start(kp["info"][:], dr["info"].rearrange("(t p) w -> p t w", p=P)).then_inc(sems["loaded"], 16)
                sp.dma_start(first[:], dr["info"].rearrange("(t p) w -> p w t", p=P)[0:1, 2, :]
                             ).then_inc(sems["loaded"], 16)
            sp.wait_ge(sems["loaded"], 32)

        @block.gpsimd
        def _(pool):
            nc.gpsimd.iota(i1[:], [[1, P]], base=0, channel_multiplier=0).then_inc(sems["iota"], 1)
            nc.gpsimd.iota(i2[:], [[0, 1]], base=0, channel_multiplier=1).then_inc(sems["iota"], 1)
            nc.gpsimd.iota(i3[:], [[1, S]], base=0, channel_multiplier=0).then_inc(sems["iota"], 1)
            nc.gpsimd.memset(kp["x"][:], 0.0).then_inc(sems["zero"], 1)
            pool.wait_ge(sems["zero"], 1)
            pool.wait_ge(sems["loaded"], 32)
            for t in range(T):
                pool.indirect_dma_start(out=kp["x"][:, t, :], out_offset=None, in_=io["x"],
                                        in_offset=bass.IndirectOffsetOnAxis(ap=kp["info"][:, t, 0:1], axis=0),
                                        bounds_check=N - 1, oob_is_err=False).then_inc(sems["nodes"], 16)
            pool.wait_ge(sems["nodes"], 16 * T)

        @block.vector
        def _(v):
            st = Steps(v, sems["steps"])
            st.add(v.memset(zero[:], 0.0))
            st.add(v.memset(kp["sched"][:], 0))
            st.add(v.memset(kp["ones"][:], 1.0))
            v.wait_ge(sems["iota"], 3)
            st.add(v.tensor_copy(f1[:], i1[:]))
            st.add(v.tensor_copy(f2[:], i2[:]))
            st.add(v.tensor_copy(kp["slot_no"][:], i3[:]))
            st.wait()
            st.add(v.tensor_scalar(kp["ident"][:], f1[:], f2[:], None, ALU.is_equal))
            v.wait_ge(sems["loaded"], 32)
            st.do(v.tensor_copy(kp["deg"][:], kp["info"][:, :, 2]))
            st.add(v.tensor_scalar(kp["has_edges"][:], kp["deg"][:], 1.0, None, ALU.min))
            st.do(v.tensor_scalar(kp["inv_deg"][:], kp["deg"][:], 1.0, None, ALU.max))
            st.do(v.reciprocal(kp["inv_deg"][:], kp["inv_deg"][:]))
            st.do(v.tensor_scalar(per[:, 0, :], first[:], float(S - 1), None, ALU.add))
            st.do(v.tensor_copy(per_i[:, 0, :], per[:, 0, :]))
            st.do(v.tensor_scalar(per_i[:, 0, :], per_i[:, 0, :], S.bit_length() - 1, None, ALU.logical_shift_right))
            st.do(v.tensor_scalar(per[:, 0, :], per_i[:, 0, :], 2.0, None, ALU.max))
            st.do(v.tensor_scalar(per[:, 1, :], per[:, 0, :], 1.0, None, ALU.add))
            st.do(v.tensor_copy(per_i[:, 1, :], per[:, 1, :]))
            st.do(v.tensor_scalar(per_i[:, 1, :], per_i[:, 1, :], 1, None, ALU.logical_shift_right))
            st.do(v.tensor_copy(per[:, 1, :], per_i[:, 1, :]))
            st.do(v.tensor_tensor(per[:, 2, :], per[:, 0, :], per[:, 1, :], ALU.subtract))
            st.do(v.tensor_copy(kp["sched"][:, PAIRS, 0:T], per[:, 2, :]))
            st.do(v.tensor_tensor(kp["sched"][:, TAIL, 0:T], per[:, 1, :], per[:, 2, :], ALU.subtract))
            for k in (CHUNKS, USES_0, USES_1):
                st.do(v.tensor_tensor_scan(cum[:, k, :], per[:, k, :], zero[:], 0.0, ALU.add, ALU.add))
                st.do(v.tensor_copy(kp["sched"][:, k, 1:T + 1], cum[:, k, :]))
    finish(nc, list(sems.values()))


def bounds(eng, kp, t):
    lo = eng.value_load(kp["sched"][0:1, 1, bass.ds(t, 1)], min_val=0, max_val=CHUNKS_MAX // 2)
    hi = eng.value_load(kp["sched"][0:1, 1, bass.ds(t + 1, 1)], min_val=1, max_val=CHUNKS_MAX // 2)
    return lo, hi


def build_slots(nc, dr, kp):
    with ExitStack() as ctx:
        def sb(name, shape, dt=F32):
            return ctx.enter_context(nc.sbuf_tensor(name, shape, dt))
        names = ["b_zero", "b_steps", "b_index", "b_runs", "b_slots", "b_stored", "b_pace", "b_begun", "b_ended"]
        sems = {n[2:]: nc.alloc_semaphore(n) for n in names}
        edge = sb("b_edge", [P, 1])
        edge_i = sb("b_edgei", [P, 1], I32)
        left = sb("b_left", [P, 1])
        run = sb("b_run", [P, 2, RUN], I32)
        src = sb("b_src", [P, RUN], I32)
        number = sb("b_number", [P, RUN])
        off, on = sb("b_off", [P, RUN]), sb("b_on", [P, RUN])
        slot_i = sb("b_sloti", [P, RUN], I32)
        slots = sb("b_slots_sb", [P, RUN // S, 4, S])
        slots_i = slots[:].bitcast(I32)
        PRO, PER = 5, 9
        block = ctx.enter_context(nc.Block())
        two = "p (k s) -> p k s"

        @block.vector
        def _(v):
            v.memset(run[:], 0).then_inc(sems["zero"], 1)
            v.wait_ge(sems["zero"], 2)
            v.tensor_copy(number[:], slot_i[:]).then_inc(sems["zero"], 1)
            v.wait_ge(sems["zero"], 3)
            with v.Fori(0, T) as t:
                lo, hi = bounds(v, kp, t)
                st = Steps(v, sems["steps"], t * 2 + lo * PER)
                st.add(v.tensor_copy(edge[:], kp["info"][:, bass.ds(t, 1), 1]))
                st.add(v.tensor_copy(left[:], kp["deg"][:, bass.ds(t, 1)]))
                st.wait()
                v.sem_inc(sems["begun"], 1)
                with v.Fori(lo, hi) as c:
                    st = Steps(v, sems["steps"], t * 2 + 2 + c * PER)
                    v.tensor_copy(edge_i[:], edge[:]).then_inc(sems["index"], 1)
                    st.do(v.tensor_scalar(on[:], number[:], left[:], None, ALU.is_lt))
                    st.do(v.tensor_scalar(off[:], on[:], -FAR, FAR, ALU.mult, ALU.add))
                    st.add(v.tensor_scalar(edge[:], edge[:], float(RUN), None, ALU.add))
                    st.add(v.tensor_scalar(left[:], left[:], float(-RUN), None, ALU.add))
                    v.wait_ge(sems["runs"], (c + 1) * 16)
                    v.wait_ge(sems["stored"], c * 16 + 16)
                    st.do(v.tensor_scalar(src[:], run[:, 0, :], 5, None, ALU.logical_shift_right))
                    st.add(v.tensor_tensor(slots_i[:, :, 0, :], src[:].rearrange(two, s=S),
                                           off[:].rearrange(two, s=S), ALU.add))
                    st.add(v.tensor_tensor(slots_i[:, :, 1, :], run[:, 0, :].rearrange(two, s=S),
                                           off[:].rearrange(two, s=S), ALU.add))
                    st.add(v.tensor_tensor(slots[:, :, 2, :], run[:, 1, :].bitcast(F32).rearrange(two, s=S),
                                           on[:].rearrange(two, s=S), ALU.mult))
                    st.add(v.tensor_scalar(slots[:, :, 3, :], off[:].rearrange(two, s=S), LOW / FAR, None, ALU.mult))
                    st.wait()
                    v.sem_inc(sems["slots"], 1)
                    assert st.n == PER

        @block.gpsimd
        def _(pool):
            nc.gpsimd.iota(slot_i[:], [[1, RUN]], base=0, channel_multiplier=0).then_inc(sems["zero"], 1)
            with pool.Fori(0, T) as t:
                lo, hi = bounds(pool, kp, t)
                with pool.Fori(lo, hi) as c:
                    pool.wait_ge(sems["slots"], c + 1)
                    pool.sem_inc(sems["pace"], 1)
                    pool.wait_ge(sems["index"], c + 1)
                    pool.sem_inc(sems["pace"], 1)
                    pool.indirect_dma_start(out=run[:].rearrange("p k s -> p (k s)"), out_offset=None, in_=dr["runs"],
                                            in_offset=bass.IndirectOffsetOnAxis(ap=edge_i[:, 0:1], axis=0),
                                            bounds_check=E - 1, oob_is_err=False).then_inc(sems["runs"], 16)

        @block.sync
        def _(sp):
            sp.sem_inc(sems["stored"], 16)
            sp.sem_inc(sems["slots"], 1)
            with sp.Fori(0, T) as t:
                lo, hi = bounds(sp, kp, t)
                with sp.Fori(lo, hi) as c:
                    sp.wait_ge(sems["slots"], c + 2)
                    sp.dma_start(dr["slots"][bass.ds(c * 2, 2)].rearrange("k p w -> p k w"),
                                 slots[:].rearrange("p k w s -> p k (w s)")).then_inc(sems["stored"], 16)
            last = sp.value_load(kp["sched"][0:1, 1, T:T + 1], min_val=1, max_val=CHUNKS_MAX // 2)
            sp.wait_ge(sems["stored"], last * 16 + 16)
            sp.sem_inc(sems["ended"], 1)
    finish(nc, list(sems.values()))


def transposed(pe, ps, tile, ident, parts=2):
    for k in range(parts):
        ins = pe.transpose(ps[:, k, :], tile[:, k * P:(k + 1) * P], ident)
    return ins


def product(pe, out, lhs_t, weight, bias=None, ones=None, start=True, stop=True):
    parts = lhs_t.shape[1]
    for k in range(parts):
        ins = pe.matmul(out, lhs_t[:, k, :], weight[:, k, :], start=start and k == 0,
                        stop=stop and bias is None and k == parts - 1)
    if bias is not None:
        ins = pe.matmul(out, ones, bias, start=False, stop=stop)
    return ins


def halves(w):
    return w.rearrange("(k p) o -> p k o", p=P)


def project_nodes(nc, io, dr, kp):
    with ExitStack() as ctx:
        def sb(name, shape, dt=F32):
            return ctx.enter_context(nc.sbuf_tensor(name, shape, dt))
        names = ["p_weights", "p_tile", "p_turned", "p_xt", "p_made", "p_actout", "p_dveout", "p_written", "p_index",
                 "p_pace"]
        sems = {n[2:]: nc.alloc_semaphore(n) for n in names}
        w = sb("p_w", [P, 2, 4 * F])
        b = sb("p_b", [1, 4 * F])
        tile = sb("p_tile_sb", [P, F])
        xt = sb("p_xt_sb", [P, 2, P])
        row = sb("p_row", [P, 2 * F])
        node = sb("p_node", [P, 1], I32)
        spare = sb("p_spare", [1, 4], I32)
        ps_t = ctx.enter_context(nc.psum_tensor("p_pst", [P, 4, P], F32))[:, 0:2, :]
        ps = ctx.enter_context(nc.psum_tensor("p_ps", [P, 2, 512], F32))
        block = ctx.enter_context(nc.Block())

        @block.sync
        def _(sp):
            for i, k in enumerate(("q", "skip", "k", "v")):
                sp.dma_start(w[:, :, i * F:(i + 1) * F], halves(io["L0_gnn_W" + k])).then_inc(sems["weights"], 16)
                sp.dma_start(b[:, i * F:(i + 1) * F], rows_of(io["L0_gnn_b" + k])).then_inc(sems["weights"], 16)

        @block.vector
        def _(v):
            with v.Fori(0, T) as t:
                v.wait_ge(sems["turned"], t + 1)
                v.tensor_copy(tile[:], kp["x"][:, bass.ds(t, 1), :].rearrange("p a f -> p (a f)")
                              ).then_inc(sems["tile"], 1)
                v.wait_ge(sems["written"], 16 * t + 16)
                v.tensor_copy(node[:], kp["info"][:, bass.ds(t, 1), 0]).then_inc(sems["index"], 1)
                v.wait_ge(sems["turned"], t + 2)
                v.tensor_copy(xt[:], ps_t[:]).then_inc(sems["xt"], 1)
                v.wait_ge(sems["made"], 2 * t + 1)
                v.tensor_copy(kp["a"][:, bass.ds(t, 1), :].rearrange("p a f -> p (a f)"),
                              ps[:, 0, 0:F]).then_inc(sems["dveout"], 1)
                v.tensor_copy(kp["b"][:, bass.ds(t, 1), :].rearrange("p a f -> p (a f)"),
                              ps[:, 0, F:2 * F]).then_inc(sems["dveout"], 1)

        @block.scalar
        def _(act):
            with act.Fori(0, T) as t:
                act.wait_ge(sems["made"], 2 * t + 2)
                act.wait_ge(sems["written"], 16 * t + 16)
                nc.scalar.activation(row[:], ps[:, 1, :], ACT.Copy).then_inc(sems["actout"], 1)

        @block.tensor
        def _(pe):
            pe.sem_inc(sems["turned"], 1)
            pe.wait_ge(sems["weights"], 16 * 8)
            with pe.Fori(0, T) as t:
                pe.wait_ge(sems["tile"], t + 1)
                transposed(pe, ps_t, tile, kp["ident"][:]).then_inc(sems["turned"], 1)
                pe.wait_ge(sems["xt"], t + 1)
                for g in range(2):
                    pe.wait_ge(sems["dveout" if g == 0 else "actout"], t * (2 - g) + 1)
                    product(pe, ps[:, g, :], xt, w[:, :, g * 512:(g + 1) * 512], b[:, g * 512:(g + 1) * 512],
                            kp["ones"][:, :]).then_inc(sems["made"], 1)

        @block.gpsimd
        def _(pool):
            pool.sem_inc(sems["dveout"], 1)
            pool.sem_inc(sems["actout"], 1)
            prime(pool, dr, spare, sems["written"])
            with pool.Fori(0, T) as t:
                pool.wait_ge(sems["index"], t + 1)
                pool.sem_inc(sems["pace"], 1)
                pool.wait_ge(sems["actout"], t + 2)
                pool.sem_inc(sems["pace"], 1)
                pool.indirect_dma_start(out=dr["kv"], in_=row[:], in_offset=None,
                                        out_offset=bass.IndirectOffsetOnAxis(ap=node[:, 0:1], axis=0)
                                        ).then_inc(sems["written"], 16)
            pool.wait_ge(sems["written"], 16 * T + 16)
    finish(nc, list(sems.values()))


def normal_stats(v, st, sems, small, src):
    st.do(v.bn_stats(small[:, 0:6], src))
    v.sem_inc(sems["stats"], 1)
    st.do(v.bn_aggr(small[:, 6:8], small[:, 0:6]))
    v.tensor_scalar(small[:, 8:9], small[:, 7:8], EPS, None, ALU.add).then_inc(sems["variance"], 1)


def normal_apply(v, st, sems, small, out, src, n, gain=None, offset=None):
    v.wait_ge(sems["root"], n)
    st.do(v.reciprocal(small[:, 10:11], small[:, 9:10]))
    ins = v.tensor_scalar(out, src, small[:, 6:7], small[:, 10:11], ALU.subtract, ALU.mult)
    if gain is not None:
        st.do(ins)
        st.do(v.tensor_tensor(out, out, gain, ALU.mult))
        ins = v.tensor_tensor(out, out, offset, ALU.add)
    return ins


def root_of(act, sems, small, n):
    act.wait_ge(sems["variance"], n)
    act.activation(small[:, 9:10], small[:, 8:9], ACT.Sqrt).then_inc(sems["root"], 1)


def tile_of(buf, t):
    if isinstance(t, int):
        return buf[:, t, :]
    return buf[:, bass.ds(t, 1), :].rearrange("p a f -> p (a f)")


LAYERS = {
    "conv": dict(heads=8, width=2 * F, table="kv", values=F, limit=NP - 1),
    "rel": dict(heads=0, width=F, table="messages", values=0, limit=NP * RELS - 1),
    "gat1": dict(heads=8, width=F + 8, table="gat1", values=0, limit=NP - 1),
    "gat2": dict(heads=1, width=F + 1, table="gat2", values=0, limit=NP - 1),
    "gat3": dict(heads=4, width=F + 4, table="gat3", values=0, limit=NP - 1),
}
PRODUCTS = {
    "conv": ([], []),
    "rel": (["fc1"], []),
    "gat1": (["wb0", "wb1a", "wb1b", "fc2"], ["bb0", "bb1"]),
    "gat2": (["gat"], []),
    "gat3": ([], []),
}
VECTORS = {
    "conv": ["L0_gnn_gamma", "L0_gnn_beta"],
    "rel": ["L2_gnn_attn_l1", "L2_gnn_attn_r1"],
    "gat1": ["L2_gnn_bias1", "L2_gnn_attn_l2", "L2_gnn_attn_r2"],
    "gat2": ["L2_gnn_bias2", "L3_gnn_gat_a_src", "L3_gnn_gat_a_tgt"],
    "gat3": [],
}
NEXT = {"rel": ("gat1", 8, "fc1"), "gat1": ("gat2", 1, "fc2"), "gat2": ("gat3", 4, "gat")}


CHUNKS, USES_0, USES_1, PAIRS, TAIL = range(5)


class Visit:

    def __init__(self, eng, kp, t):
        def read(row, at, least, most):
            return eng.value_load(kp["sched"][0:1, row, bass.ds(at, 1)], min_val=least, max_val=most)
        self.chunks = read(CHUNKS, t, 0, CHUNKS_MAX)
        self.before = [read(USES_0, t, 0, CHUNKS_MAX // 2), read(USES_1, t, 0, CHUNKS_MAX // 2)]
        self.pairs, self.tail = read(PAIRS, t, 1, E // RUN + 1), read(TAIL, t, 0, 1)
        self.chunks_end = self.chunks + self.pairs * 2 + self.tail

    def uses(self, j, b):
        return self.before[b] + j

    def chunk(self, j, b):
        return self.chunks + j * 2 + b


def visit(eng, kp, t, chunk, in_first=None):
    w = Visit(eng, kp, t)
    if in_first is None:
        with eng.Fori(0, w.pairs) as j:
            chunk(w, j, 0)
            chunk(w, j, 1)
    else:
        in_first(w)
        with eng.If(w.pairs > 1):
            with eng.Fori(1, w.pairs) as j:
                chunk(w, j, 0)
                chunk(w, j, 1)
    with eng.If(w.tail > 0):
        chunk(w, w.pairs, 0)
    return w


def edge_layer(nc, io, dr, kp, layer):
    cfg = LAYERS[layer]
    H, width, values, table = cfg["heads"], cfg["width"], cfg["values"], dr[cfg["table"]]
    D = F // H if H else 0
    nxt = NEXT.get(layer)
    weights, biases = PRODUCTS[layer]
    scans = layer == "gat2"
    with ExitStack() as ctx:
        def sb(name, shape, dt=F32):
            return ctx.enter_context(nc.sbuf_tensor(f"{layer}_{name}", shape, dt))

        def sem(name):
            s = nc.alloc_semaphore(f"{layer}_{name}")
            all_sems.append(s)
            return s
        all_sems = []
        index_in, extras_in, gathered, released = (
            [sem(f"{n}{b}") for b in range(2)] for n in ("index_in", "extras_in", "gathered", "released"))
        begun, zeroed, folded = sem("begun"), sem("zeroed"), sem("folded")
        pace, steps, logits_ready, probs_ready = sem("pace"), sem("steps"), sem("logits_ready"), sem("probs_ready")
        loaded, rows_ready, written, xt_ready = sem("loaded"), sem("rows_ready"), sem("written"), sem("xt_ready")
        turned, made, pre_gelu, gelu_done = sem("turned"), sem("made"), sem("pre_gelu"), sem("gelu_done")
        new_x, ended = sem("new_x"), sem("ended")
        sems = {"stats": sem("stats"), "variance": sem("variance"), "root": sem("root")}

        index = [sb(f"index{b}", [P, S], I32) for b in range(2)]
        extras = [sb(f"extras{b}", [P, 2, S]) for b in range(2)]
        rows = [sb(f"rows{b}", [P, S, width]) for b in range(2)]
        spares = [sb(f"spare{b}", [1, 4], I32) for b in range(3)]
        h = max(H, 1)
        acc, red = sb("acc", [P, F]), sb("red", [P, F])
        work = sb("work", [P, S, F])
        own = sb("own", [P, F if layer == "conv" else 8])
        logit, logit2 = sb("logit", [P, S + 1, h]), sb("logit2", [P, S, h])
        prob = sb("prob", [P, S + 1, h])
        top, new_top, den, part = (sb(n, [P, h]) for n in ("top", "newtop", "den", "part"))
        small = sb("small", [P, 12])
        out, tmp, cur, act_out = sb("out", [P, F]), sb("tmp", [P, F]), sb("cur", [P, F]), sb("actout", [P, F])
        hid = sb("hid", [P, F])
        vec = {n: sb("v_" + n, [P, F]) for n in VECTORS[layer]}
        HN = nxt[1] if nxt else 0
        wide = F + 2 * HN
        wt = {n: sb("w_" + n, [P, 2, wide if nxt and n == nxt[2] else F]) for n in weights}
        bias = {n: sb("b_" + n, [1, F]) for n in biases}
        xt, ht = sb("xt", [P, 2, P]), sb("ht", [P, 2, P])
        stage = sb("stage", [P, F + HN])
        node = sb("node", [P, 2], I32)
        banks = [ctx.enter_context(nc.psum_tensor(f"{layer}_ps{k}", [P, 512], F32)) for k in range(5)]
        ps_t, ps_h = (bank[:, 0:F].rearrange("p (k c) -> p k c", k=2) for bank in banks[0:2])
        ps = banks[2:5]
        loads = 16 * (len(VECTORS[layer]) + len(weights) + len(biases))
        block = ctx.enter_context(nc.Block())
        which = 1 if layer == "rel" else 0
        per_head = "p s (h d) -> p s h d"
        as_heads = "p (h d) -> p h d"

        @block.sync
        def _(sp):
            for n in VECTORS[layer]:
                flat = io[n] if len(io[n].shape) == 1 else io[n].rearrange("a b -> (a b)")
                sp.dma_start(vec[n][:], on_all(flat)).then_inc(loaded, 16)
            for n in weights:
                sp.dma_start(wt[n][:, :, 0:F], halves(io[n])).then_inc(loaded, 16)
            for n in biases:
                sp.dma_start(bias[n][:], rows_of(io["L2_gnn_" + n])).then_inc(loaded, 16)

            def load_record(w, a, b):
                u = w.uses(a, b)
                record = dr["slots"][bass.ds(w.uses(a, 0).with_bounds(min_val=0, max_val=CHUNKS_MAX // 2) * 2 + b, 1)].rearrange("k p (w s) -> p (k w) s", s=S)
                sp.wait_ge(gathered[b], 16 + u * 16 * S)
                sp.dma_start(index[b][:], record[:, which, :].bitcast(I32)).then_inc(index_in[b], 16)
                sp.wait_ge(released[b], u + 1)
                sp.dma_start(extras[b][:], record[:, 2:4, :]).then_inc(extras_in[b], 16)

            with sp.Fori(0, T) as t:
                visit(sp, kp, t, load_record)

        @block.gpsimd
        def _(pool):
            prime(pool, dr, spares[2], written)
            for b in range(2):
                nc.gpsimd.memset(rows[b][:], 0.0).then_inc(zeroed, 1)
                prime(pool, dr, spares[b], gathered[b])
            pool.wait_ge(zeroed, 2)

            def gather(w, a, b):
                u = w.uses(a, b)
                pool.wait_ge(index_in[b], (u + 1) * 16)
                pool.sem_inc(pace, 1)
                pool.wait_ge(released[b], u + 1)
                pool.sem_inc(pace, 1)
                for s in range(S):
                    pool.indirect_dma_start(
                        out=rows[b][:, s, :], out_offset=None, in_=table,
                        in_offset=bass.IndirectOffsetOnAxis(ap=index[b][:, s:s + 1], axis=0),
                        bounds_check=cfg["limit"], oob_is_err=False).then_inc(gathered[b], 16)

            def scatter(t):
                pool.wait_ge(rows_ready, t + 2)
                pool.sem_inc(pace, 1)
                pool.indirect_dma_start(out=dr[nxt[0]], in_=stage[:], in_offset=None,
                                        out_offset=bass.IndirectOffsetOnAxis(ap=node[:, 0:1], axis=0)
                                        ).then_inc(written, 16)
                if scans:
                    pool.indirect_dma_start(out=dr["scan_x"], in_=cur[:], in_offset=None,
                                            out_offset=bass.IndirectOffsetOnAxis(ap=node[:, 1:2], axis=0)
                                            ).then_inc(written, 16)

            visit(pool, kp, 0, gather)
            with pool.Fori(1, T) as t:
                visit(pool, kp, t, gather)
                if nxt:
                    scatter(t - 1)
            if nxt:
                scatter(T - 1)
            pool.wait_ge(written, 16 + (16 * T * (1 + scans) if nxt else 0))

        @block.vector
        def _(v):
            PER, PRO, END, HOOKS, START = kp["counts"][layer]
            TILE = PRO + END + HOOKS
            for b in range(2):
                v.sem_inc(released[b], 1)
            st = Steps(v, steps)
            if loads:
                v.wait_ge(loaded, loads)
            if nxt:
                left, right = VECTORS[layer][-2:]
                full = wt[nxt[2]]
                for k in range(2):
                    for i, name in enumerate((left, right)):
                        st.do(v.tensor_tensor(tmp[:], full[:, k, 0:F], vec[name][:], ALU.mult))
                        st.do(v.tensor_reduce(full[:, k, F + i * HN:F + (i + 1) * HN],
                                              tmp[:].rearrange(as_heads, h=HN), X, ALU.add))
                v.sem_inc(folded, 1)
            assert st.n == START, (layer, 4, st.n)

            def logits(st, w, a, b):
                u = w.uses(a, b)
                v.wait_ge(gathered[b], 16 + (u + 1) * 16 * S)
                v.wait_ge(extras_in[b], (u + 1) * 16)
                if not H:
                    for s in range(S):
                        ins = v.scalar_tensor_tensor(acc[:], rows[b][:, s, :], extras[b][:, 0, s:s + 1], acc[:],
                                                     ALU.mult, ALU.add)
                        if s < S - 1:
                            st.do(ins)
                    ins.then_inc(released[b], 1)
                    v.wait_ge(released[b], u + 2)
                    return
                lg = logit[:, 0:S, :]
                if layer == "conv":
                    st.do(v.tensor_tensor(work[:], rows[b][:, :, 0:F], over_slots(own[:], S), ALU.mult))
                    st.do(v.tensor_reduce(lg, work[:].rearrange(per_head, h=H), X, ALU.add))
                else:
                    st.do(v.tensor_tensor(logit2[:], rows[b][:, :, F:F + H], over_slots(own[:, 0:H], S), ALU.add))
                    st.do(v.scalar_tensor_tensor(lg, logit2[:], 0.2, logit2[:], ALU.mult, ALU.max))
                st.do(v.tensor_tensor(lg, lg, over_dims(extras[b][:, 1, :], H), ALU.add))
                st.do(v.tensor_reduce(new_top[:], lg.rearrange("p s h -> p h s"), X, ALU.max))
                st.do(v.tensor_tensor(new_top[:], new_top[:], top[:], ALU.max))
                st.add(v.tensor_tensor(lg, lg, over_slots(new_top[:], S), ALU.subtract))
                v.tensor_tensor(logit[:, S, :], top[:], new_top[:], ALU.subtract).then_inc(logits_ready, 1)

            def weigh(st, w, a, b):
                if not H:
                    return
                u = w.uses(a, b)
                v.wait_ge(probs_ready, w.chunk(a, b) + 1)
                v.tensor_tensor(work[:].rearrange(per_head, h=H),
                                rows[b][:, :, values:values + F].rearrange(per_head, h=H),
                                over_dims(prob[:, 0:S, :], D), ALU.mult).then_inc(released[b], 1)
                st.add(v.tensor_copy(top[:], new_top[:]))
                st.add(v.tensor_tensor(den[:], den[:], prob[:, S, :], ALU.mult))
                st.add(v.tensor_reduce(part[:], prob[:, 0:S, :].rearrange("p s h -> p h s"), X, ALU.add))
                st.add(v.tensor_tensor(acc[:].rearrange(as_heads, h=H), acc[:].rearrange(as_heads, h=H),
                                       over_dims(prob[:, S, :], D), ALU.mult))
                v.wait_ge(released[b], u + 2)
                st.add(v.tensor_reduce(red[:], work[:].rearrange("p s f -> p f s"), X, ALU.add))
                st.wait()
                st.add(v.tensor_tensor(den[:], den[:], part[:], ALU.add))
                st.do(v.tensor_tensor(acc[:], acc[:], red[:], ALU.add))

            def softmax_sum(st, t):
                st.do(v.reciprocal(part[:], den[:]))
                st.do(v.tensor_scalar(part[:], part[:], kp["has_edges"][:, bass.ds(t, 1)], None, ALU.mult))
                return v.tensor_tensor(out[:].rearrange(as_heads, h=H), acc[:].rearrange(as_heads, h=H),
                                       over_dims(part[:], D), ALU.mult)

            def end_tile(st, t):
                if layer == "conv":
                    st.do(softmax_sum(st, t))
                    v.tensor_tensor(out[:], out[:], tile_of(kp["b"], t), ALU.add).then_inc(pre_gelu, 1)
                elif layer == "rel":
                    st.do(v.scalar_tensor_tensor(out[:], acc[:], 0.0, tile_of(kp["x"], t), ALU.max, ALU.add))
                    normal_stats(v, st, sems, small, out[:])
                elif layer == "gat1":
                    st.do(softmax_sum(st, t))
                    st.add(v.tensor_tensor(out[:], out[:], vec["L2_gnn_bias1"][:], ALU.add))
                    v.wait_ge(rows_ready, t + 1)
                    v.tensor_copy(cur[:], tile_of(kp["x"], t)).then_inc(new_x, 1)
                elif layer == "gat2":
                    st.do(softmax_sum(st, t))
                    st.do(v.tensor_tensor(out[:], out[:], vec["L2_gnn_bias2"][:], ALU.add))
                    st.do(v.scalar_tensor_tensor(out[:], tile_of(kp["a"], t), kp["inv_deg"][:, bass.ds(t, 1)],
                                                 out[:], ALU.mult, ALU.add))
                    st.do(v.tensor_tensor(out[:], out[:], tile_of(kp["x"], t), ALU.add))
                    normal_stats(v, st, sems, small, out[:])
                else:
                    st.add(v.tensor_copy(tile_of(kp["a"], t), acc[:]))
                    st.add(v.tensor_copy(tile_of(kp["den"], t), den[:]))
                    st.add(v.tensor_copy(tile_of(kp["top"], t), top[:]))
                    st.wait()

            def node_numbers(st, t):
                v.wait_ge(written, 16 + 16 * (1 + scans) * t)
                st.add(v.tensor_copy(node[:, 0:1], kp["info"][:, bass.ds(t, 1), 0]))
                st.add(v.tensor_copy(node[:, 1:2], kp["info"][:, bass.ds(t, 1), 3]))

            def finish_tile(st, t, place):
                if layer == "conv" and place == 1:
                    v.wait_ge(gelu_done, t + 1)
                    st.do(v.tensor_tensor(out[:], act_out[:], tile_of(kp["x"], t), ALU.add))
                    normal_stats(v, st, sems, small, out[:])
                elif layer == "conv" and place == 2:
                    st.do(normal_apply(v, st, sems, small, tmp[:], out[:], 2 * t + 1, vec["L0_gnn_gamma"][:],
                                       vec["L0_gnn_beta"][:]))
                    st.do(v.tensor_tensor(out[:], tmp[:], tile_of(kp["x"], t), ALU.add))
                    normal_stats(v, st, sems, small, out[:])
                    st.do(normal_apply(v, st, sems, small, tile_of(kp["x"], t), out[:], 2 * t + 2))
                elif (layer, place) in (("rel", 0), ("gat2", 1)):
                    node_numbers(st, t)
                    v.wait_ge(rows_ready, t + 1)
                    st.do(normal_apply(v, st, sems, small, cur[:], out[:], t + 1))
                    v.sem_inc(new_x, 1)
                elif layer == "gat1" and place == 1:
                    node_numbers(st, t)
                    v.wait_ge(made, 2 * t + 1)
                    st.do(v.scalar_tensor_tensor(out[:], ps[0][:, 0:F], kp["inv_deg"][:, bass.ds(t, 1)], out[:],
                                                 ALU.mult, ALU.add))
                    st.do(v.tensor_scalar(hid[:], out[:], 0.0, None, ALU.max))
                    v.sem_inc(new_x, 1)

            def tile(t, first):
                base = START + PRO + END + (t - 1) * TILE if not first else START
                hooks = 0 if first else HOOKS
                w = Visit(v, kp, t)
                st = Steps(v, steps, base + w.chunk(0, 0) * PER)
                st.add(v.memset(acc[:], 0.0))
                if H:
                    st.add(v.memset(den[:], 0.0))
                    st.add(v.memset(top[:], LOW))
                    st.add(v.tensor_copy(own[:] if layer == "conv" else own[:, 0:H],
                                         tile_of(kp["a"], t) if layer == "conv" else
                                         kp["er"][:, bass.ds(t, 1), 0:H].rearrange("p a h -> p (a h)")))
                st.wait()
                v.sem_inc(begun, 1)
                assert st.n == PRO, (layer, 1, st.n)
                for b in range(2):
                    n = st.n
                    logits(st, w, 0, b)
                    PER_NOW = st.n - n
                    if b == 1 and not first:
                        finish_tile(st, t - 1, 1)
                    n = st.n
                    weigh(st, w, 0, b)
                    PER_NOW += st.n - n
                    assert PER_NOW == PER, (layer, 0, PER_NOW)
                    if not first:
                        finish_tile(st, t - 1, 0 if b == 0 else 2)
                if not first:
                    assert st.n - PRO - 2 * PER == HOOKS, (layer, 3, st.n - PRO - 2 * PER)

                def chunk(w, a, b):
                    st = Steps(v, steps, base + PRO + hooks + w.chunk(a, b) * PER)
                    logits(st, w, a, b)
                    weigh(st, w, a, b)

                v.sem_inc(ended, 1)
                with v.If(w.pairs > 1):
                    with v.Fori(1, w.pairs) as a:
                        chunk(w, a, 0)
                        chunk(w, a, 1)
                        v.sem_inc(ended, 1)
                with v.If(w.tail > 0):
                    chunk(w, w.pairs, 0)
                    v.sem_inc(ended, 1)
                st = Steps(v, steps, base + PRO + hooks + w.chunks_end * PER)
                end_tile(st, t)
                v.sem_inc(ended, 1)
                assert st.n == END, (layer, 2, st.n)

            tile(0, True)
            with v.Fori(1, T) as t:
                tile(t, False)
            chunks = v.value_load(kp["sched"][0:1, CHUNKS, T:T + 1], min_val=1, max_val=CHUNKS_MAX)
            st = Steps(v, steps, START + T * TILE - HOOKS + chunks * PER)
            for place in range(3):
                finish_tile(st, T - 1, place)
            v.sem_inc(ended, 1)

        @block.scalar
        def _(act):
            act.sem_inc(rows_ready, 1)

            def exp(w, a, b):
                act.wait_ge(logits_ready, w.chunk(a, b) + 1)
                act.activation(prob[:], logit[:], ACT.Exp, scale=float(D) ** -0.5 if layer == "conv" else 1.0
                               ).then_inc(probs_ready, 1)

            def next_rows(t, source):
                act.wait_ge(written, 16 + 16 * (1 + scans) * t)
                act.activation(stage[:], source[:, 0:F + HN], ACT.Copy)
                act.activation(kp["er"][:, bass.ds(t, 1), 0:HN].rearrange("p a h -> p (a h)"),
                               source[:, F + HN:wide], ACT.Copy).then_inc(rows_ready, 1)

            def turn_new_x(t):
                act.wait_ge(turned, t + 1)
                act.activation(xt[:], ps_t, ACT.Copy).then_inc(xt_ready, 1)
                act.activation(tile_of(kp["x"], t), cur[:], ACT.Copy)
                act.wait_ge(made, t + 1)
                next_rows(t, ps[0])

            def finish_tile(t, place):
                if layer == "conv" and place == 0:
                    act.wait_ge(pre_gelu, t + 1)
                    act.activation(act_out[:], out[:], ACT.Gelu).then_inc(gelu_done, 1)
                elif layer == "conv":
                    root_of(act, sems, small, 2 * t + 1)
                    root_of(act, sems, small, 2 * t + 2)
                elif layer == "rel" and place == 0:
                    root_of(act, sems, small, t + 1)
                elif layer == "rel":
                    turn_new_x(t)
                elif layer == "gat1" and place == 0:
                    act.wait_ge(turned, 2 * t + 1)
                    act.activation(xt[:], ps_t, ACT.Copy).then_inc(xt_ready, 1)
                elif layer == "gat1":
                    act.wait_ge(turned, 2 * t + 2)
                    act.activation(ht[:], ps_h, ACT.Copy).then_inc(xt_ready, 1)
                    act.wait_ge(made, 2 * t + 2)
                    act.activation(tile_of(kp["a"], t), ps[1][:, 0:F], ACT.Copy)
                    next_rows(t, ps[2])
                elif layer == "gat2" and place == 0:
                    root_of(act, sems, small, t + 1)
                elif layer == "gat2":
                    turn_new_x(t)

            def first_pair(t):
                def run(w):
                    for b in range(2):
                        exp(w, 0, b)
                        finish_tile(t, b)
                return run

            if H:
                visit(act, kp, 0, exp)
                with act.Fori(1, T) as t:
                    visit(act, kp, t, exp, first_pair(t - 1))
                for place in range(2):
                    finish_tile(T - 1, place)
            else:
                with act.Fori(0, T) as t:
                    for place in range(2):
                        finish_tile(t, place)

        @block.tensor
        def _(pe):
            ident, ones = kp["ident"][:], kp["ones"][:, :]
            if nxt:
                pe.wait_ge(loaded, loads)
                pe.wait_ge(folded, 1)
                with pe.Fori(0, T) as t:
                    if layer == "gat1":
                        pe.wait_ge(new_x, 2 * t + 1)
                        transposed(pe, ps_t, cur, ident).then_inc(turned, 1)
                        pe.wait_ge(xt_ready, 2 * t + 1)
                        product(pe, ps[1][:, 0:F], xt, wt["wb1a"], bias["bb1"][:], ones, stop=False)
                        product(pe, ps[0][:, 0:F], xt, wt["wb0"], bias["bb0"][:], ones).then_inc(made, 1)
                        pe.wait_ge(new_x, 2 * t + 2)
                        transposed(pe, ps_h, hid, ident).then_inc(turned, 1)
                        pe.wait_ge(xt_ready, 2 * t + 2)
                        product(pe, ps[1][:, 0:F], ht, wt["wb1b"], start=False)
                        product(pe, ps[2][:, 0:wide], ht, wt["fc2"]).then_inc(made, 1)
                    else:
                        pe.wait_ge(new_x, t + 1)
                        transposed(pe, ps_t, cur, ident).then_inc(turned, 1)
                        pe.wait_ge(xt_ready, t + 1)
                        product(pe, ps[0][:, 0:wide], xt, wt[weights[0]]).then_inc(made, 1)
    finish(nc, all_sems)


def layer_norm(v, st, sems, small, out, src, gain=None, offset=None):
    normal_stats(v, st, sems, small, src)
    sems["roots_asked"] += 1
    return normal_apply(v, st, sems, small, out, src, sems["roots_before"] + sems["roots_asked"], gain, offset)




def relation_messages(nc, io, dr, kp):
    with ExitStack() as ctx:
        def sb(name, shape, dt=F32):
            return ctx.enter_context(nc.sbuf_tensor(name, shape, dt))
        names = ["r_loaded", "r_weights", "r_tile", "r_turned", "r_xt", "r_made", "r_actout", "r_dveout", "r_index",
                 "r_written0", "r_written1", "r_pace"]
        sems = {n[2:]: nc.alloc_semaphore(n) for n in names}
        bases = sb("r_bases", [P, BASES, 2, F])
        comp = sb("r_comp", [P, RELS * BASES])
        w = sb("r_w", [P, 2, RELS * F])
        stage = [sb(f"r_stage{k}", [P, RELS * F // 2]) for k in range(2)]
        tile, xt = sb("r_tile_sb", [P, F]), sb("r_xt_sb", [P, 2, P])
        node = [sb(f"r_node{k}", [P, 1], I32) for k in range(2)]
        spare = [sb(f"r_spare{k}", [1, 4], I32) for k in range(2)]
        ps_t = ctx.enter_context(nc.psum_tensor("r_pst", [P, 4, P], F32))[:, 0:2, :]
        ps = ctx.enter_context(nc.psum_tensor("r_ps", [P, 4, 512], F32))
        G = RELS * F // 512
        written = [sems["written0"], sems["written1"]]
        half_rows = dr["messages"].rearrange("(n k r) f -> (n k) (r f)", k=2, r=RELS // 2)
        block = ctx.enter_context(nc.Block())

        @block.sync
        def _(sp):
            for b in range(BASES):
                sp.dma_start(bases[:, b, :, :], halves(io["L1_gnn_bases"][b])).then_inc(sems["loaded"], 16)
            sp.dma_start(comp[:], on_all(io["L1_gnn_w_comp"].rearrange("r b -> (r b)"))).then_inc(sems["loaded"], 16)

        @block.vector
        def _(v):
            v.wait_ge(sems["loaded"], 16 * (BASES + 1))
            with v.Fori(0, RELS) as r:
                dst = w[:, :, bass.ds(r * F, F)]
                for b in range(BASES):
                    scale = comp[:, bass.ds(r * BASES + b, 1)]
                    if b == 0:
                        ins = v.tensor_scalar(dst, bases[:, 0, :, :], scale, None, ALU.mult)
                    else:
                        ins = v.scalar_tensor_tensor(dst, bases[:, b, :, :], scale, dst, ALU.mult, ALU.add)
                    ins.then_inc(sems["weights"], 1)
                    v.wait_ge(sems["weights"], r * BASES + b + 1)
            with v.Fori(0, T) as t:
                v.wait_ge(sems["turned"], t + 1)
                v.tensor_copy(tile[:], tile_of(kp["x"], t)).then_inc(sems["tile"], 1)
                v.wait_ge(sems["turned"], t + 2)
                v.tensor_copy(xt[:], ps_t).then_inc(sems["xt"], 1)
                for k in range(2):
                    v.wait_ge(written[k], 16 * t + 16)
                    v.tensor_scalar(node[k][:], kp["info"][:, bass.ds(t, 1), 0], 2.0, float(k), ALU.mult,
                                    ALU.add).then_inc(sems["index"], 1)
                    for g in range(k * G // 2 + 1, (k + 1) * G // 2, 2):
                        v.wait_ge(sems["made"], t * G + g + 1)
                        v.tensor_copy(stage[k][:, (g % (G // 2)) * 512:(g % (G // 2) + 1) * 512],
                                      ps[:, g % 4, :]).then_inc(sems["dveout"], 1)

        @block.scalar
        def _(act):
            with act.Fori(0, T) as t:
                for k in range(2):
                    act.wait_ge(written[k], 16 * t + 16)
                    for g in range(k * G // 2, (k + 1) * G // 2, 2):
                        act.wait_ge(sems["made"], t * G + g + 1)
                        act.activation(stage[k][:, (g % (G // 2)) * 512:(g % (G // 2) + 1) * 512], ps[:, g % 4, :],
                                       ACT.Copy).then_inc(sems["actout"], 1)

        @block.tensor
        def _(pe):
            pe.sem_inc(sems["turned"], 1)
            pe.sem_inc(sems["actout"], 2)
            pe.sem_inc(sems["dveout"], 2)
            pe.wait_ge(sems["weights"], RELS * BASES)
            with pe.Fori(0, T) as t:
                pe.wait_ge(sems["tile"], t + 1)
                transposed(pe, ps_t, tile, kp["ident"][:]).then_inc(sems["turned"], 1)
                pe.wait_ge(sems["xt"], t + 1)
                for g in range(G):
                    pe.wait_ge(sems["dveout" if g % 2 else "actout"], t * (G // 2) + g // 2 + 1)
                    product(pe, ps[:, g % 4, :], xt, w[:, :, g * 512:(g + 1) * 512]).then_inc(sems["made"], 1)

        @block.gpsimd
        def _(pool):
            for k in range(2):
                prime(pool, dr, spare[k], written[k])
            with pool.Fori(0, T) as t:
                for k in range(2):
                    for s, n in (("index", t * 2 + k + 1), ("actout", t * (G // 2) + (k + 1) * G // 4 + 2),
                                 ("dveout", t * (G // 2) + (k + 1) * G // 4 + 2)):
                        pool.wait_ge(sems[s], n)
                        pool.sem_inc(sems["pace"], 1)
                    pool.indirect_dma_start(out=half_rows, in_=stage[k][:], in_offset=None,
                                            out_offset=bass.IndirectOffsetOnAxis(ap=node[k][:, 0:1], axis=0)
                                            ).then_inc(written[k], 16)
            for k in range(2):
                pool.wait_ge(written[k], 16 * T + 16)
    finish(nc, list(sems.values()))


def state_scan(nc, io, dr, kp):
    NS, R = 16, 16
    with ExitStack() as ctx:
        def sb(name, shape, dt=F32):
            return ctx.enter_context(nc.sbuf_tensor("m_" + name, shape, dt))
        names = ["loaded", "steps", "rows", "turned", "xt", "xz", "neg", "exp", "xc", "dbc", "dbc_out", "spread_w",
                 "spread", "dt", "soft_a", "soft_b", "dt_ready", "decay", "z_exp", "y", "made", "yout", "stored", "alog"]
        sems = {n: nc.alloc_semaphore("m_" + n) for n in names}
        w_in, w_out, w_x = sb("win", [P, 2, 2 * F]), sb("wout", [P, 2, F]), sb("wx", [P, 2, R + 2 * NS])
        w_dt = sb("wdt", [R, F])
        cw, cb, db, dp = sb("cw", [P, 2, 4]), sb("cb", [P, 2]), sb("db", [P, 2]), sb("dp", [P, 2])
        a = sb("a", [P, 2, NS])
        xs, xst = sb("xs", [P, F]), sb("xst", [P, 2, P])
        seq = sb("seq", [P, 2, P + 3])
        cv, ex, xc, zz = sb("cv", [P, 2, P]), sb("ex", [P, 2, P]), sb("xc", [P, 2, P]), sb("zz", [P, 2, P])
        ez = sb("ez", [P, 2, P])
        dbc = sb("dbc", [R + 2 * NS, P])
        bc = sb("bc", [P, 2, NS, P])
        u, dt, dtx, e, w1, d1, ln, z0 = (sb(n, [P, 2, P]) for n in ("u", "dt", "dtx", "e", "w1", "d1", "ln", "z0"))
        da, db_x, hs = sb("da", [P, 2, NS, P]), sb("dbx", [P, 2, NS, P]), sb("hs", [P, 2, NS, P])
        last = sb("last", [P, 2, NS])
        y, yr = sb("y", [P, 2, P]), sb("yr", [P, F])
        bank = [ctx.enter_context(nc.psum_tensor(f"m_ps{k}", [P, 512], F32)) for k in range(5)]
        ps_t = bank[0][:, 0:F].rearrange("p (k c) -> p k c", k=2)
        ps_xz = bank[1][:].rearrange("p (k c) -> p k c", k=4)
        ps_d = bank[2][0:R + 2 * NS, 0:P]
        ps_dt = bank[3][:, 0:F].rearrange("p (k c) -> p k c", k=2)
        ps_o = bank[4][:, 0:F]
        block = ctx.enter_context(nc.Block())
        LOADS = 9

        def per_channel(vec):
            return vec.rearrange("(k p) -> p k", p=P)

        @block.sync
        def _(sp):
            with nc.allow_non_contiguous_dma(reason="one word per channel"):
                for dst, src in ((w_in, halves(io["in_proj"])), (w_out, halves(io["out_proj"])),
                                 (w_x, halves(io["x_proj"])), (w_dt, io["dt_proj"]),
                                 (cw, halves(io["L3_gnn_conv_w"])), (cb, per_channel(io["L3_gnn_conv_b"])),
                                 (db, per_channel(io["L3_gnn_dt_proj_b"])), (dp, per_channel(io["L3_gnn_D_param"])),
                                 (a, halves(io["L3_gnn_A_log"]))):
                    sp.dma_start(dst[:], src).then_inc(sems["loaded"], 16)
            with sp.Fori(0, T) as t:
                sp.wait_ge(sems["turned"], t + 1)
                sp.dma_start(xs[:], dr["scan_x"][bass.ds(t * P, P), :]).then_inc(sems["rows"], 16)
                sp.wait_ge(sems["dbc_out"], t + 1)
                sp.dma_start(dr["bc"], dbc[R:R + 2 * NS, :]).then_inc(sems["spread_w"], 16)
                sp.wait_ge(sems["spread_w"], 16 * t + 16)
                sp.dma_start(bc[:].rearrange("p k n c -> p (k n c)"), on_all(dr["bc"].rearrange("a c -> (a c)"))
                             ).then_inc(sems["spread"], 16)
                sp.wait_ge(sems["yout"], t + 1)
                sp.dma_start(dr["scan_y"][bass.ds(t * P, P), :], yr[:]).then_inc(sems["stored"], 16)
            sp.wait_ge(sems["stored"], 16 * T + 16)

        @block.tensor
        def _(pe):
            pe.sem_inc(sems["turned"], 1)
            pe.wait_ge(sems["loaded"], 16 * LOADS)
            with pe.Fori(0, T) as t:
                pe.wait_ge(sems["rows"], 16 * t + 16)
                transposed(pe, ps_t, xs, kp["ident"][:]).then_inc(sems["turned"], 1)
                pe.wait_ge(sems["xt"], t + 1)
                for m in range(4):
                    for k in range(2):
                        ins = pe.matmul(ps_xz[:, m, :], w_in[:, k, m * P:(m + 1) * P], xst[:, k, :], start=k == 0,
                                        stop=k == 1)
                ins.then_inc(sems["xz"], 1)
                pe.wait_ge(sems["xc"], t + 1)
                for k in range(2):
                    ins = pe.matmul(ps_d, w_x[:, k, :], xc[:, k, :], start=k == 0, stop=k == 1)
                ins.then_inc(sems["dbc"], 1)
                pe.wait_ge(sems["dbc_out"], t + 1)
                for k in range(2):
                    ins = pe.matmul(ps_dt[:, k, :], w_dt[:, k * P:(k + 1) * P], dbc[0:R, :], start=True, stop=True)
                ins.then_inc(sems["dt"], 1)
                pe.wait_ge(sems["y"], t + 1)
                for k in range(2):
                    ins = pe.matmul(ps_o, y[:, k, :], w_out[:, k, :], start=k == 0, stop=k == 1)
                ins.then_inc(sems["made"], 1)

        @block.scalar
        def _(act):
            act.wait_ge(sems["loaded"], 16 * LOADS)
            act.activation(a[:], a[:], ACT.Exp).then_inc(sems["alog"], 1)
            with act.Fori(0, T) as t:
                act.wait_ge(sems["turned"], t + 2)
                act.activation(xst[:], ps_t, ACT.Copy).then_inc(sems["xt"], 1)
                act.wait_ge(sems["neg"], t + 1)
                act.activation(ex[:], cv[:], ACT.Exp, scale=-1.0).then_inc(sems["exp"], 1)
                act.activation(ez[:], zz[:], ACT.Exp, scale=-1.0).then_inc(sems["z_exp"], 1)
                act.wait_ge(sems["soft_a"], 2 * t + 1)
                act.activation(e[:], d1[:], ACT.Exp, scale=-1.0).then_inc(sems["soft_b"], 1)
                act.wait_ge(sems["soft_a"], 2 * t + 2)
                act.activation(ln[:], w1[:], ACT.Ln).then_inc(sems["soft_b"], 1)
                act.wait_ge(sems["dt_ready"], t + 1)
                for k in range(2):
                    for n in range(NS):
                        ins = act.activation(da[:, k, n, :], dt[:, k, :], ACT.Exp, scale=a[:, k, n:n + 1])
                ins.then_inc(sems["decay"], 1)
                act.wait_ge(sems["made"], t + 1)
                act.wait_ge(sems["stored"], 16 * t + 16)
                act.activation(yr[:], ps_o, ACT.Copy).then_inc(sems["yout"], 1)

        @block.gpsimd
        def _(pool):
            pool.sem_inc(sems["stored"], 16)

        @block.vector
        def _(v):
            PER = 68
            st = Steps(v, sems["steps"])
            st.add(v.memset(seq[:], 0.0))
            st.add(v.memset(last[:], 0.0))
            v.wait_ge(sems["alog"], 1)
            st.add(v.tensor_scalar(a[:], a[:], -1.0, None, ALU.mult))
            st.wait()
            with v.Fori(0, T) as t:
                st = Steps(v, sems["steps"], 3 + t * PER)
                st.do(v.tensor_copy(seq[:, :, 0:3], seq[:, :, P:P + 3]))
                v.wait_ge(sems["xz"], t + 1)
                st.do(v.tensor_copy(seq[:, :, 3:P + 3], ps_xz[:, 0:2, :]))
                st.add(v.tensor_copy(zz[:], ps_xz[:, 2:4, :]))
                for k in range(2):
                    st.do(v.tensor_scalar(cv[:, k, :], seq[:, k, 0:P], cw[:, k, 0:1], cb[:, k:k + 1], ALU.mult, ALU.add))
                    for j in range(1, 4):
                        st.do(v.scalar_tensor_tensor(cv[:, k, :], seq[:, k, j:j + P], cw[:, k, j:j + 1], cv[:, k, :],
                                                     ALU.mult, ALU.add))
                v.sem_inc(sems["neg"], 1)
                v.wait_ge(sems["exp"], t + 1)
                st.do(v.tensor_scalar(ex[:], ex[:], 1.0, None, ALU.add))
                st.do(v.reciprocal(ex[:], ex[:]))
                v.tensor_tensor(xc[:], cv[:], ex[:], ALU.mult).then_inc(sems["xc"], 1)
                v.wait_ge(sems["xc"], t + 1)
                v.wait_ge(sems["z_exp"], t + 1)
                st.do(v.tensor_scalar(ez[:], ez[:], 1.0, None, ALU.add))
                st.do(v.reciprocal(ez[:], ez[:]))
                st.add(v.tensor_tensor(zz[:], zz[:], ez[:], ALU.mult))
                v.wait_ge(sems["dbc"], t + 1)
                v.tensor_copy(dbc[:], ps_d).then_inc(sems["dbc_out"], 1)
                v.wait_ge(sems["dt"], t + 1)
                for k in range(2):
                    st.do(v.tensor_scalar(u[:, k, :], ps_dt[:, k, :], db[:, k:k + 1], None, ALU.add))
                st.do(v.scalar_tensor_tensor(d1[:], u[:], -1.0, u[:], ALU.mult, ALU.max))
                v.sem_inc(sems["soft_a"], 1)
                v.wait_ge(sems["soft_b"], 2 * t + 1)
                v.tensor_scalar(w1[:], e[:], 1.0, None, ALU.add).then_inc(sems["soft_a"], 1)
                v.wait_ge(sems["soft_a"], 2 * t + 2)
                st.do(v.tensor_scalar(d1[:], w1[:], -1.0, None, ALU.add))
                st.do(v.tensor_scalar(z0[:], d1[:], 0.0, None, ALU.is_equal))
                st.do(v.tensor_tensor(d1[:], d1[:], z0[:], ALU.add))
                st.do(v.reciprocal(d1[:], d1[:]))
                v.wait_ge(sems["soft_b"], 2 * t + 2)
                st.do(v.tensor_tensor(d1[:], d1[:], ln[:], ALU.mult))
                st.do(v.tensor_tensor(d1[:], d1[:], z0[:], ALU.add))
                st.do(v.tensor_tensor(d1[:], d1[:], e[:], ALU.mult))
                v.scalar_tensor_tensor(dt[:], u[:], 0.0, d1[:], ALU.max, ALU.add).then_inc(sems["dt_ready"], 1)
                v.wait_ge(sems["dt_ready"], t + 1)
                st.do(v.tensor_tensor(dtx[:], dt[:], xc[:], ALU.mult))
                v.wait_ge(sems["spread"], 16 * t + 16)
                for k in range(2):
                    st.add(v.tensor_tensor(db_x[:, k, :, :], over_slots(dtx[:, k, :], NS), bc[:, 0, :, :], ALU.mult))
                st.wait()
                v.wait_ge(sems["decay"], t + 1)
                for k in range(2):
                    for n in range(NS):
                        st.add(v.tensor_tensor_scan(hs[:, k, n, :], da[:, k, n, :], db_x[:, k, n, :],
                                                    last[:, k, n:n + 1], ALU.mult, ALU.add))
                st.wait()
                st.add(v.tensor_copy(last[:], hs[:, :, :, P - 1]))
                for k in range(2):
                    st.do(v.tensor_tensor(db_x[:, k, :, :], hs[:, k, :, :], bc[:, 1, :, :], ALU.mult))
                    st.do(v.tensor_reduce(y[:, k, :], db_x[:, k, :, :].rearrange("p n c -> p c n"), X, ALU.add))
                    st.do(v.scalar_tensor_tensor(y[:, k, :], xc[:, k, :], dp[:, k:k + 1], y[:, k, :], ALU.mult,
                                                 ALU.add))
                v.tensor_tensor(y[:], y[:], zz[:], ALU.mult).then_inc(sems["y"], 1)
                v.wait_ge(sems["y"], t + 1)
                assert st.n == PER, st.n
    finish(nc, list(sems.values()))


def join(nc, io, dr, kp, result):
    with ExitStack() as ctx:
        def sb(name, shape, dt=F32):
            return ctx.enter_context(nc.sbuf_tensor("j_" + name, shape, dt))
        names = ["loaded", "steps", "gathered", "gmax_in", "gmax_turned", "gmax_row", "gmax_spread", "top_ready",
                 "top_exp", "elu_in", "elu_exp", "stats", "variance", "root", "turn", "turned", "copied", "made", "gate_in",
                 "gate_exp", "out_ready", "written", "pace"]
        sems = {n: nc.alloc_semaphore("j_" + n) for n in names}
        vectors = ["gat_b", "ln_local_g", "ln_local_b", "ln_global_g", "ln_global_b", "ln2_g", "ln2_b"]
        vec = {n: sb("v_" + n, [P, F]) for n in vectors}
        wl, wg = sb("wl", [P, 2, F]), sb("wg", [P, 2, F])
        w1, w2 = sb("w1", [P, 2, 2 * F]), sb("w2", [P, 4, F])
        b1, b2 = sb("b1", [1, 2 * F]), sb("b2", [1, F])
        fac = sb("fac", [P, T, 4])
        gm, grow, gall = sb("gm", [P, 1]), sb("grow", [1, 1]), sb("gall", [P, 1])
        small = sb("small", [P, 12])
        u, ev, hl, ha, s, g = (sb(n, [P, F]) for n in ("u", "ev", "hl", "ha", "s", "g"))
        hlt, hat, ht, ft = sb("hlt", [P, 2, P]), sb("hat", [P, 2, P]), sb("ht", [P, 2, P]), sb("ft", [P, 4, P])
        h, f, o = sb("h", [P, F]), sb("f", [P, 2 * F]), sb("o", [P, F])
        node, spare = sb("node", [P, 1], I32), sb("spare", [1, 4], I32)
        bank = [ctx.enter_context(nc.psum_tensor(f"j_ps{k}", [P, 4, P], F32)) for k in range(6)]
        block = ctx.enter_context(nc.Block())
        LOADS = len(vectors) + 6

        @block.sync
        def _(sp):
            for n in vectors:
                sp.dma_start(vec[n][:], on_all(io["L3_gnn_" + n])).then_inc(sems["loaded"], 16)
            for dst, src in ((wl, halves(io["wl"])), (wg, halves(io["wg"])), (w1, halves(io["ff1"])),
                             (w2, halves(io["ff2"])), (b1, rows_of(io["L3_gnn_ff1_b"])),
                             (b2, rows_of(io["L3_gnn_ff2_b"]))):
                sp.dma_start(dst[:], src).then_inc(sems["loaded"], 16)

        @block.gpsimd
        def _(pool):
            for t in range(T):
                pool.indirect_dma_start(out=kp["b"][:, t, :], out_offset=None, in_=dr["scan_y"],
                                        in_offset=bass.IndirectOffsetOnAxis(ap=kp["info"][:, t, 3:4], axis=0),
                                        bounds_check=NP - 1, oob_is_err=False).then_inc(sems["gathered"], 16)
            prime(pool, dr, spare, sems["written"])
            with pool.Fori(0, T) as t:
                pool.wait_ge(sems["out_ready"], t + 1)
                pool.sem_inc(sems["pace"], 1)
                pool.indirect_dma_start(out=result, in_=o[:], in_offset=None,
                                        out_offset=bass.IndirectOffsetOnAxis(ap=node[:, 0:1], axis=0),
                                        bounds_check=N - 1, oob_is_err=False).then_inc(sems["written"], 16)
            pool.wait_ge(sems["written"], 16 * T + 16)

        @block.tensor
        def _(pe):
            ident, ones = kp["ident"][:], kp["ones"][:, :]
            pe.wait_ge(sems["loaded"], 16 * LOADS)
            pe.wait_ge(sems["gmax_in"], 1)
            pe.transpose(bank[0][0:1, 0, :], gm[:], ident).then_inc(sems["gmax_turned"], 1)
            pe.wait_ge(sems["gmax_row"], 1)
            pe.matmul(bank[1][:, 0, 0:1], ones, grow[:], start=True, stop=True).then_inc(sems["gmax_spread"], 1)
            with pe.Fori(0, T) as t:
                pe.wait_ge(sems["turn"], t * 4 + 1)
                transposed(pe, bank[0], hl, ident).then_inc(sems["turned"], 1)
                pe.wait_ge(sems["turn"], t * 4 + 2)
                transposed(pe, bank[1], ha, ident).then_inc(sems["turned"], 1)
                pe.wait_ge(sems["copied"], t * 4 + 2)
                ps = bank[2][:, 0:2, :].rearrange("p k c -> p (k c)")
                product(pe, ps, hlt, wl, stop=False)
                product(pe, ps, hat, wg, start=False).then_inc(sems["made"], 1)
                pe.wait_ge(sems["turn"], t * 4 + 3)
                transposed(pe, bank[0], h, ident).then_inc(sems["turned"], 1)
                pe.wait_ge(sems["copied"], t * 4 + 3)
                product(pe, bank[3][:].rearrange("p k c -> p (k c)"), ht, w1, b1[:], ones).then_inc(sems["made"], 1)
                pe.wait_ge(sems["turn"], t * 4 + 4)
                transposed(pe, bank[4], f, ident, 4).then_inc(sems["turned"], 1)
                pe.wait_ge(sems["copied"], t * 4 + 4)
                product(pe, bank[5][:, 0:2, :].rearrange("p k c -> p (k c)"), ft, w2, b2[:], ones
                        ).then_inc(sems["made"], 1)

        @block.scalar
        def _(act):
            act.wait_ge(sems["top_ready"], 1)
            act.activation(fac[:], fac[:], ACT.Exp).then_inc(sems["top_exp"], 1)
            with act.Fori(0, T) as t:
                act.wait_ge(sems["elu_in"], t + 1)
                act.activation(ev[:], ev[:], ACT.Exp).then_inc(sems["elu_exp"], 1)
                root_of(act, sems, small, t * 4 + 1)
                root_of(act, sems, small, t * 4 + 2)
                for i, (dst, src) in enumerate(((hlt, bank[0][:, 0:2, :]), (hat, bank[1][:, 0:2, :]),
                                                (ht, bank[0][:, 0:2, :]), (ft, bank[4][:]))):
                    act.wait_ge(sems["turned"], t * 4 + i + 1)
                    act.activation(dst[:], src, ACT.Copy).then_inc(sems["copied"], 1)
                    if i == 1:
                        act.wait_ge(sems["gate_in"], t + 1)
                        act.activation(g[:], g[:], ACT.Exp, scale=-1.0).then_inc(sems["gate_exp"], 1)
                root_of(act, sems, small, t * 4 + 3)
                root_of(act, sems, small, t * 4 + 4)

        @block.vector
        def _(v):
            BEFORE, PER = 4, 33
            st = Steps(v, sems["steps"])
            v.tensor_reduce(gm[:], kp["top"][:].rearrange("p t h -> p (t h)"), X, ALU.max).then_inc(sems["gmax_in"], 1)
            v.wait_ge(sems["gmax_turned"], 1)
            v.tensor_reduce(grow[:], bank[0][0:1, 0, :], X, ALU.max).then_inc(sems["gmax_row"], 1)
            v.wait_ge(sems["gmax_spread"], 1)
            st.do(v.tensor_copy(gall[:], bank[1][:, 0, 0:1]))
            v.tensor_scalar(fac[:], kp["top"][:], gall[:], None, ALU.subtract).then_inc(sems["top_ready"], 1)
            v.wait_ge(sems["top_exp"], 1)
            st.do(v.tensor_tensor(kp["den"][:], kp["den"][:], fac[:], ALU.mult))
            st.do(v.tensor_scalar(kp["den"][:], kp["den"][:], 1e-16, None, ALU.add))
            st.do(v.reciprocal(kp["den"][:], kp["den"][:]))
            v.tensor_tensor(fac[:], fac[:], kp["den"][:], ALU.mult).then_inc(sems["top_ready"], 1)
            v.wait_ge(sems["top_ready"], 2)
            v.wait_ge(sems["loaded"], 16 * LOADS)
            v.wait_ge(sems["gathered"], 16 * T)
            with v.Fori(0, T) as t:
                st = Steps(v, sems["steps"], BEFORE + t * PER)
                sems["roots_asked"], sems["roots_before"] = 0, t * 4
                x_t = tile_of(kp["x"], t)
                st.do(v.tensor_tensor(u[:].rearrange("p (h d) -> p h d", h=4),
                                      kp["a"][:, bass.ds(t, 1), :].rearrange("p a (h d) -> p (a h) d", h=4),
                                      over_dims(fac[:, bass.ds(t, 1), :].rearrange("p a h -> p (a h)"), F // 4),
                                      ALU.mult))
                st.do(v.tensor_tensor(u[:], u[:], x_t, ALU.add))
                st.do(v.tensor_tensor(u[:], u[:], vec["gat_b"][:], ALU.add))
                v.tensor_scalar(ev[:], u[:], 0.0, None, ALU.min).then_inc(sems["elu_in"], 1)
                v.wait_ge(sems["elu_exp"], t + 1)
                st.do(v.scalar_tensor_tensor(u[:], u[:], 0.0, ev[:], ALU.max, ALU.add))
                st.do(v.tensor_scalar(u[:], u[:], -1.0, None, ALU.add))
                layer_norm(v, st, sems, small, hl[:], u[:], vec["ln_local_g"][:], vec["ln_local_b"][:]
                           ).then_inc(sems["turn"], 1)
                st.do(v.tensor_tensor(s[:], x_t, tile_of(kp["b"], t), ALU.add))
                layer_norm(v, st, sems, small, ha[:], s[:], vec["ln_global_g"][:], vec["ln_global_b"][:]
                           ).then_inc(sems["turn"], 1)
                v.wait_ge(sems["made"], t * 3 + 1)
                v.tensor_copy(g[:], bank[2][:, 0:2, :].rearrange("p k c -> p (k c)")).then_inc(sems["gate_in"], 1)
                v.wait_ge(sems["gate_exp"], t + 1)
                st.do(v.tensor_scalar(g[:], g[:], 1.0, None, ALU.add))
                st.do(v.reciprocal(g[:], g[:]))
                v.wait_ge(sems["turn"], t * 4 + 2)
                st.do(v.tensor_tensor(u[:], hl[:], ha[:], ALU.subtract))
                st.do(v.tensor_tensor(u[:], u[:], g[:], ALU.mult))
                v.tensor_tensor(h[:], u[:], ha[:], ALU.add).then_inc(sems["turn"], 1)
                v.wait_ge(sems["made"], t * 3 + 2)
                v.tensor_scalar(f[:], bank[3][:].rearrange("p k c -> p (k c)"), 0.0, None, ALU.max
                                ).then_inc(sems["turn"], 1)
                v.wait_ge(sems["made"], t * 3 + 3)
                st.do(v.tensor_tensor(u[:], h[:], bank[5][:, 0:2, :].rearrange("p k c -> p (k c)"), ALU.add))
                st.do(layer_norm(v, st, sems, small, s[:], u[:], vec["ln2_g"][:], vec["ln2_b"][:]))
                st.do(v.tensor_tensor(s[:], s[:], x_t, ALU.add))
                v.wait_ge(sems["written"], 16 * t + 16)
                st.add(v.tensor_copy(node[:], kp["info"][:, bass.ds(t, 1), 0]))
                st.do(layer_norm(v, st, sems, small, o[:], s[:]))
                v.sem_inc(sems["out_ready"], 1)
                assert st.n == PER, st.n
    finish(nc, [sems[n] for n in names])


def network(nc, io, result):
    def scratch(name, shape, dt=F32):
        return nc.dram_tensor("scratch_" + name, shape, dt).ap()
    dr = {
        "indeg": scratch("indeg", (NP,)), "outdeg": scratch("outdeg", (NP,)), "starts": scratch("starts", (NP,)),
        "keys": scratch("keys", (NP,)), "info": scratch("info", (NP, 4), I32),
        "runs": scratch("runs", (E, 2 * RUN), I32), "slots": scratch("slots", (CHUNKS_MAX + 4 * T, P, META)),
        "kv": scratch("kv", (NP, 2 * F)), "messages": scratch("messages", (NP * RELS, F)),
        "gat1": scratch("gat1", (NP, F + 8)), "gat2": scratch("gat2", (NP, F + 1)),
        "gat3": scratch("gat3", (NP, F + 4)), "scan_x": scratch("scan_x", (NP, F)),
        "scan_y": scratch("scan_y", (NP, F)), "bc": scratch("bc", (32, P)),
    }
    count_edges(nc, io, dr)
    order_nodes(nc, io, dr)
    with ExitStack() as ctx:
        def sb(name, shape, dt=F32):
            return ctx.enter_context(nc.sbuf_tensor("k_" + name, shape, dt))
        kp = {
            "info": sb("info", [P, T, 4], I32), "x": sb("x", [P, T, F]), "a": sb("a", [P, T, F]),
            "b": sb("b", [P, T, F]), "er": sb("er", [P, T, 8]), "den": sb("den", [P, T, 4]),
            "top": sb("top", [P, T, 4]), "deg": sb("deg", [P, T]), "has_edges": sb("has", [P, T]),
            "inv_deg": sb("inv", [P, T]), "sched": sb("sched", [1, 5, 32], I32), "ident": sb("ident", [P, P]),
            "ones": sb("ones", [1, P]), "slot_no": sb("slotno", [P, S]),
            "counts": COUNTS,
        }
        fetch_nodes(nc, io, dr, kp)
        build_slots(nc, dr, kp)
        project_nodes(nc, io, dr, kp)
        for name in ("conv", "messages", "rel", "gat1", "gat2", "gat3", "scan", "join"):
            if name == "messages":
                relation_messages(nc, io, dr, kp)
            elif name == "scan":
                state_scan(nc, io, dr, kp)
            elif name == "join":
                join(nc, io, dr, kp, result)
            else:
                edge_layer(nc, io, dr, kp, name)


COUNTS = {"conv": (13, 4, 3, 12, 0), "rel": (7, 1, 3, 4, 8), "gat1": (13, 4, 4, 4, 8),
          "gat2": (13, 4, 8, 4, 8), "gat3": (13, 4, 3, 0, 0)}

DIRECT = ["x", "src", "dst", "edge_type_32", "edge_weight1", "node_vec",
          "L0_gnn_Wq", "L0_gnn_bq", "L0_gnn_Wk", "L0_gnn_bk", "L0_gnn_Wv", "L0_gnn_bv", "L0_gnn_Wskip", "L0_gnn_bskip",
          "L0_gnn_gamma", "L0_gnn_beta", "L1_gnn_bases", "L1_gnn_w_comp", "L2_gnn_attn_l1", "L2_gnn_attn_r1",
          "L2_gnn_bias1", "L2_gnn_attn_l2", "L2_gnn_attn_r2", "L2_gnn_bias2", "L2_gnn_bb0", "L2_gnn_bb1",
          "L3_gnn_gat_a_src", "L3_gnn_gat_a_tgt", "L3_gnn_gat_b", "L3_gnn_ln_local_g", "L3_gnn_ln_local_b",
          "L3_gnn_ln_global_g", "L3_gnn_ln_global_b", "L3_gnn_ln2_g", "L3_gnn_ln2_b", "L3_gnn_conv_w",
          "L3_gnn_conv_b", "L3_gnn_dt_proj_b", "L3_gnn_A_log", "L3_gnn_D_param", "L3_gnn_ff1_b", "L3_gnn_ff2_b"]
TURNED = {"fc1": "L2_gnn_fc1_w", "fc2": "L2_gnn_fc2_w", "wb0": "L2_gnn_wb0", "gat": "L3_gnn_gat_w",
          "in_proj": "L3_gnn_in_proj_w", "x_proj": "L3_gnn_x_proj_w", "dt_proj": "L3_gnn_dt_proj_w",
          "out_proj": "L3_gnn_out_proj_w", "wl": "L3_gnn_wl", "wg": "L3_gnn_wg", "ff1": "L3_gnn_ff1_w",
          "ff2": "L3_gnn_ff2_w"}


def kernel(**inputs):
    import numpy as np
    import concourse.bacc as bacc
    from concourse.bass_utils import run_bass_kernel_spmd

    nc = bacc.Bacc("TRN2", target_bir_lowering=False, num_devices=1)
    arrays = {n: np.ascontiguousarray(inputs[n]) for n in DIRECT}
    arrays.update({n: np.ascontiguousarray(np.asarray(inputs[src]).T) for n, src in TURNED.items()})
    both = np.asarray(inputs["L2_gnn_wb1"]).T
    arrays["wb1a"], arrays["wb1b"] = np.ascontiguousarray(both[:F]), np.ascontiguousarray(both[F:])
    io = {n: nc.dram_tensor("in_" + n, a.shape, mybir.dt.from_np(a.dtype), kind="ExternalInput").ap()
          for n, a in arrays.items()}
    result = nc.dram_tensor("out_x", (N, F), F32, kind="ExternalOutput").ap()
    network(nc, io, result)
    r = run_bass_kernel_spmd(nc, [{"in_" + n: a for n, a in arrays.items()}], core_ids=[0])
    return r.results[0]["out_x"]
```

```python
from contextlib import ExitStack

import concourse.bass as bass
from concourse import mybir

F32 = mybir.dt.float32
I32 = mybir.dt.int32
BF16 = mybir.dt.bfloat16
ALU = mybir.AluOpType
ACT = mybir.ActivationFunctionType
X = mybir.AxisListType.X

P = 128
N = 3125
E = 103125
F = 256
T = (N + P - 1) // P
NP = T * P
RELS = 32
BASES = 8
EP = 125
EC = E // EP
HIST_HI, HIST_LO = 49, 64
HB = 32
EC_PAD = 832
S = 8
RUN = 16
MB = 4
NB = S // MB
META = 4 * S
CHUNKS_MAX = 2 * ((E + E // P + P) // RUN + 2 * T + 2)
FAR = 1.0e6
LOW = -1.0e30
EPS = 1e-5
assert E == EP * EC and HIST_HI * HIST_LO >= N and EC_PAD % (2 * HB) == 0


class Steps:

    def __init__(self, eng, sem, base=0):
        self.eng, self.sem, self.base, self.n = eng, sem, base, 0

    def add(self, ins):
        ins.then_inc(self.sem, 1)
        self.n += 1

    def wait(self):
        self.eng.wait_ge(self.sem, self.base + self.n)

    def do(self, ins):
        self.add(ins)
        self.wait()


def over_slots(ap, n):
    return ap.unsqueeze(1).to_broadcast([ap.shape[0], n, ap.shape[1]])


def over_dims(ap, n):
    return ap.unsqueeze(len(ap.shape)).to_broadcast(list(ap.shape) + [n])


def rows_of(vec):
    return vec.rearrange("(a f) -> a f", a=1)


def on_all(vec, n=P):
    return rows_of(vec).to_broadcast([n, vec.shape[0]])


def prime(pool, dr, spare, sem):
    pool.dma_start(spare[:], dr["info"][0:1, :]).then_inc(sem, 16)


def finish(nc, sems):
    nc.clear_and_free_semaphores(sems)
    nc.all_engine_barrier()


def count_edges(nc, io, dr):
    with ExitStack() as ctx:
        def sb(name, shape, dt=F32):
            return ctx.enter_context(nc.sbuf_tensor(name, shape, dt))
        names = ["e_pads", "e_loaded", "e_iota", "e_steps", "e_casts", "e_hot0", "e_hot1", "e_summed0", "e_summed1",
                 "e_zeroed", "e_hist", "e_counts", "e_packed", "e_runs", "e_actruns", "e_stored"]
        sems = {n[2:]: nc.alloc_semaphore(n) for n in names}
        hot, summed = [sems["hot0"], sems["hot1"]], [sems["summed0"], sems["summed1"]]
        W = EC + RUN
        dst = sb("e_dst", [EP, EC_PAD], I32)
        src = sb("e_src", [EP, W], I32)
        rel = sb("e_rel", [EP, W], I32)
        nrm = sb("e_nrm", [EP, W])
        packed = sb("e_pack", [EP, W], I32)
        part_i = sb("e_parti", [EP, EC_PAD], I32)
        parts = {k: sb("e_part" + k, [EP, EC_PAD], BF16) for k in ("dh", "dl", "sh", "sl")}
        iota_i = sb("e_ioi", [EP, HIST_LO], I32)
        iota = sb("e_io", [EP, HIST_LO], BF16)
        ones_at = {k: [sb(f"e_hot{k}{b}", [EP, HB, HIST_HI if k[1] == "h" else HIST_LO], BF16) for b in range(2)]
                   for k in parts}
        runs = sb("e_runs_sb", [EP, EC, 2 * RUN], I32)
        zero = sb("e_zero", [EP, HIST_LO], BF16)
        counts = sb("e_counts_sb", [HIST_HI, 2, HIST_LO])
        zrow = sb("e_zrow", [1, 64])
        ps = ctx.enter_context(nc.psum_tensor("e_ps", [HIST_HI, 2, 512], F32))
        block = ctx.enter_context(nc.Block())

        @block.sync
        def _(sp):
            sp.wait_ge(sems["pads"], 3)
            sp.dma_start(dst[:, 0:EC], io["dst"].rearrange("(p c) -> p c", p=EP)).then_inc(sems["loaded"], 16)
            for tile, name in ((src, "src"), (rel, "edge_type_32"), (nrm, "edge_weight1")):
                flat = io[name] if name != "edge_weight1" else io[name].rearrange("e a -> (e a)")
                rows = flat.rearrange("(p c) -> p c", p=EP)
                sp.dma_start(tile[:, 0:EC], rows).then_inc(sems["loaded"], 16)
                sp.dma_start(tile[0:EP - 1, EC:W], rows[1:EP, 0:RUN]).then_inc(sems["loaded"], 16)
            sp.wait_ge(sems["counts"], 2)
            for k, name in enumerate(("indeg", "outdeg")):
                sp.dma_start(dr[name][0:HIST_HI * HIST_LO].rearrange("(h l) -> h l", h=HIST_HI),
                             counts[:, k, :]).then_inc(sems["stored"], 16)
                sp.dma_start(rows_of(dr[name][HIST_HI * HIST_LO:NP]), zrow[:, :]).then_inc(sems["stored"], 16)
            sp.wait_ge(sems["runs"], RUN)
            sp.wait_ge(sems["actruns"], RUN)
            sp.dma_start(dr["runs"].rearrange("(p c) w -> p c w", p=EP), runs[:]).then_inc(sems["stored"], 16)
            sp.wait_ge(sems["stored"], 16 * 5)

        @block.gpsimd
        def _(pool):
            nc.gpsimd.memset(src[:, EC:W], 0).then_inc(sems["pads"], 1)
            nc.gpsimd.memset(rel[:, EC:W], 0).then_inc(sems["pads"], 1)
            nc.gpsimd.memset(nrm[:, EC:W], 0.0).then_inc(sems["pads"], 1)
            nc.gpsimd.iota(iota_i[:], [[1, HIST_LO]], base=0, channel_multiplier=0).then_inc(sems["iota"], 1)

        @block.vector
        def _(v):
            st = Steps(v, sems["steps"])
            st.add(nc.vector.memset(zero[:], 0.0))
            st.add(nc.vector.memset(zrow[:], 0.0))
            for k in parts:
                st.add(nc.vector.memset(parts[k][:, EC:EC_PAD], 16384.0))
            v.wait_ge(sems["iota"], 1)
            st.do(nc.vector.tensor_copy(iota[:], iota_i[:]))
            v.wait_ge(sems["loaded"], 16 * 7)
            for k, tile in (("d", dst), ("s", src)):
                st.do(nc.vector.tensor_scalar(part_i[:, 0:EC], tile[:, 0:EC], 6, None, ALU.logical_shift_right))
                st.do(nc.vector.tensor_copy(parts[k + "h"][:, 0:EC], part_i[:, 0:EC]))
                st.do(nc.vector.tensor_scalar(part_i[:, 0:EC], tile[:, 0:EC], 63, None, ALU.bitwise_and))
                st.do(nc.vector.tensor_copy(parts[k + "l"][:, 0:EC], part_i[:, 0:EC]))
            nc.vector.scalar_tensor_tensor(packed[:], src[:], float(RELS), rel[:], ALU.mult,
                                           ALU.add).then_inc(sems["packed"], 1)
            with v.Fori(0, EC_PAD // HB // 2) as i:
                for b in range(2):
                    v.wait_ge(summed[b], i + 1)
                    for k in ("dh", "dl", "sh", "sl"):
                        w = HIST_HI if k[1] == "h" else HIST_LO
                        cols = parts[k][:, bass.ds((2 * i + b) * HB, HB)]
                        ins = nc.vector.tensor_tensor(ones_at[k][b][:], over_dims(cols, w),
                                                      over_slots(iota[:, 0:w], HB), ALU.is_equal)
                    ins.then_inc(hot[b], 1)
            v.wait_ge(sems["packed"], 1)
            for s in range(RUN):
                nc.vector.tensor_copy(runs[:, :, s], packed[:, s:s + EC]).then_inc(sems["runs"], 1)
            v.wait_ge(sems["hist"], 1)
            for k in range(2):
                nc.vector.tensor_copy(counts[:, k, :], ps[:, k, 0:HIST_LO]).then_inc(sems["counts"], 1)

        @block.scalar
        def _(act):
            act.wait_ge(sems["loaded"], 16 * 7)
            for s in range(RUN):
                nc.scalar.activation(runs[:, :, RUN + s].bitcast(F32), nrm[:, s:s + EC],
                                     ACT.Copy).then_inc(sems["actruns"], 1)

        @block.tensor
        def _(pe):
            pe.sem_inc(summed[0], 1)
            pe.sem_inc(summed[1], 1)
            pe.wait_ge(sems["steps"], 1)
            for k in range(2):
                nc.tensor.matmul(ps[:, k, 0:HIST_LO], zero[:, 0:HIST_HI], zero[:, :], start=True, stop=False)
            with pe.Fori(0, EC_PAD // HB // 2) as i:
                for b in range(2):
                    pe.wait_ge(hot[b], i + 1)
                    for c in range(HB):
                        for k, (h, l) in enumerate((("dh", "dl"), ("sh", "sl"))):
                            ins = nc.tensor.matmul(ps[:, k, 0:HIST_LO], ones_at[h][b][:, c, :], ones_at[l][b][:, c, :],
                                                   start=False, stop=False, skip_group_check=True)
                    ins.then_inc(summed[b], 1)
            for k in range(2):
                ins = nc.tensor.matmul(ps[:, k, 0:HIST_LO], zero[:, 0:HIST_HI], zero[:, :], start=False, stop=True)
            ins.then_inc(sems["hist"], 1)
    finish(nc, list(sems.values()))


def rank(v, st, out, keys_all, keys_own, before, upto_own, tri, junk, cnt):
    for t in range(T):
        own = keys_own[:, t:t + 1]
        lo, hi = t * P, (t + 1) * P
        if t:
            st.add(v.tensor_scalar(junk[:, 0:lo], keys_all[:, 0:lo], own, 0.0, upto_own, ALU.add,
                                         accum_out=cnt[:, 0:1]))
        else:
            st.add(v.memset(cnt[:, 0:1], 0.0))
        if t < T - 1:
            st.add(v.tensor_scalar(junk[:, hi:NP], keys_all[:, hi:NP], own, 0.0, before, ALU.add,
                                         accum_out=cnt[:, 1:2]))
        else:
            st.add(v.memset(cnt[:, 1:2], 0.0))
        st.add(v.tensor_scalar(junk[:, lo:hi], keys_all[:, lo:hi], own, 0.0, before, ALU.add,
                                     accum_out=cnt[:, 2:3]))
        st.wait()
        st.do(v.scalar_tensor_tensor(junk[:, lo:hi], keys_all[:, lo:hi], own, tri, ALU.is_equal, ALU.mult,
                                           accum_out=cnt[:, 3:4]))
        st.do(v.tensor_reduce(out[:, t:t + 1], cnt[:, 0:4], X, ALU.add))


def order_nodes(nc, io, dr):
    with ExitStack() as ctx:
        def sb(name, shape, dt=F32):
            return ctx.enter_context(nc.sbuf_tensor(name, shape, dt))
        names = ["n_pad", "n_loaded", "n_iota", "n_steps", "n_starts", "n_stored", "n_reloaded", "n_keys",
                 "n_info", "n_scattered"]
        sems = {n[2:]: nc.alloc_semaphore(n) for n in names}
        deg_all = sb("n_degall", [P, NP])
        key_all = sb("n_keyall", [P, NP])
        junk = sb("n_junk", [P, NP], BF16)
        row = sb("n_row", [1, NP])
        cum = sb("n_cum", [1, NP])
        zero = sb("n_zero", [1, NP])
        deg, start, key, nv = (sb("n_" + k, [P, T]) for k in ("deg", "start", "key", "nv"))
        node_i = sb("n_nodei", [P, T], I32)
        by_deg, by_key = sb("n_bydeg", [P, T]), sb("n_bykey", [P, T])
        place = sb("n_place", [P, T], I32)
        info = sb("n_infosb", [P, T, 4], I32)
        cnt = sb("n_cnt", [P, 4])
        lane_i, col_i = sb("n_lanei", [P, 1], I32), sb("n_coli", [P, P], I32)
        lane, col, tri = sb("n_lane", [P, 1]), sb("n_col", [P, P]), sb("n_tri", [P, P])
        block = ctx.enter_context(nc.Block())
        by_col = "(t p) -> p t"
        whole = (T - 1) * P

        @block.sync
        def _(sp):
            with nc.allow_non_contiguous_dma(reason="one word per node"):
                sp.dma_start(deg_all[:], on_all(dr["indeg"])).then_inc(sems["loaded"], 16)
                sp.dma_start(row[:], rows_of(dr["indeg"])).then_inc(sems["loaded"], 16)
                sp.dma_start(deg[:], dr["indeg"].rearrange(by_col, p=P)).then_inc(sems["loaded"], 16)
                sp.dma_start(key[:], dr["outdeg"].rearrange(by_col, p=P)).then_inc(sems["loaded"], 16)
                sp.wait_ge(sems["pad"], 1)
                sp.dma_start(nv[:, 0:T - 1], io["node_vec"][0:whole].rearrange(by_col, p=P)).then_inc(sems["loaded"], 16)
                sp.dma_start(nv[0:N - whole, T - 1:T],
                             io["node_vec"][whole:N].rearrange("(p a) -> p a", a=1)).then_inc(sems["loaded"], 16)
                sp.wait_ge(sems["starts"], 1)
                sp.dma_start(rows_of(dr["starts"]), cum[:]).then_inc(sems["stored"], 16)
                sp.wait_ge(sems["keys"], 1)
                sp.dma_start(dr["keys"].rearrange(by_col, p=P), key[:]).then_inc(sems["stored"], 16)
                sp.wait_ge(sems["stored"], 32)
                sp.dma_start(start[:], dr["starts"].rearrange(by_col, p=P)).then_inc(sems["reloaded"], 16)
                sp.dma_start(key_all[:], on_all(dr["keys"])).then_inc(sems["reloaded"], 16)

        @block.gpsimd
        def _(pool):
            nc.gpsimd.memset(nv[:], 1.0e30).then_inc(sems["pad"], 1)
            nc.gpsimd.iota(lane_i[:], [[0, 1]], base=0, channel_multiplier=1).then_inc(sems["iota"], 1)
            nc.gpsimd.iota(col_i[:], [[1, P]], base=0, channel_multiplier=0).then_inc(sems["iota"], 1)
            nc.gpsimd.iota(node_i[:], [[P, T]], base=0, channel_multiplier=1).then_inc(sems["iota"], 1)
            pool.wait_ge(sems["info"], 1)
            for t in range(T):
                pool.indirect_dma_start(out=dr["info"], in_=info[:, t, :], in_offset=None,
                                        out_offset=bass.IndirectOffsetOnAxis(ap=place[:, t:t + 1], axis=0)
                                        ).then_inc(sems["scattered"], 16)
            pool.wait_ge(sems["scattered"], 16 * T)

        @block.vector
        def _(v):
            st = Steps(v, sems["steps"])
            v.wait_ge(sems["iota"], 3)
            st.add(v.tensor_copy(lane[:], lane_i[:]))
            st.add(v.tensor_copy(col[:], col_i[:]))
            st.add(v.memset(zero[:], 0.0))
            st.wait()
            st.do(v.tensor_scalar(tri[:], col[:], lane[:], None, ALU.is_lt))
            v.wait_ge(sems["loaded"], 16 * 6)
            st.do(v.tensor_tensor_scan(cum[:], row[:], zero[:], 0.0, ALU.add, ALU.add))
            v.tensor_tensor(cum[:], cum[:], row[:], ALU.subtract).then_inc(sems["starts"], 1)
            v.tensor_tensor(key[:], key[:], nv[:], ALU.add).then_inc(sems["keys"], 1)
            rank(v, st, by_deg, deg_all, deg, ALU.is_gt, ALU.is_ge, tri[:], junk, cnt)
            v.wait_ge(sems["reloaded"], 32)
            v.wait_ge(sems["keys"], 1)
            rank(v, st, by_key, key_all, key, ALU.is_lt, ALU.is_le, tri[:], junk, cnt)
            st.add(v.tensor_copy(info[:, :, 0], node_i[:]))
            st.add(v.tensor_copy(info[:, :, 1], start[:]))
            st.add(v.tensor_copy(info[:, :, 2], deg[:]))
            st.add(v.tensor_copy(info[:, :, 3], by_key[:]))
            v.tensor_copy(place[:], by_deg[:]).then_inc(sems["info"], 1)
    finish(nc, list(sems.values()))


def fetch_nodes(nc, io, dr, kp):
    with ExitStack() as ctx:
        def sb(name, shape, dt=F32):
            return ctx.enter_context(nc.sbuf_tensor(name, shape, dt))
        names = ["f_loaded", "f_steps", "f_zero", "f_nodes", "f_iota"]
        sems = {n[2:]: nc.alloc_semaphore(n) for n in names}
        first = sb("f_first", [1, T], I32)
        per_i = sb("f_per", [1, 3, T], I32)
        per = sb("f_perf", [1, 3, T])
        cum = sb("f_cum", [1, 3, T])
        zero = sb("f_zero_sb", [1, T])
        deg_i = sb("f_degi", [P, T], I32)
        i1, i2, i3 = sb("f_i1", [P, P], I32), sb("f_i2", [P, 1], I32), sb("f_i3", [P, S], I32)
        f1, f2 = sb("f_f1", [P, P]), sb("f_f2", [P, 1])
        block = ctx.enter_context(nc.Block())

        @block.sync
        def _(sp):
            with nc.allow_non_contiguous_dma(reason="records of four words"):
                sp.dma_start(kp["info"][:], dr["info"].rearrange("(t p) w -> p t w", p=P)).then_inc(sems["loaded"], 16)
                sp.dma_start(first[:], dr["info"].rearrange("(t p) w -> p w t", p=P)[0:1, 2, :]
                             ).then_inc(sems["loaded"], 16)
            sp.wait_ge(sems["loaded"], 32)

        @block.gpsimd
        def _(pool):
            nc.gpsimd.iota(i1[:], [[1, P]], base=0, channel_multiplier=0).then_inc(sems["iota"], 1)
            nc.gpsimd.iota(i2[:], [[0, 1]], base=0, channel_multiplier=1).then_inc(sems["iota"], 1)
            nc.gpsimd.iota(i3[:], [[1, S]], base=0, channel_multiplier=0).then_inc(sems["iota"], 1)
            nc.gpsimd.memset(kp["x"][:], 0.0).then_inc(sems["zero"], 1)
            pool.wait_ge(sems["zero"], 1)
            pool.wait_ge(sems["loaded"], 32)
            for t in range(T):
                pool.indirect_dma_start(out=kp["x"][:, t, :], out_offset=None, in_=io["x"],
                                        in_offset=bass.IndirectOffsetOnAxis(ap=kp["info"][:, t, 0:1], axis=0),
                                        bounds_check=N - 1, oob_is_err=False).then_inc(sems["nodes"], 16)
            pool.wait_ge(sems["nodes"], 16 * T)

        @block.vector
        def _(v):
            st = Steps(v, sems["steps"])
            st.add(v.memset(zero[:], 0.0))
            st.add(v.memset(kp["sched"][:], 0))
            st.add(v.memset(kp["ones"][:], 1.0))
            v.wait_ge(sems["iota"], 3)
            st.add(v.tensor_copy(f1[:], i1[:]))
            st.add(v.tensor_copy(f2[:], i2[:]))
            st.add(v.tensor_copy(kp["slot_no"][:], i3[:]))
            st.wait()
            st.add(v.tensor_scalar(kp["ident"][:], f1[:], f2[:], None, ALU.is_equal))
            v.wait_ge(sems["loaded"], 32)
            st.do(v.tensor_copy(kp["deg"][:], kp["info"][:, :, 2]))
            st.add(v.tensor_scalar(kp["has_edges"][:], kp["deg"][:], 1.0, None, ALU.min))
            st.do(v.tensor_scalar(kp["inv_deg"][:], kp["deg"][:], 1.0, None, ALU.max))
            st.do(v.reciprocal(kp["inv_deg"][:], kp["inv_deg"][:]))
            st.do(v.tensor_scalar(per[:, 0, :], first[:], float(S - 1), None, ALU.add))
            st.do(v.tensor_copy(per_i[:, 0, :], per[:, 0, :]))
            st.do(v.tensor_scalar(per_i[:, 0, :], per_i[:, 0, :], S.bit_length() - 1, None, ALU.logical_shift_right))
            st.do(v.tensor_scalar(per[:, 0, :], per_i[:, 0, :], 2.0, None, ALU.max))
            st.do(v.tensor_scalar(per[:, 1, :], per[:, 0, :], 1.0, None, ALU.add))
            st.do(v.tensor_copy(per_i[:, 1, :], per[:, 1, :]))
            st.do(v.tensor_scalar(per_i[:, 1, :], per_i[:, 1, :], 1, None, ALU.logical_shift_right))
            st.do(v.tensor_copy(per[:, 1, :], per_i[:, 1, :]))
            st.do(v.tensor_tensor(per[:, 2, :], per[:, 0, :], per[:, 1, :], ALU.subtract))
            st.do(v.tensor_copy(kp["sched"][:, PAIRS, 0:T], per[:, 2, :]))
            st.do(v.tensor_tensor(kp["sched"][:, TAIL, 0:T], per[:, 1, :], per[:, 2, :], ALU.subtract))
            for k in (CHUNKS, USES_0, USES_1):
                st.do(v.tensor_tensor_scan(cum[:, k, :], per[:, k, :], zero[:], 0.0, ALU.add, ALU.add))
                st.do(v.tensor_copy(kp["sched"][:, k, 1:T + 1], cum[:, k, :]))
    finish(nc, list(sems.values()))


def bounds(eng, kp, t):
    lo = eng.value_load(kp["sched"][0:1, 1, bass.ds(t, 1)], min_val=0, max_val=CHUNKS_MAX // 2)
    hi = eng.value_load(kp["sched"][0:1, 1, bass.ds(t + 1, 1)], min_val=1, max_val=CHUNKS_MAX // 2)
    return lo, hi


def build_slots(nc, io, dr, kp):
    with ExitStack() as ctx:
        def sb(name, shape, dt=F32):
            return ctx.enter_context(nc.sbuf_tensor(name, shape, dt))
        names = ["b_zero", "b_steps", "b_index", "b_runs", "b_slots", "b_stored", "b_pace", "b_begun", "b_ended",
                 "b_loaded", "b_tile", "b_turned", "b_xt", "b_made", "b_row", "b_written", "b_kept"]
        sems = {n[2:]: nc.alloc_semaphore(n) for n in names}
        edge = sb("b_edge", [P, 1])
        edge_i = sb("b_edgei", [P, 1], I32)
        left = sb("b_left", [P, 1])
        run = sb("b_run", [P, 2, RUN], I32)
        src = sb("b_src", [P, RUN], I32)
        number = sb("b_number", [P, RUN])
        off, on = sb("b_off", [P, RUN]), sb("b_on", [P, RUN])
        slot_i = sb("b_sloti", [P, RUN], I32)
        slots = sb("b_slots_sb", [P, RUN // S, 4, S])
        slots_i = slots[:].bitcast(I32)
        w, bias = sb("p_w", [P, 2, 4 * F]), sb("p_b", [1, 4 * F])
        x_all = sb("p_xall", [P, T, F])
        tile = [sb(f"p_tile{k}", [P, F]) for k in range(2)]
        xt = [sb(f"p_xt{k}", [P, 2, P]) for k in range(2)]
        row = sb("p_row", [P, 2 * F])
        ps_t = [ctx.enter_context(nc.psum_tensor(f"p_pst{k}", [P, 4, P], F32))[:, 0:2, :] for k in range(2)]
        ps = [ctx.enter_context(nc.psum_tensor(f"p_ps{k}", [P, 512], F32)) for k in range(2)]
        full = N // P
        LOADS = 2 + 8
        PER = 9
        block = ctx.enter_context(nc.Block())
        two = "p (k s) -> p k s"

        @block.vector
        def _(v):
            v.memset(run[:], 0).then_inc(sems["zero"], 1)
            v.wait_ge(sems["zero"], 2)
            v.tensor_copy(number[:], slot_i[:]).then_inc(sems["zero"], 1)
            v.wait_ge(sems["zero"], 3)
            with v.Fori(0, T) as t:
                lo, hi = bounds(v, kp, t)
                st = Steps(v, sems["steps"], t * 2 + lo * PER)
                st.add(v.tensor_copy(edge[:], kp["info"][:, bass.ds(t, 1), 1]))
                st.add(v.tensor_copy(left[:], kp["deg"][:, bass.ds(t, 1)]))
                st.wait()
                v.sem_inc(sems["begun"], 1)
                with v.Fori(lo, hi) as c:
                    st = Steps(v, sems["steps"], t * 2 + 2 + c * PER)
                    v.tensor_copy(edge_i[:], edge[:]).then_inc(sems["index"], 1)
                    st.do(v.tensor_scalar(on[:], number[:], left[:], None, ALU.is_lt))
                    st.do(v.tensor_scalar(off[:], on[:], -FAR, FAR, ALU.mult, ALU.add))
                    st.add(v.tensor_scalar(edge[:], edge[:], float(RUN), None, ALU.add))
                    st.add(v.tensor_scalar(left[:], left[:], float(-RUN), None, ALU.add))
                    v.wait_ge(sems["runs"], (c + 1) * 16)
                    v.wait_ge(sems["stored"], c * 16 + 16)
                    st.do(v.tensor_scalar(src[:], run[:, 0, :], 5, None, ALU.logical_shift_right))
                    st.add(v.tensor_tensor(slots_i[:, :, 0, :], src[:].rearrange(two, s=S),
                                           off[:].rearrange(two, s=S), ALU.add))
                    st.add(v.tensor_tensor(slots_i[:, :, 1, :], run[:, 0, :].rearrange(two, s=S),
                                           off[:].rearrange(two, s=S), ALU.add))
                    st.add(v.tensor_tensor(slots[:, :, 2, :], run[:, 1, :].bitcast(F32).rearrange(two, s=S),
                                           on[:].rearrange(two, s=S), ALU.mult))
                    st.add(v.tensor_scalar(slots[:, :, 3, :], off[:].rearrange(two, s=S), LOW / FAR, None, ALU.mult))
                    st.wait()
                    v.sem_inc(sems["slots"], 1)
                    assert st.n == PER

        @block.gpsimd
        def _(pool):
            nc.gpsimd.iota(slot_i[:], [[1, RUN]], base=0, channel_multiplier=0).then_inc(sems["zero"], 1)
            with pool.Fori(0, T) as t:
                lo, hi = bounds(pool, kp, t)
                with pool.Fori(lo, hi) as c:
                    pool.wait_ge(sems["slots"], c + 1)
                    pool.sem_inc(sems["pace"], 1)
                    pool.wait_ge(sems["index"], c + 1)
                    pool.sem_inc(sems["pace"], 1)
                    pool.indirect_dma_start(out=run[:].rearrange("p k s -> p (k s)"), out_offset=None, in_=dr["runs"],
                                            in_offset=bass.IndirectOffsetOnAxis(ap=edge_i[:, 0:1], axis=0),
                                            bounds_check=E - 1, oob_is_err=False).then_inc(sems["runs"], 16)

        @block.sync
        def _(sp):
            sp.sem_inc(sems["stored"], 16)
            sp.sem_inc(sems["slots"], 1)
            with sp.Fori(0, T) as t:
                lo, hi = bounds(sp, kp, t)
                with sp.Fori(lo, hi) as c:
                    sp.wait_ge(sems["slots"], c + 2)
                    sp.dma_start(dr["slots"][bass.ds(c * 2, 2)].rearrange("k p w -> p k w"),
                                 slots[:].rearrange("p k w s -> p k (w s)")).then_inc(sems["stored"], 16)
            last = sp.value_load(kp["sched"][0:1, 1, T:T + 1], min_val=1, max_val=CHUNKS_MAX // 2)
            sp.wait_ge(sems["stored"], last * 16 + 16)
            sp.sem_inc(sems["ended"], 1)

        @block.tensor
        def _(pe):
            pe.wait_ge(sems["loaded"], 16 * LOADS)
            with pe.Fori(0, T) as t:
                for k in range(2):
                    pe.wait_ge(sems["tile"], t * 2 + k + 1)
                    transposed(pe, ps_t[k], tile[k], kp["ident"][:]).then_inc(sems["turned"], 1)
                for k in range(2):
                    pe.wait_ge(sems["xt"], t * 2 + k + 1)
                    product(pe, ps[k][:], xt[k], w[:, :, k * 512:(k + 1) * 512], bias[:, k * 512:(k + 1) * 512],
                            kp["ones"][:, :]).then_inc(sems["made"], 1)

        @block.scalar
        def _(act):
            act.sem_inc(sems["written"], 16)
            for i, k in enumerate(("k", "v", "q", "skip")):
                act.dma_start(w[:, :, i * F:(i + 1) * F], halves(io["L0_gnn_W" + k])).then_inc(sems["loaded"], 16)
                act.dma_start(bias[:, i * F:(i + 1) * F], rows_of(io["L0_gnn_b" + k])).then_inc(sems["loaded"], 16)
            act.activation(x_all[:, full, :], kp["x"][:, 0, :], ACT.Copy).then_inc(sems["row"], 1)
            act.wait_ge(sems["row"], 1)
            act.dma_start(x_all[:, 0:full, :], io["x"][0:full * P, :].rearrange("(t p) f -> p t f", p=P)
                          ).then_inc(sems["loaded"], 16)
            act.dma_start(x_all[0:N - full * P, full, :], io["x"][full * P:N, :]).then_inc(sems["loaded"], 16)
            act.wait_ge(sems["loaded"], 16 * LOADS)
            with act.Fori(0, T) as t:
                for k in range(2):
                    act.activation(tile[k][:], tile_of((x_all, kp["x"])[k], t), ACT.Copy).then_inc(sems["tile"], 1)
                for k in range(2):
                    act.wait_ge(sems["turned"], t * 2 + k + 1)
                    act.activation(xt[k][:], ps_t[k], ACT.Copy).then_inc(sems["xt"], 1)
                act.wait_ge(sems["made"], t * 2 + 1)
                act.wait_ge(sems["written"], t * 16 + 16)
                act.activation(row[:], ps[0][:], ACT.Copy).then_inc(sems["row"], 1)
                act.wait_ge(sems["row"], t + 2)
                act.dma_start(dr["kv"][bass.ds(t * P, P), :], row[:]).then_inc(sems["written"], 16)
                act.wait_ge(sems["made"], t * 2 + 2)
                act.activation(tile_of(kp["a"], t), ps[1][:, 0:F], ACT.Copy).then_inc(sems["kept"], 1)
                act.activation(tile_of(kp["b"], t), ps[1][:, F:2 * F], ACT.Copy).then_inc(sems["kept"], 1)
            act.wait_ge(sems["written"], T * 16 + 16)
    finish(nc, list(sems.values()))


def transposed(pe, ps, tile, ident, parts=2):
    for k in range(parts):
        ins = pe.transpose(ps[:, k, :], tile[:, k * P:(k + 1) * P], ident)
    return ins


def product(pe, out, lhs_t, weight, bias=None, ones=None, start=True, stop=True):
    parts = lhs_t.shape[1]
    for k in range(parts):
        ins = pe.matmul(out, lhs_t[:, k, :], weight[:, k, :], start=start and k == 0,
                        stop=stop and bias is None and k == parts - 1)
    if bias is not None:
        ins = pe.matmul(out, ones, bias, start=False, stop=stop)
    return ins


def halves(w):
    return w.rearrange("(k p) o -> p k o", p=P)


def normal_stats(v, st, sems, small, src):
    st.do(v.bn_stats(small[:, 0:6], src))
    v.sem_inc(sems["stats"], 1)
    st.do(v.bn_aggr(small[:, 6:8], small[:, 0:6]))
    v.tensor_scalar(small[:, 8:9], small[:, 7:8], EPS, None, ALU.add).then_inc(sems["variance"], 1)


def normal_apply(v, st, sems, small, out, src, n, gain=None, offset=None):
    v.wait_ge(sems["root"], n)
    st.do(v.reciprocal(small[:, 10:11], small[:, 9:10]))
    ins = v.tensor_scalar(out, src, small[:, 6:7], small[:, 10:11], ALU.subtract, ALU.mult)
    if gain is not None:
        st.do(ins)
        st.do(v.tensor_tensor(out, out, gain, ALU.mult))
        ins = v.tensor_tensor(out, out, offset, ALU.add)
    return ins


def root_of(act, sems, small, n):
    act.wait_ge(sems["variance"], n)
    act.activation(small[:, 9:10], small[:, 8:9], ACT.Sqrt).then_inc(sems["root"], 1)


def tile_of(buf, t):
    if isinstance(t, int):
        return buf[:, t, :]
    return buf[:, bass.ds(t, 1), :].rearrange("p a f -> p (a f)")


LAYERS = {
    "conv": dict(heads=8, width=2 * F, table="kv", values=F, limit=NP - 1),
    "rel": dict(heads=0, width=F, table="messages", values=0, limit=NP * RELS - 1),
    "gat1": dict(heads=8, width=F + 8, table="gat1", values=0, limit=NP - 1),
    "gat2": dict(heads=1, width=F + 1, table="gat2", values=0, limit=NP - 1),
    "gat3": dict(heads=4, width=F + 4, table="gat3", values=0, limit=NP - 1),
}
PRODUCTS = {
    "conv": ([], []),
    "rel": (["fc1"], []),
    "gat1": (["wb0", "wb1a", "wb1b", "fc2"], ["bb0", "bb1"]),
    "gat2": (["gat"], []),
    "gat3": ([], []),
}
VECTORS = {
    "conv": ["L0_gnn_gamma", "L0_gnn_beta"],
    "rel": ["L2_gnn_attn_l1", "L2_gnn_attn_r1"],
    "gat1": ["L2_gnn_bias1", "L2_gnn_attn_l2", "L2_gnn_attn_r2"],
    "gat2": ["L2_gnn_bias2", "L3_gnn_gat_a_src", "L3_gnn_gat_a_tgt"],
    "gat3": [],
}
NEXT = {"rel": ("gat1", 8, "fc1"), "gat1": ("gat2", 1, "fc2"), "gat2": ("gat3", 4, "gat")}


CHUNKS, USES_0, USES_1, PAIRS, TAIL = range(5)


class Visit:

    def __init__(self, eng, kp, t):
        def read(row, at, least, most):
            return eng.value_load(kp["sched"][0:1, row, bass.ds(at, 1)], min_val=least, max_val=most)
        self.chunks = read(CHUNKS, t, 0, CHUNKS_MAX)
        self.before = [read(USES_0, t, 0, CHUNKS_MAX // 2), read(USES_1, t, 0, CHUNKS_MAX // 2)]
        self.pairs, self.tail = read(PAIRS, t, 1, E // RUN + 1), read(TAIL, t, 0, 1)
        self.chunks_end = self.chunks + self.pairs * 2 + self.tail

    def uses(self, j, b):
        return self.before[b] + j

    def chunk(self, j, b):
        return self.chunks + j * 2 + b


def visit(eng, kp, t, chunk, in_first=None):
    w = Visit(eng, kp, t)
    if in_first is None:
        with eng.Fori(0, w.pairs) as j:
            chunk(w, j, 0)
            chunk(w, j, 1)
    else:
        in_first(w)
        with eng.If(w.pairs > 1):
            with eng.Fori(1, w.pairs) as j:
                chunk(w, j, 0)
                chunk(w, j, 1)
    with eng.If(w.tail > 0):
        chunk(w, w.pairs, 0)
    return w


def edge_layer(nc, io, dr, kp, layer):
    cfg = LAYERS[layer]
    H, width, values, table = cfg["heads"], cfg["width"], cfg["values"], dr[cfg["table"]]
    D = F // H if H else 0
    nxt = NEXT.get(layer)
    weights, biases = PRODUCTS[layer]
    scans = layer == "gat2"
    with ExitStack() as ctx:
        def sb(name, shape, dt=F32):
            return ctx.enter_context(nc.sbuf_tensor(f"{layer}_{name}", shape, dt))

        def sem(name):
            s = nc.alloc_semaphore(f"{layer}_{name}")
            all_sems.append(s)
            return s
        all_sems = []
        index_in, extras_in, gathered, released = (
            [sem(f"{n}{b}") for b in range(2)] for n in ("index_in", "extras_in", "gathered", "released"))
        begun, zeroed, folded = sem("begun"), sem("zeroed"), sem("folded")
        pace, steps, logits_ready, probs_ready = sem("pace"), sem("steps"), sem("logits_ready"), sem("probs_ready")
        loaded, rows_ready, written, xt_ready = sem("loaded"), sem("rows_ready"), sem("written"), sem("xt_ready")
        turned, made, pre_gelu, gelu_done = sem("turned"), sem("made"), sem("pre_gelu"), sem("gelu_done")
        new_x, ended, summed = sem("new_x"), sem("ended"), sem("summed")
        sems = {"stats": sem("stats"), "variance": sem("variance"), "root": sem("root")}

        index = [sb(f"index{b}", [P, S], I32) for b in range(2)]
        extras = [sb(f"extras{b}", [P, 2, S]) for b in range(2)]
        rows = [sb(f"rows{b}", [P, S, width]) for b in range(2)]
        spares = [sb(f"spare{b}", [1, 4], I32) for b in range(3)]
        h = max(H, 1)
        acc, red = sb("acc", [P, F]), sb("red", [P, F])
        work = sb("work", [P, S, F])
        dots = sb("dots", [P, S, F]) if layer == "conv" else None
        pe_sums = layer == "conv"
        own = sb("own", [P, F if layer == "conv" else 8])
        logit, logit2 = sb("logit", [P, S + 1, h]), sb("logit2", [P, S, h])
        prob = sb("prob", [P, S + 1, h])
        top, new_top, den, part = (sb(n, [P, h]) for n in ("top", "newtop", "den", "part"))
        small = sb("small", [P, 12])
        out, tmp, cur, act_out = sb("out", [P, F]), sb("tmp", [P, F]), sb("cur", [P, F]), sb("actout", [P, F])
        hid = sb("hid", [P, F])
        vec = {n: sb("v_" + n, [P, F]) for n in VECTORS[layer]}
        HN = nxt[1] if nxt else 0
        wide = F + 2 * HN
        wt = {n: sb("w_" + n, [P, 2, wide if nxt and n == nxt[2] else F]) for n in weights}
        bias = {n: sb("b_" + n, [1, F]) for n in biases}
        xt, ht = sb("xt", [P, 2, P]), sb("ht", [P, 2, P])
        stage = sb("stage", [P, F + HN])
        node = sb("node", [P, 2], I32)
        banks = [ctx.enter_context(nc.psum_tensor(f"{layer}_ps{k}", [P, 512], F32)) for k in range(6)]
        ps_t, ps_h = (bank[:, 0:F].rearrange("p (k c) -> p k c", k=2) for bank in banks[0:2])
        ps, ps_sum = banks[2:5], banks[5][:, 0:F]
        loads = 16 * (len(VECTORS[layer]) + len(weights) + len(biases))
        block = ctx.enter_context(nc.Block())
        which = 1 if layer == "rel" else 0
        per_head = "p s (h d) -> p s h d"
        as_heads = "p (h d) -> p h d"

        @block.sync
        def _(sp):
            for n in VECTORS[layer]:
                flat = io[n] if len(io[n].shape) == 1 else io[n].rearrange("a b -> (a b)")
                sp.dma_start(vec[n][:], on_all(flat)).then_inc(loaded, 16)
            for n in weights:
                sp.dma_start(wt[n][:, :, 0:F], halves(io[n])).then_inc(loaded, 16)
            for n in biases:
                sp.dma_start(bias[n][:], rows_of(io["L2_gnn_" + n])).then_inc(loaded, 16)

            def load_record(w, a, b):
                u = w.uses(a, b)
                pair = w.uses(a, 0).with_bounds(min_val=0, max_val=CHUNKS_MAX // 2)
                record = dr["slots"][bass.ds(pair * 2 + b, 1)].rearrange("k p (w s) -> p (k w) s", s=S)
                sp.wait_ge(gathered[b], 16 + u * 16 * S)
                sp.dma_start(index[b][:], record[:, which, :].bitcast(I32)).then_inc(index_in[b], 16)
                sp.wait_ge(released[b], u + 1)
                sp.dma_start(extras[b][:], record[:, 2:4, :]).then_inc(extras_in[b], 16)

            with sp.Fori(0, T) as t:
                visit(sp, kp, t, load_record)

        @block.gpsimd
        def _(pool):
            prime(pool, dr, spares[2], written)
            for b in range(2):
                nc.gpsimd.memset(rows[b][:], 0.0).then_inc(zeroed, 1)
                prime(pool, dr, spares[b], gathered[b])
            pool.wait_ge(zeroed, 2)

            def gather(w, a, b):
                u = w.uses(a, b)
                pool.wait_ge(index_in[b], (u + 1) * 16)
                pool.sem_inc(pace, 1)
                pool.wait_ge(released[b], u + 1)
                pool.sem_inc(pace, 1)
                for s in range(S):
                    pool.indirect_dma_start(
                        out=rows[b][:, s, :], out_offset=None, in_=table,
                        in_offset=bass.IndirectOffsetOnAxis(ap=index[b][:, s:s + 1], axis=0),
                        bounds_check=cfg["limit"], oob_is_err=False).then_inc(gathered[b], 16)

            def scatter(t):
                pool.wait_ge(rows_ready, t + 2)
                pool.sem_inc(pace, 1)
                pool.indirect_dma_start(out=dr[nxt[0]], in_=stage[:], in_offset=None,
                                        out_offset=bass.IndirectOffsetOnAxis(ap=node[:, 0:1], axis=0)
                                        ).then_inc(written, 16)
                if scans:
                    pool.indirect_dma_start(out=dr["scan_x"], in_=cur[:], in_offset=None,
                                            out_offset=bass.IndirectOffsetOnAxis(ap=node[:, 1:2], axis=0)
                                            ).then_inc(written, 16)

            visit(pool, kp, 0, gather)
            with pool.Fori(1, T) as t:
                visit(pool, kp, t, gather)
                if nxt:
                    scatter(t - 1)
            if nxt:
                scatter(T - 1)
            pool.wait_ge(written, 16 + (16 * T * (1 + scans) if nxt else 0))

        @block.vector
        def _(v):
            PER, PRO, END, HOOKS, START = kp["counts"][layer]
            TILE = PRO + END + HOOKS
            for b in range(2):
                v.sem_inc(released[b], 1)
            st = Steps(v, steps)
            if loads:
                v.wait_ge(loaded, loads)
            if nxt:
                left, right = VECTORS[layer][-2:]
                full = wt[nxt[2]]
                for k in range(2):
                    for i, name in enumerate((left, right)):
                        st.do(v.tensor_tensor(tmp[:], full[:, k, 0:F], vec[name][:], ALU.mult))
                        st.do(v.tensor_reduce(full[:, k, F + i * HN:F + (i + 1) * HN],
                                              tmp[:].rearrange(as_heads, h=HN), X, ALU.add))
                v.sem_inc(folded, 1)
            assert st.n == START, (layer, 4, st.n)

            def logits(st, w, a, b):
                u = w.uses(a, b)
                v.wait_ge(gathered[b], 16 + (u + 1) * 16 * S)
                v.wait_ge(extras_in[b], (u + 1) * 16)
                if not H:
                    for s in range(S):
                        ins = v.scalar_tensor_tensor(acc[:], rows[b][:, s, :], extras[b][:, 0, s:s + 1], acc[:],
                                                     ALU.mult, ALU.add)
                        if s < S - 1:
                            st.do(ins)
                    ins.then_inc(released[b], 1)
                    v.wait_ge(released[b], u + 2)
                    return
                lg = logit[:, 0:S, :]
                if layer == "conv":
                    st.do(v.tensor_tensor(dots[:], rows[b][:, :, 0:F], over_slots(own[:], S), ALU.mult))
                    st.do(v.tensor_reduce(lg, dots[:].rearrange(per_head, h=H), X, ALU.add))
                else:
                    st.do(v.tensor_tensor(logit2[:], rows[b][:, :, F:F + H], over_slots(own[:, 0:H], S), ALU.add))
                    st.do(v.scalar_tensor_tensor(lg, logit2[:], 0.2, logit2[:], ALU.mult, ALU.max))
                st.do(v.tensor_tensor(lg, lg, over_dims(extras[b][:, 1, :], H), ALU.add))
                st.do(v.tensor_reduce(new_top[:], lg.rearrange("p s h -> p h s"), X, ALU.max))
                st.do(v.tensor_tensor(new_top[:], new_top[:], top[:], ALU.max))
                st.add(v.tensor_tensor(lg, lg, over_slots(new_top[:], S), ALU.subtract))
                v.tensor_tensor(logit[:, S, :], top[:], new_top[:], ALU.subtract).then_inc(logits_ready, 1)

            def add_sums(count):
                v.wait_ge(summed, count)
                return v.tensor_tensor(acc[:], acc[:], ps_sum, ALU.add)

            def weigh(st, w, a, b):
                if not H:
                    return
                if pe_sums:
                    if isinstance(a, int) and a == 0 and b == 0:
                        st.do(v.memset(acc[:], 0.0))
                    else:
                        st.do(add_sums(w.chunk(a, b)))
                u = w.uses(a, b)
                v.wait_ge(probs_ready, w.chunk(a, b) + 1)
                v.tensor_tensor(work[:].rearrange(per_head, h=H),
                                rows[b][:, :, values:values + F].rearrange(per_head, h=H),
                                over_dims(prob[:, 0:S, :], D), ALU.mult).then_inc(released[b], 1)
                st.add(v.tensor_copy(top[:], new_top[:]))
                st.add(v.tensor_tensor(den[:], den[:], prob[:, S, :], ALU.mult))
                st.add(v.tensor_reduce(part[:], prob[:, 0:S, :].rearrange("p s h -> p h s"), X, ALU.add))
                st.add(v.tensor_tensor(acc[:].rearrange(as_heads, h=H), acc[:].rearrange(as_heads, h=H),
                                       over_dims(prob[:, S, :], D), ALU.mult))
                if not pe_sums:
                    v.wait_ge(released[b], u + 2)
                    st.add(v.tensor_reduce(red[:], work[:].rearrange("p s f -> p f s"), X, ALU.add))
                st.wait()
                ins = v.tensor_tensor(den[:], den[:], part[:], ALU.add)
                if not pe_sums:
                    st.add(ins)
                    ins = v.tensor_tensor(acc[:], acc[:], red[:], ALU.add)
                st.do(ins)

            def softmax_sum(st, t):
                st.do(v.reciprocal(part[:], den[:]))
                st.do(v.tensor_scalar(part[:], part[:], kp["has_edges"][:, bass.ds(t, 1)], None, ALU.mult))
                return v.tensor_tensor(out[:].rearrange(as_heads, h=H), acc[:].rearrange(as_heads, h=H),
                                       over_dims(part[:], D), ALU.mult)

            def end_tile(st, w, t):
                if pe_sums:
                    st.do(add_sums(w.chunks_end))
                if layer == "conv":
                    st.do(softmax_sum(st, t))
                    v.tensor_tensor(out[:], out[:], tile_of(kp["b"], t), ALU.add).then_inc(pre_gelu, 1)
                elif layer == "rel":
                    st.do(v.scalar_tensor_tensor(out[:], acc[:], 0.0, tile_of(kp["x"], t), ALU.max, ALU.add))
                    normal_stats(v, st, sems, small, out[:])
                elif layer == "gat1":
                    st.do(softmax_sum(st, t))
                    st.add(v.tensor_tensor(out[:], out[:], vec["L2_gnn_bias1"][:], ALU.add))
                    v.wait_ge(rows_ready, t + 1)
                    v.tensor_copy(cur[:], tile_of(kp["x"], t)).then_inc(new_x, 1)
                elif layer == "gat2":
                    st.do(softmax_sum(st, t))
                    st.do(v.tensor_tensor(out[:], out[:], vec["L2_gnn_bias2"][:], ALU.add))
                    st.do(v.scalar_tensor_tensor(out[:], tile_of(kp["a"], t), kp["inv_deg"][:, bass.ds(t, 1)],
                                                 out[:], ALU.mult, ALU.add))
                    st.do(v.tensor_tensor(out[:], out[:], tile_of(kp["x"], t), ALU.add))
                    normal_stats(v, st, sems, small, out[:])
                else:
                    st.add(v.tensor_copy(tile_of(kp["a"], t), acc[:]))
                    st.add(v.tensor_copy(tile_of(kp["den"], t), den[:]))
                    st.add(v.tensor_copy(tile_of(kp["top"], t), top[:]))
                    st.wait()

            def node_numbers(st, t):
                v.wait_ge(written, 16 + 16 * (1 + scans) * t)
                st.add(v.tensor_copy(node[:, 0:1], kp["info"][:, bass.ds(t, 1), 0]))
                st.add(v.tensor_copy(node[:, 1:2], kp["info"][:, bass.ds(t, 1), 3]))

            def finish_tile(st, t, place):
                if layer == "conv" and place == 1:
                    v.wait_ge(gelu_done, t + 1)
                    st.do(v.tensor_tensor(out[:], act_out[:], tile_of(kp["x"], t), ALU.add))
                    normal_stats(v, st, sems, small, out[:])
                elif layer == "conv" and place == 2:
                    st.do(normal_apply(v, st, sems, small, tmp[:], out[:], 2 * t + 1, vec["L0_gnn_gamma"][:],
                                       vec["L0_gnn_beta"][:]))
                    st.do(v.tensor_tensor(out[:], tmp[:], tile_of(kp["x"], t), ALU.add))
                    normal_stats(v, st, sems, small, out[:])
                    st.do(normal_apply(v, st, sems, small, tile_of(kp["x"], t), out[:], 2 * t + 2))
                elif (layer, place) in (("rel", 0), ("gat2", 0)):
                    node_numbers(st, t)
                    v.wait_ge(rows_ready, t + 1)
                    st.do(normal_apply(v, st, sems, small, cur[:], out[:], t + 1))
                    v.sem_inc(new_x, 1)
                elif layer == "gat1" and place == 0:
                    node_numbers(st, t)
                    v.wait_ge(made, 2 * t + 1)
                    st.do(v.scalar_tensor_tensor(out[:], ps[0][:, 0:F], kp["inv_deg"][:, bass.ds(t, 1)], out[:],
                                                 ALU.mult, ALU.add))
                    st.do(v.tensor_scalar(hid[:], out[:], 0.0, None, ALU.max))
                    v.sem_inc(new_x, 1)

            def tile(t, first):
                base = START + PRO + END + (t - 1) * TILE if not first else START
                hooks = 0 if first else HOOKS
                w = Visit(v, kp, t)
                st = Steps(v, steps, base + w.chunk(0, 0) * PER)
                if not pe_sums:
                    st.add(v.memset(acc[:], 0.0))
                if H:
                    st.add(v.memset(den[:], 0.0))
                    st.add(v.memset(top[:], LOW))
                    st.add(v.tensor_copy(own[:] if layer == "conv" else own[:, 0:H],
                                         tile_of(kp["a"], t) if layer == "conv" else
                                         kp["er"][:, bass.ds(t, 1), 0:H].rearrange("p a h -> p (a h)")))
                st.wait()
                v.sem_inc(begun, 1)
                assert st.n == PRO, (layer, 1, st.n)
                for b in range(2):
                    n = st.n
                    logits(st, w, 0, b)
                    PER_NOW = st.n - n
                    if b == 1 and not first:
                        finish_tile(st, t - 1, 1)
                    n = st.n
                    weigh(st, w, 0, b)
                    PER_NOW += st.n - n
                    assert PER_NOW == PER, (layer, 0, PER_NOW)
                    if not first:
                        finish_tile(st, t - 1, 0 if b == 0 else 2)
                if not first:
                    assert st.n - PRO - 2 * PER == HOOKS, (layer, 3, st.n - PRO - 2 * PER)

                def chunk(w, a, b):
                    st = Steps(v, steps, base + PRO + hooks + w.chunk(a, b) * PER)
                    logits(st, w, a, b)
                    weigh(st, w, a, b)

                v.sem_inc(ended, 1)
                with v.If(w.pairs > 1):
                    with v.Fori(1, w.pairs) as a:
                        chunk(w, a, 0)
                        chunk(w, a, 1)
                        v.sem_inc(ended, 1)
                with v.If(w.tail > 0):
                    chunk(w, w.pairs, 0)
                    v.sem_inc(ended, 1)
                st = Steps(v, steps, base + PRO + hooks + w.chunks_end * PER)
                end_tile(st, w, t)
                v.sem_inc(ended, 1)
                assert st.n == END, (layer, 2, st.n)

            tile(0, True)
            with v.Fori(1, T) as t:
                tile(t, False)
            chunks = v.value_load(kp["sched"][0:1, CHUNKS, T:T + 1], min_val=1, max_val=CHUNKS_MAX)
            st = Steps(v, steps, START + T * TILE - HOOKS + chunks * PER)
            for place in range(3):
                finish_tile(st, T - 1, place)
            v.sem_inc(ended, 1)

        @block.scalar
        def _(act):
            act.sem_inc(rows_ready, 1)

            def exp(w, a, b):
                act.wait_ge(logits_ready, w.chunk(a, b) + 1)
                act.activation(prob[:], logit[:], ACT.Exp, scale=float(D) ** -0.5 if layer == "conv" else 1.0
                               ).then_inc(probs_ready, 1)

            def next_rows(t, source):
                act.wait_ge(written, 16 + 16 * (1 + scans) * t)
                act.activation(stage[:], source[:, 0:F + HN], ACT.Copy)
                act.activation(kp["er"][:, bass.ds(t, 1), 0:HN].rearrange("p a h -> p (a h)"),
                               source[:, F + HN:wide], ACT.Copy).then_inc(rows_ready, 1)

            def turn_new_x(t):
                act.wait_ge(turned, t + 1)
                act.activation(xt[:], ps_t, ACT.Copy).then_inc(xt_ready, 1)
                act.activation(tile_of(kp["x"], t), cur[:], ACT.Copy)
                act.wait_ge(made, t + 1)
                next_rows(t, ps[0])

            def finish_tile(t, place):
                if layer == "conv" and place == 0:
                    act.wait_ge(pre_gelu, t + 1)
                    act.activation(act_out[:], out[:], ACT.Gelu).then_inc(gelu_done, 1)
                elif layer == "conv":
                    root_of(act, sems, small, 2 * t + 1)
                    root_of(act, sems, small, 2 * t + 2)
                elif layer == "rel" and place == 0:
                    root_of(act, sems, small, t + 1)
                elif layer == "rel":
                    turn_new_x(t)
                elif layer == "gat1" and place == 0:
                    act.wait_ge(turned, 2 * t + 1)
                    act.activation(xt[:], ps_t, ACT.Copy).then_inc(xt_ready, 1)
                elif layer == "gat1":
                    act.wait_ge(turned, 2 * t + 2)
                    act.activation(ht[:], ps_h, ACT.Copy).then_inc(xt_ready, 1)
                    act.wait_ge(made, 2 * t + 2)
                    act.activation(tile_of(kp["a"], t), ps[1][:, 0:F], ACT.Copy)
                    next_rows(t, ps[2])
                elif layer == "gat2" and place == 0:
                    root_of(act, sems, small, t + 1)
                elif layer == "gat2":
                    turn_new_x(t)

            def first_pair(t):
                def run(w):
                    for b in range(2):
                        exp(w, 0, b)
                        finish_tile(t, b)
                return run

            if H:
                visit(act, kp, 0, exp)
                with act.Fori(1, T) as t:
                    visit(act, kp, t, exp, first_pair(t - 1))
                for place in range(2):
                    finish_tile(T - 1, place)
            else:
                with act.Fori(0, T) as t:
                    for place in range(2):
                        finish_tile(t, place)

        @block.tensor
        def _(pe):
            ident, ones = kp["ident"][:], kp["ones"][:, :]
            if nxt:
                pe.wait_ge(loaded, loads)
                pe.wait_ge(folded, 1)

            def sum_slots(w, a, b):
                pe.wait_ge(released[b], w.uses(a, b) + 2)
                for s in range(S):
                    ins = pe.matmul(ps_sum, ident, work[:, s, :], start=s == 0, stop=s == S - 1)
                ins.then_inc(summed, 1)

            def finish_tile(t, place):
                if layer == "gat1" and place == 0:
                    pe.wait_ge(new_x, 2 * t + 1)
                    transposed(pe, ps_t, cur, ident).then_inc(turned, 1)
                    pe.wait_ge(xt_ready, 2 * t + 1)
                    product(pe, ps[1][:, 0:F], xt, wt["wb1a"], bias["bb1"][:], ones, stop=False)
                    product(pe, ps[0][:, 0:F], xt, wt["wb0"], bias["bb0"][:], ones).then_inc(made, 1)
                elif layer == "gat1":
                    pe.wait_ge(new_x, 2 * t + 2)
                    transposed(pe, ps_h, hid, ident).then_inc(turned, 1)
                    pe.wait_ge(xt_ready, 2 * t + 2)
                    product(pe, ps[1][:, 0:F], ht, wt["wb1b"], start=False)
                    product(pe, ps[2][:, 0:wide], ht, wt["fc2"]).then_inc(made, 1)
                elif nxt and place == 1:
                    pe.wait_ge(new_x, t + 1)
                    transposed(pe, ps_t, cur, ident).then_inc(turned, 1)
                    pe.wait_ge(xt_ready, t + 1)
                    product(pe, ps[0][:, 0:wide], xt, wt[weights[0]]).then_inc(made, 1)

            def first_pair(t):
                def run(w):
                    for b in range(2):
                        sum_slots(w, 0, b)
                        finish_tile(t, b)
                return run

            if pe_sums:
                visit(pe, kp, 0, sum_slots)
                with pe.Fori(1, T) as t:
                    visit(pe, kp, t, sum_slots, first_pair(t - 1))
                for place in range(2):
                    finish_tile(T - 1, place)
            elif nxt:
                with pe.Fori(0, T) as t:
                    for place in range(2):
                        finish_tile(t, place)
    finish(nc, all_sems)


def layer_norm(v, st, sems, small, out, src, gain=None, offset=None):
    normal_stats(v, st, sems, small, src)
    sems["roots_asked"] += 1
    return normal_apply(v, st, sems, small, out, src, sems["roots_before"] + sems["roots_asked"], gain, offset)


def relation_messages(nc, io, dr, kp):
    PARTS = 4
    R = RELS // PARTS
    G = R * F // 512
    with ExitStack() as ctx:
        def sb(name, shape, dt=F32):
            return ctx.enter_context(nc.sbuf_tensor(name, shape, dt))
        names = ["r_loaded", "r_weights", "r_tile", "r_turned", "r_turned_copied", "r_xt", "r_made", "r_staged", "r_index",
                 "r_written0", "r_written1", "r_pace"]
        sems = {n[2:]: nc.alloc_semaphore(n) for n in names}
        bases = sb("r_bases", [P, BASES, 2, F])
        comp = sb("r_comp", [P, RELS * BASES])
        w = [sb(f"r_w{k}", [P, 2, R * F]) for k in range(2)]
        stage = [sb(f"r_stage{k}", [P, R * F]) for k in range(2)]
        tile, xt_all = sb("r_tile_sb", [P, F]), sb("r_xt_all", [P, T, 2 * P])
        xt = [sb(f"r_xt{k}", [P, 2, P]) for k in range(2)]
        numbers = sb("r_numbers", [P, PARTS, T], I32)
        node = [sb(f"r_node{k}", [P, 1], I32) for k in range(2)]
        spare = [sb(f"r_spare{k}", [1, 4], I32) for k in range(2)]
        ps_t = ctx.enter_context(nc.psum_tensor("r_pst", [P, 4, P], F32))[:, 0:2, :]
        ps = ctx.enter_context(nc.psum_tensor("r_ps", [P, 4, 512], F32))
        written = [sems["written0"], sems["written1"]]
        part_rows = dr["messages"].rearrange("(n r) f -> n (r f)", r=R)
        block = ctx.enter_context(nc.Block())

        def steps(eng, q, step):
            first = q * T
            with eng.Fori(0, T // 2) as j:
                for i in range(2):
                    step(j * 2 + i, j * 2 + (first + i), j + (first + i) // 2, (first + i) % 2)
            step(T - 1, first + T - 1, (first + T - 1) // 2, (first + T - 1) % 2)

        assert T % 2 == 1

        @block.sync
        def _(sp):
            for b in range(BASES):
                sp.dma_start(bases[:, b, :, :], halves(io["L1_gnn_bases"][b])).then_inc(sems["loaded"], 16)
            sp.dma_start(comp[:], on_all(io["L1_gnn_w_comp"].rearrange("r b -> (r b)"))).then_inc(sems["loaded"], 16)

        @block.vector
        def _(v):
            for q in range(PARTS):
                v.tensor_scalar(numbers[:, q, :], kp["info"][:, :, 0], float(PARTS), float(q), ALU.mult, ALU.add
                                ).then_inc(sems["index"], 1)
            v.wait_ge(sems["loaded"], 16 * (BASES + 1))
            for q in range(PARTS):
                if q >= 2:
                    v.wait_ge(sems["made"], (q - 1) * T * G + 1)
                with v.Fori(0, R) as r:
                    dst = w[q % 2][:, :, bass.ds(r * F, F)]
                    for b in range(BASES):
                        scale = comp[:, bass.ds(r * BASES + (q * R * BASES + b), 1)]
                        if b == 0:
                            ins = v.tensor_scalar(dst, bases[:, 0, :, :], scale, None, ALU.mult)
                        else:
                            ins = v.scalar_tensor_tensor(dst, bases[:, b, :, :], scale, dst, ALU.mult, ALU.add)
                        ins.then_inc(sems["weights"], 1)
                        v.wait_ge(sems["weights"], r * BASES + (q * R * BASES + b + 1))

        @block.scalar
        def _(act):
            act.sem_inc(sems["made"], 1)
            act.sem_inc(sems["staged"], 4)
            act.sem_inc(sems["turned_copied"], 1)
            with act.Fori(0, T) as t:
                act.wait_ge(sems["turned"], t + 1)
                act.activation(tile[:], tile_of(kp["x"], t), ACT.Copy).then_inc(sems["tile"], 1)
                act.wait_ge(sems["turned"], t + 2)
                act.activation(tile_of(xt_all, t).rearrange("p (k c) -> p k c", k=2), ps_t, ACT.Copy
                               ).then_inc(sems["turned_copied"], 1)
            act.wait_ge(sems["turned_copied"], T + 1)

            def hand_over(t, b):
                act.activation(xt[b][:].rearrange("p k c -> p (k c)"), tile_of(xt_all, t), ACT.Copy
                               ).then_inc(sems["xt"], 1)

            hand_over(0, 0)
            for q in range(PARTS):
                def step(t, n, uses, b):
                    last = isinstance(t, int)
                    if not (last and q == PARTS - 1):
                        act.wait_ge(sems["made"], n * G + 1)
                        hand_over(0 if last else t + 1, 1 - b)
                    act.wait_ge(written[b], uses * 16 + 16)
                    for g in range(G):
                        act.wait_ge(sems["made"], n * G + g + 2)
                        act.activation(stage[b][:, g * 512:(g + 1) * 512], ps[:, g % 4, :], ACT.Copy
                                       ).then_inc(sems["staged"], 1)
                steps(act, q, step)

        @block.tensor
        def _(pe):
            pe.sem_inc(sems["turned"], 1)
            with pe.Fori(0, T) as t:
                pe.wait_ge(sems["tile"], t + 1)
                pe.wait_ge(sems["turned_copied"], t + 1)
                transposed(pe, ps_t, tile, kp["ident"][:]).then_inc(sems["turned"], 1)
            for q in range(PARTS):
                pe.wait_ge(sems["weights"], (q + 1) * R * BASES)

                def step(t, n, uses, b):
                    pe.wait_ge(sems["xt"], n + 1)
                    for g in range(G):
                        pe.wait_ge(sems["staged"], n * G + g + 1)
                        product(pe, ps[:, g % 4, :], xt[b], w[q % 2][:, :, g * 512:(g + 1) * 512]
                                ).then_inc(sems["made"], 1)
                steps(pe, q, step)

        @block.gpsimd
        def _(pool):
            for k in range(2):
                prime(pool, dr, spare[k], written[k])
            pool.wait_ge(sems["index"], PARTS)
            for q in range(PARTS):
                def step(t, n, uses, b):
                    pool.wait_ge(written[b], uses * 16 + 16)
                    pool.sem_inc(sems["pace"], 1)
                    nc.gpsimd.tensor_copy(node[b][:], numbers[:, q, t:t + 1] if isinstance(t, int) else
                                          numbers[:, q, bass.ds(t, 1)]).then_inc(sems["index"], 1)
                    pool.wait_ge(sems["index"], n + 1 + PARTS)
                    pool.sem_inc(sems["pace"], 1)
                    pool.wait_ge(sems["staged"], n * G + G + 4)
                    pool.sem_inc(sems["pace"], 1)
                    pool.indirect_dma_start(out=part_rows, in_=stage[b][:], in_offset=None,
                                            out_offset=bass.IndirectOffsetOnAxis(ap=node[b][:, 0:1], axis=0)
                                            ).then_inc(written[b], 16)
                steps(pool, q, step)
            for k in range(2):
                pool.wait_ge(written[k], (PARTS * T // 2) * 16 + 16)
    finish(nc, list(sems.values()))


def state_scan(nc, io, dr, kp):
    NS, R = 16, 16
    with ExitStack() as ctx:
        def sb(name, shape, dt=F32):
            return ctx.enter_context(nc.sbuf_tensor("m_" + name, shape, dt))
        names = ["loaded", "steps", "rows", "turned", "xt", "xz", "conv", "exps", "xc", "dbc", "dbc_out", "spread_w",
                 "spread", "dt", "soft_in", "soft_out", "dt_ready", "decay", "inflow", "states", "sums", "y", "made",
                 "yout", "stored", "alog", "scanned", "states_pool", "pace"]
        sems = {n: nc.alloc_semaphore("m_" + n) for n in names}
        w_in, w_out, w_x = sb("win", [P, 2, 2 * F]), sb("wout", [P, 2, F]), sb("wx", [P, 2, R + 2 * NS])
        w_dt = sb("wdt", [R, F])
        cw, cb, db, dp = sb("cw", [P, 2, 4]), sb("cb", [P, 2]), sb("db", [P, 2]), sb("dp", [P, 2])
        a = sb("a", [P, 2, NS])
        xs, xst = sb("xs", [P, F]), sb("xst", [P, 2, P])
        seq = sb("seq", [P, 2, P + 3])
        cv, ex, ez = sb("cv", [P, 2, P]), sb("ex", [P, 2, P]), sb("ez", [P, 2, P])
        xc, zz = sb("xc", [P, 2, 2 * P]), sb("zz", [P, 2, 2 * P])
        zr = sb("zr", [P, 2, P])
        dbc = sb("dbc", [R + 2 * NS, P])
        bc = sb("bc", [P, 2, 2 * NS * P])
        u, dt, dtx, e, w1, d1, ln, z0 = (sb(n, [P, 2 * P]) for n in ("u", "dt", "dtx", "e", "w1", "d1", "ln", "z0"))
        da, dbx, hs = (sb(n, [P, 2, NS, P]) for n in ("da", "dbx", "hs"))
        last, carry = sb("last", [P, 2, NS]), sb("carry", [P, 2, NS])
        y, yr = sb("y", [P, 2, P]), sb("yr", [P, F])
        bank = [ctx.enter_context(nc.psum_tensor(f"m_ps{k}", [P, 512], F32)) for k in range(6)]
        ps_t = bank[0][:, 0:F].rearrange("p (k c) -> p k c", k=2)
        ps_xz = bank[1][:].rearrange("p (k c) -> p k c", k=4)
        ps_d = bank[2][0:R + 2 * NS, 0:P]
        ps_dt = bank[3][:, 0:F].rearrange("p (k c) -> p k c", k=2)
        ps_o = bank[4][:, 0:F]
        ps_y = bank[5][:, 0:F].rearrange("p (k c) -> p k c", k=2)
        block = ctx.enter_context(nc.Block())
        LOADS = 9

        def per_channel(vec):
            return vec.rearrange("(k p) -> p k", p=P)

        def parity(buf, t):
            return buf[:, t % 2, :] if isinstance(t, int) else \
                buf[:, bass.ds(t % 2, 1), :].rearrange("p a w -> p (a w)")

        def pipeline(eng, first, body):
            first()
            with eng.Fori(0, T - 2) as t:
                body(t, True, True)
            body(T - 2, True, False)
            body(T - 1, False, False)

        @block.sync
        def _(sp):
            with nc.allow_non_contiguous_dma(reason="one word per channel"):
                for dst, src in ((w_in, halves(io["in_proj"])), (w_out, halves(io["out_proj"])),
                                 (w_x, halves(io["x_proj"])), (w_dt, io["dt_proj"]),
                                 (cw, halves(io["L3_gnn_conv_w"])), (cb, per_channel(io["L3_gnn_conv_b"])),
                                 (db, per_channel(io["L3_gnn_dt_proj_b"])), (dp, per_channel(io["L3_gnn_D_param"])),
                                 (a, halves(io["L3_gnn_A_log"]))):
                    sp.dma_start(dst[:], src).then_inc(sems["loaded"], 16)

            def load_rows(t):
                if not (isinstance(t, int) and t == 0):
                    sp.wait_ge(sems["turned"], t)
                rows = dr["scan_x"][t * P:(t + 1) * P, :] if isinstance(t, int) else \
                    dr["scan_x"][bass.ds(t * P, P), :]
                sp.dma_start(xs[:], rows).then_inc(sems["rows"], 16)

            def spread(t):
                sp.wait_ge(sems["dbc_out"], t + 1)
                sp.dma_start(dr["bc"], dbc[R:R + 2 * NS, :]).then_inc(sems["spread_w"], 16)
                sp.wait_ge(sems["spread_w"], t * 16 + 16)
                sp.dma_start(parity(bc, t), on_all(dr["bc"].rearrange("a c -> (a c)"))).then_inc(sems["spread"], 16)

            def first():
                load_rows(0)
                spread(0)
                load_rows(1)

            def body(t, front, ahead):
                if front:
                    spread(t + 1)
                if ahead:
                    load_rows(t + 2)
                sp.wait_ge(sems["yout"], t + 2)
                rows = dr["scan_y"][t * P:(t + 1) * P, :] if isinstance(t, int) else \
                    dr["scan_y"][bass.ds(t * P, P), :]
                sp.dma_start(rows, yr[:]).then_inc(sems["stored"], 16)

            pipeline(sp, first, body)
            sp.wait_ge(sems["stored"], 16 * T + 16)

        @block.tensor
        def _(pe):
            pe.wait_ge(sems["loaded"], 16 * LOADS)

            def project(t):
                pe.wait_ge(sems["rows"], t * 16 + 16)
                transposed(pe, ps_t, xs, kp["ident"][:]).then_inc(sems["turned"], 1)
                pe.wait_ge(sems["xt"], t + 1)
                for m in range(4):
                    for k in range(2):
                        ins = pe.matmul(ps_xz[:, m, :], w_in[:, k, m * P:(m + 1) * P], xst[:, k, :], start=k == 0,
                                        stop=k == 1)
                ins.then_inc(sems["xz"], 1)

            def front(t):
                pe.wait_ge(sems["xc"], t + 1)
                src = parity(xc, t)
                for k in range(2):
                    ins = pe.matmul(ps_d, w_x[:, k, :], src[:, k * P:(k + 1) * P], start=k == 0, stop=k == 1)
                ins.then_inc(sems["dbc"], 1)
                pe.wait_ge(sems["dbc_out"], t + 1)
                for k in range(2):
                    ins = pe.matmul(ps_dt[:, k, :], w_dt[:, k * P:(k + 1) * P], dbc[0:R, :], start=True, stop=True)
                ins.then_inc(sems["dt"], 1)

            def first():
                project(0)
                front(0)
                project(1)

            def body(t, has_front, ahead):
                if has_front:
                    front(t + 1)
                if ahead:
                    project(t + 2)
                for k in range(2):
                    pe.wait_ge(sems["states" if k else "states_pool"], t + 1)
                    for n in range(NS):
                        ins = pe.matmul(ps_y[:, k, :], kp["ident"][:], hs[:, k, n, :], start=n == 0, stop=n == NS - 1)
                    ins.then_inc(sems["sums"], 1)
                pe.wait_ge(sems["y"], t + 2)
                pe.wait_ge(sems["yout"], t + 1)
                for k in range(2):
                    ins = pe.matmul(ps_o, y[:, k, :], w_out[:, k, :], start=k == 0, stop=k == 1)
                ins.then_inc(sems["made"], 1)

            pipeline(pe, first, body)

        @block.scalar
        def _(act):
            act.sem_inc(sems["stored"], 16)
            act.sem_inc(sems["yout"], 1)
            act.wait_ge(sems["loaded"], 16 * LOADS)
            act.activation(a[:], a[:], ACT.Exp).then_inc(sems["alog"], 1)

            def turn(t):
                act.wait_ge(sems["turned"], t + 1)
                act.activation(xst[:], ps_t, ACT.Copy).then_inc(sems["xt"], 1)

            def exps(t):
                act.wait_ge(sems["conv"], t + 1)
                act.activation(ex[:], cv[:], ACT.Sigmoid).then_inc(sems["exps"], 1)
                act.activation(ez[:], zr[:], ACT.Sigmoid).then_inc(sems["exps"], 1)

            def decay(k):
                for n in range(NS):
                    ins = act.activation(da[:, k, n, :], dt[:, k * P:(k + 1) * P], ACT.Exp, scale=a[:, k, n:n + 1])
                ins.then_inc(sems["decay"], 1)

            def front(t, ahead):
                act.wait_ge(sems["soft_in"], t * 2 + 1)
                act.activation(e[:], d1[:], ACT.Exp, scale=-1.0).then_inc(sems["soft_out"], 1)
                act.wait_ge(sems["soft_in"], t * 2 + 2)
                act.activation(ln[:], w1[:], ACT.Ln).then_inc(sems["soft_out"], 1)
                if ahead:
                    turn(t + 1)
                act.wait_ge(sems["dt_ready"], t + 1)
                decay(0)
                if ahead:
                    exps(t + 1)
                decay(1)

            def first():
                turn(0)
                exps(0)
                front(0, True)

            def body(t, has_front, ahead):
                if has_front:
                    front(t + 1, ahead)
                act.wait_ge(sems["made"], t + 1)
                act.wait_ge(sems["stored"], t * 16 + 16)
                act.activation(yr[:], ps_o, ACT.Copy).then_inc(sems["yout"], 1)

            pipeline(act, first, body)

        @block.gpsimd
        def _(pool):
            def front(t):
                pool.wait_ge(sems["dt_ready"], t + 1)
                pool.sem_inc(sems["inflow"], 1)
                pool.wait_ge(sems["spread"], t * 16 + 16)
                pool.sem_inc(sems["inflow"], 1)
                for k in range(2):
                    b_rows = parity(bc, t)[:, 0:NS * P].rearrange("p (n c) -> p n c", n=NS)
                    nc.gpsimd.tensor_tensor(dbx[:, k, :, :], over_slots(dtx[:, k * P:(k + 1) * P], NS), b_rows,
                                            ALU.mult).then_inc(sems["inflow"], 1)

            def body(t, has_front, ahead):
                pool.wait_ge(sems["scanned"], t + 1)
                pool.sem_inc(sems["pace"], 1)
                c_rows = parity(bc, t)[:, NS * P:2 * NS * P].rearrange("p (n c) -> p n c", n=NS)
                nc.gpsimd.tensor_tensor(hs[:, 0, :, :], hs[:, 0, :, :], c_rows, ALU.mult
                                        ).then_inc(sems["states_pool"], 1)
                if has_front:
                    front(t + 1)

            pipeline(pool, lambda: front(0), body)

        @block.vector
        def _(v):
            START, PER, CONV = 38, 37, 11
            st = Steps(v, sems["steps"])
            st.add(v.memset(seq[:], 0.0))
            st.add(v.memset(last[:], 0.0))
            v.sem_inc(sems["y"], 1)
            v.wait_ge(sems["alog"], 1)
            st.add(v.tensor_scalar(a[:], a[:], -1.0, None, ALU.mult))
            st.wait()

            def front_conv(st, t):
                st.do(v.tensor_copy(seq[:, :, 0:3], seq[:, :, P:P + 3]))
                v.wait_ge(sems["xz"], t + 1)
                st.do(v.tensor_copy(seq[:, :, 3:P + 3], ps_xz[:, 0:2, :]))
                st.add(v.tensor_copy(zr[:], ps_xz[:, 2:4, :]))
                for j in range(4):
                    for k in range(2):
                        if j == 0:
                            ins = v.tensor_scalar(cv[:, k, :], seq[:, k, 0:P], cw[:, k, 0:1], cb[:, k:k + 1], ALU.mult,
                                                  ALU.add)
                        else:
                            ins = v.scalar_tensor_tensor(cv[:, k, :], seq[:, k, j:j + P], cw[:, k, j:j + 1],
                                                         cv[:, k, :], ALU.mult, ALU.add)
                        st.add(ins)
                    st.wait()
                v.sem_inc(sems["conv"], 1)

            def front_gates(st, t):
                v.wait_ge(sems["exps"], t * 2 + 1)
                v.tensor_tensor(parity(xc, t), cv[:].rearrange("p k c -> p (k c)"), ex[:].rearrange("p k c -> p (k c)"),
                                ALU.mult).then_inc(sems["xc"], 1)
                v.wait_ge(sems["exps"], t * 2 + 2)
                if not (isinstance(t, int) and t == 0):
                    v.wait_ge(sems["y"], t)
                st.add(v.tensor_tensor(parity(zz, t), zr[:].rearrange("p k c -> p (k c)"),
                                       ez[:].rearrange("p k c -> p (k c)"), ALU.mult))

            def front_project(t):
                v.wait_ge(sems["dbc"], t + 1)
                if not (isinstance(t, int) and t == 0):
                    v.wait_ge(sems["spread_w"], t * 16)
                v.tensor_copy(dbc[:], ps_d).then_inc(sems["dbc_out"], 1)

            def front_soft_in(st, t):
                v.wait_ge(sems["dt"], t + 1)
                for k in range(2):
                    st.add(v.tensor_scalar(u[:, k * P:(k + 1) * P], ps_dt[:, k, :], db[:, k:k + 1], None, ALU.add))
                st.wait()
                st.do(v.scalar_tensor_tensor(d1[:], u[:], -1.0, u[:], ALU.mult, ALU.max))
                v.sem_inc(sems["soft_in"], 1)

            def front_soft_ln(st, t):
                v.wait_ge(sems["soft_out"], t * 2 + 1)
                v.tensor_scalar(w1[:], e[:], 1.0, None, ALU.add).then_inc(sems["soft_in"], 1)
                v.wait_ge(sems["soft_in"], t * 2 + 2)
                st.do(v.tensor_scalar(d1[:], w1[:], -1.0, None, ALU.add))
                st.do(v.tensor_scalar(z0[:], d1[:], 0.0, None, ALU.is_equal))
                st.do(v.tensor_tensor(d1[:], d1[:], z0[:], ALU.add))
                st.do(v.reciprocal(d1[:], d1[:]))

            def front_soft_out(st, t):
                v.wait_ge(sems["soft_out"], t * 2 + 2)
                st.do(v.tensor_tensor(d1[:], d1[:], ln[:], ALU.mult))
                st.do(v.tensor_tensor(d1[:], d1[:], z0[:], ALU.add))
                st.do(v.tensor_tensor(d1[:], d1[:], e[:], ALU.mult))
                st.do(v.scalar_tensor_tensor(dt[:], u[:], 0.0, d1[:], ALU.max, ALU.add))
                st.do(v.tensor_tensor(dtx[:], dt[:], parity(xc, t), ALU.mult))
                v.sem_inc(sems["dt_ready"], 1)

            def scan(st, t, k):
                v.wait_ge(sems["decay"], t * 2 + k + 1)
                v.wait_ge(sems["inflow"], t * 4 + k + 3)
                if not (isinstance(t, int) and t == 0):
                    v.wait_ge(sems["sums"], t * 2)
                st.do(v.tensor_tensor(carry[:, k, :], da[:, k, :, 0], last[:, k, :], ALU.mult))
                st.add(v.tensor_tensor(dbx[:, k, :, 0], dbx[:, k, :, 0], carry[:, k, :], ALU.add))
                st.add(v.memset(da[:, k, :, 0], 0.0))
                st.wait()
                st.do(v.tensor_tensor_scan(hs[:, k, :, :].rearrange("p n c -> p (n c)"),
                                           da[:, k, :, :].rearrange("p n c -> p (n c)"),
                                           dbx[:, k, :, :].rearrange("p n c -> p (n c)"), 0.0, ALU.mult, ALU.add))
                st.do(v.tensor_copy(last[:, k, :], hs[:, k, :, P - 1]))

            def outflow(st, t, k):
                c_rows = parity(bc, t)[:, NS * P:2 * NS * P].rearrange("p (n c) -> p n c", n=NS)
                st.do(v.tensor_tensor(hs[:, k, :, :], hs[:, k, :, :], c_rows, ALU.mult))
                v.sem_inc(sems["states"], 1)

            def finish_y(st, t):
                v.wait_ge(sems["sums"], t * 2 + 2)
                for k in range(2):
                    st.add(v.scalar_tensor_tensor(y[:, k, :], parity(xc, t)[:, k * P:(k + 1) * P], dp[:, k:k + 1],
                                                  ps_y[:, k, :], ALU.mult, ALU.add))
                st.wait()
                v.tensor_tensor(y[:].rearrange("p k c -> p (k c)"), y[:].rearrange("p k c -> p (k c)"), parity(zz, t),
                                ALU.mult).then_inc(sems["y"], 1)

            def first():
                front_conv(st, 0)
                front_gates(st, 0)
                front_project(0)
                front_soft_in(st, 0)
                front_soft_ln(st, 0)
                front_soft_out(st, 0)
                front_conv(st, 1)
                assert st.n == START, ("scan", "START", st.n)

            def body(t, front, ahead):
                st = Steps(v, sems["steps"], START + t * PER - (0 if front else CONV))
                if front:
                    front_gates(st, t + 1)
                    front_project(t + 1)
                scan(st, t, 0)
                v.sem_inc(sems["scanned"], 1)
                if front:
                    front_soft_in(st, t + 1)
                    front_soft_ln(st, t + 1)
                scan(st, t, 1)
                if front:
                    front_soft_out(st, t + 1)
                outflow(st, t, 1)
                if ahead:
                    front_conv(st, t + 2)
                finish_y(st, t)
                assert not front or st.n == PER - (0 if ahead else CONV), ("scan", "PER", st.n)

            pipeline(v, first, body)
    finish(nc, list(sems.values()))


def join(nc, io, dr, kp, result):
    B = 5
    assert T % B == 0 and (B * P) % 2 == 0
    W = B * P // 2
    with ExitStack() as ctx:
        def sb(name, shape, dt=F32):
            return ctx.enter_context(nc.sbuf_tensor("j_" + name, shape, dt))
        names = ["loaded", "steps", "gathered", "gmax_in", "gmax_turned", "gmax_row", "gmax_spread", "top_ready",
                 "top_exp", "elu_in", "elu_exp", "variance", "root", "turn", "turned", "copied", "gate", "gate_open",
                 "hidden", "relu", "forward", "out_ready", "written", "pace"]
        sems = {n: nc.alloc_semaphore("j_" + n) for n in names}
        vectors = ["gat_b", "ln_local_g", "ln_local_b", "ln_global_g", "ln_global_b", "ln2_g", "ln2_b"]
        vec = {n: sb("v_" + n, [P, F]) for n in vectors}
        wl, wg = sb("wl", [P, 2, F]), sb("wg", [P, 2, F])
        w1, w2 = sb("w1", [P, 2, 2 * F]), sb("w2", [P, 4, F])
        b1, b2 = sb("b1", [P, 4]), sb("b2", [1, F])
        fac = sb("fac", [P, T, 4])
        gm, grow, gall = sb("gm", [P, 1]), sb("grow", [1, 1]), sb("gall", [P, 1])
        stats, moments = sb("stats", [P, B, 6]), sb("moments", [P, B, 2])
        var, root, inv = sb("var", [P, B]), sb("root", [P, B]), sb("inv", [P, B])
        u, ev, hl, ha, g, h, o = (sb(n, [P, B, F]) for n in ("u", "ev", "hl", "ha", "g", "h", "o"))
        hlt, hat, ht = (sb(n, [P, 2, B * P]) for n in ("hlt", "hat", "ht"))
        ft = sb("ft", [P, 4, B * P])
        node, spare = sb("node", [P, B], I32), sb("spare", [1, 4], I32)
        region = [ctx.enter_context(nc.psum_tensor(f"j_ps{k}", [P, 6, F], F32)) for k in range(2)]
        hidden = ctx.enter_context(nc.psum_tensor("j_ps2", [P, 2, 512], F32))
        block = ctx.enter_context(nc.Block())
        LOADS = len(vectors) + 6

        @block.sync
        def _(sp):
            for n in vectors:
                sp.dma_start(vec[n][:], on_all(io["L3_gnn_" + n])).then_inc(sems["loaded"], 16)
            with nc.allow_non_contiguous_dma(reason="one word per hidden unit"):
                sp.dma_start(b1[:], io["L3_gnn_ff1_b"].rearrange("(m p) -> p m", p=P)).then_inc(sems["loaded"], 16)
            for dst, src in ((wl, halves(io["wl"])), (wg, halves(io["wg"])), (w1, halves(io["ff1"])),
                             (w2, halves(io["ff2"])), (b2, rows_of(io["L3_gnn_ff2_b"]))):
                sp.dma_start(dst[:], src).then_inc(sems["loaded"], 16)

        @block.gpsimd
        def _(pool):
            for t in range(T):
                pool.indirect_dma_start(out=kp["b"][:, t, :], out_offset=None, in_=dr["scan_y"],
                                        in_offset=bass.IndirectOffsetOnAxis(ap=kp["info"][:, t, 3:4], axis=0),
                                        bounds_check=NP - 1, oob_is_err=False).then_inc(sems["gathered"], 16)
            prime(pool, dr, spare, sems["written"])
            with pool.Fori(0, T // B) as i:
                pool.wait_ge(sems["out_ready"], i + 1)
                pool.sem_inc(sems["pace"], 1)
                for j in range(B):
                    pool.indirect_dma_start(out=result, in_=o[:, j, :], in_offset=None,
                                            out_offset=bass.IndirectOffsetOnAxis(ap=node[:, j:j + 1], axis=0),
                                            bounds_check=N - 1, oob_is_err=False).then_inc(sems["written"], 16)
            pool.wait_ge(sems["written"], 16 * T + 16)

        @block.tensor
        def _(pe):
            ident, ones = kp["ident"][:], kp["ones"][:, :]
            pe.wait_ge(sems["loaded"], 16 * LOADS)
            pe.wait_ge(sems["gmax_in"], 1)
            pe.transpose(region[0][0:1, 0, 0:P], gm[:], ident).then_inc(sems["gmax_turned"], 1)
            pe.wait_ge(sems["gmax_row"], 1)
            pe.matmul(region[1][:, 0, 0:1], ones, grow[:], start=True, stop=True).then_inc(sems["gmax_spread"], 1)

            def turn(dst, src):
                for j in range(B):
                    for k in range(2):
                        ins = pe.transpose(dst[:, j, k * P:(k + 1) * P], src[:, j, k * P:(k + 1) * P], ident)
                ins.then_inc(sems["turned"], 1)

            with pe.Fori(0, T // B) as i:
                pe.wait_ge(sems["turn"], i * 3 + 1)
                turn(region[0], hl)
                pe.wait_ge(sems["turn"], i * 3 + 2)
                turn(region[1], ha)
                pe.wait_ge(sems["copied"], i * 3 + 2)
                for j in range(B):
                    ps = region[0][:, j, :]
                    at = slice(j * P, (j + 1) * P)
                    product(pe, ps, hlt[:, :, at], wl, stop=False)
                    ins = product(pe, ps, hat[:, :, at], wg, start=False)
                ins.then_inc(sems["gate"], 1)
                pe.wait_ge(sems["turn"], i * 3 + 3)
                turn(region[1], h)
                pe.wait_ge(sems["copied"], i * 3 + 3)
                for m in range(4):
                    for c in range(2):
                        pe.wait_ge(sems["relu"], i * 8 + m * 2 + c + 1)
                        for k in range(2):
                            ins = pe.matmul(hidden[:, c, 0:W], w1[:, k, m * P:(m + 1) * P],
                                            ht[:, k, c * W:(c + 1) * W], start=k == 0, stop=k == 1)
                        ins.then_inc(sems["hidden"], 1)
                pe.wait_ge(sems["relu"], i * 8 + 10)
                for j in range(B):
                    ins = product(pe, region[1][:, j, :], ft[:, :, j * P:(j + 1) * P], w2, b2[:], ones)
                ins.then_inc(sems["forward"], 1)

        @block.scalar
        def _(act):
            act.sem_inc(sems["relu"], 2)
            act.wait_ge(sems["loaded"], 16 * LOADS)
            act.wait_ge(sems["top_ready"], 1)
            act.activation(fac[:], fac[:], ACT.Exp).then_inc(sems["top_exp"], 1)

            def copy_turned(i, n, dst, src):
                act.wait_ge(sems["turned"], i * 3 + n)
                act.activation(dst[:].rearrange("p k (j c) -> p j k c", j=B),
                               src[:, 0:B, :].rearrange("p j (k c) -> p j k c", k=2), ACT.Copy
                               ).then_inc(sems["copied"], 1)

            def take_root(i, n):
                act.wait_ge(sems["variance"], i * 4 + n)
                act.activation(root[:], var[:], ACT.Sqrt).then_inc(sems["root"], 1)

            with act.Fori(0, T // B) as i:
                act.wait_ge(sems["elu_in"], i + 1)
                act.activation(ev[:], ev[:], ACT.Exp).then_inc(sems["elu_exp"], 1)
                take_root(i, 1)
                take_root(i, 2)
                copy_turned(i, 1, hlt, region[0])
                copy_turned(i, 2, hat, region[1])
                act.wait_ge(sems["gate"], i + 1)
                act.activation(g[:], region[0][:, 0:B, :], ACT.Sigmoid).then_inc(sems["gate_open"], 1)
                copy_turned(i, 3, ht, region[1])
                for m in range(4):
                    for c in range(2):
                        act.wait_ge(sems["hidden"], i * 8 + m * 2 + c + 1)
                        act.activation(ft[:, m, c * W:(c + 1) * W], hidden[:, c, 0:W], ACT.Relu, bias=b1[:, m:m + 1]
                                       ).then_inc(sems["relu"], 1)
                take_root(i, 3)
                take_root(i, 4)

        @block.vector
        def _(v):
            BEFORE, PER = 4, 81
            st = Steps(v, sems["steps"])
            v.tensor_reduce(gm[:], kp["top"][:].rearrange("p t h -> p (t h)"), X, ALU.max).then_inc(sems["gmax_in"], 1)
            v.wait_ge(sems["gmax_turned"], 1)
            v.tensor_reduce(grow[:], region[0][0:1, 0, 0:P], X, ALU.max).then_inc(sems["gmax_row"], 1)
            v.wait_ge(sems["gmax_spread"], 1)
            st.do(v.tensor_copy(gall[:], region[1][:, 0, 0:1]))
            v.tensor_scalar(fac[:], kp["top"][:], gall[:], None, ALU.subtract).then_inc(sems["top_ready"], 1)
            v.wait_ge(sems["top_exp"], 1)
            st.do(v.tensor_tensor(kp["den"][:], kp["den"][:], fac[:], ALU.mult))
            st.do(v.tensor_scalar(kp["den"][:], kp["den"][:], 1e-16, None, ALU.add))
            st.do(v.reciprocal(kp["den"][:], kp["den"][:]))
            v.tensor_tensor(fac[:], fac[:], kp["den"][:], ALU.mult).then_inc(sems["top_ready"], 1)
            v.wait_ge(sems["top_ready"], 2)
            v.wait_ge(sems["loaded"], 16 * LOADS)
            v.wait_ge(sems["gathered"], 16 * T)

            def normalise(st, i, n, out, src, gain=None, offset=None, done=None):
                for j in range(B):
                    st.add(v.bn_stats(stats[:, j, :], src[:, j, :]))
                st.wait()
                v.sem_inc(sems["pace"], 1)
                for j in range(B):
                    st.add(v.bn_aggr(moments[:, j, :], stats[:, j, :]))
                st.wait()
                v.tensor_scalar(var[:], moments[:, :, 1], EPS, None, ALU.add).then_inc(sems["variance"], 1)
                v.wait_ge(sems["root"], i * 4 + n)
                st.do(v.reciprocal(inv[:], root[:]))
                for j in range(B):
                    st.add(v.tensor_scalar(out[:, j, :], src[:, j, :], moments[:, j, 0:1], inv[:, j:j + 1],
                                           ALU.subtract, ALU.mult))
                st.wait()
                if gain is not None:
                    st.do(v.tensor_tensor(out[:], out[:], over_slots(gain[:], B), ALU.mult))
                    st.do(v.tensor_tensor(out[:], out[:], over_slots(offset[:], B), ALU.add))
                if done is not None:
                    v.sem_inc(sems[done], 1)

            with v.Fori(0, T // B) as i:
                st = Steps(v, sems["steps"], BEFORE + i * PER)
                tiles = bass.ds(i * B, B)
                x_b = kp["x"][:, tiles, :]
                st.do(v.tensor_tensor(u[:].rearrange("p t (h d) -> p (t h) d", h=4),
                                      kp["a"][:, tiles, :].rearrange("p t (h d) -> p (t h) d", h=4),
                                      over_dims(fac[:, tiles, :].rearrange("p t h -> p (t h)"), F // 4), ALU.mult))
                st.do(v.tensor_tensor(u[:], u[:], x_b, ALU.add))
                st.do(v.tensor_tensor(u[:], u[:], over_slots(vec["gat_b"][:], B), ALU.add))
                v.tensor_scalar(ev[:], u[:], 0.0, None, ALU.min).then_inc(sems["elu_in"], 1)
                v.wait_ge(sems["elu_exp"], i + 1)
                st.do(v.scalar_tensor_tensor(u[:], u[:], 0.0, ev[:], ALU.max, ALU.add))
                st.do(v.tensor_scalar(u[:], u[:], -1.0, None, ALU.add))
                normalise(st, i, 1, hl, u, vec["ln_local_g"], vec["ln_local_b"], "turn")
                st.do(v.tensor_tensor(u[:], x_b, kp["b"][:, tiles, :], ALU.add))
                normalise(st, i, 2, ha, u, vec["ln_global_g"], vec["ln_global_b"], "turn")
                st.do(v.tensor_tensor(u[:], hl[:], ha[:], ALU.subtract))
                v.wait_ge(sems["gate_open"], i + 1)
                st.do(v.tensor_tensor(u[:], u[:], g[:], ALU.mult))
                v.tensor_tensor(h[:], u[:], ha[:], ALU.add).then_inc(sems["turn"], 1)
                v.wait_ge(sems["forward"], i + 1)
                st.do(v.tensor_tensor(u[:], h[:], region[1][:, 0:B, :], ALU.add))
                normalise(st, i, 3, h, u, vec["ln2_g"], vec["ln2_b"])
                st.do(v.tensor_tensor(h[:], h[:], x_b, ALU.add))
                v.wait_ge(sems["written"], i * (16 * B) + 16)
                st.add(v.tensor_copy(node[:], kp["info"][:, tiles, 0]))
                normalise(st, i, 4, o, h, done="out_ready")
                assert st.n == PER, st.n
    finish(nc, [sems[n] for n in names])


def network(nc, io, result):
    def scratch(name, shape, dt=F32):
        return nc.dram_tensor("scratch_" + name, shape, dt).ap()
    dr = {
        "indeg": scratch("indeg", (NP,)), "outdeg": scratch("outdeg", (NP,)), "starts": scratch("starts", (NP,)),
        "keys": scratch("keys", (NP,)), "info": scratch("info", (NP, 4), I32),
        "runs": scratch("runs", (E, 2 * RUN), I32), "slots": scratch("slots", (CHUNKS_MAX + 4 * T, P, META)),
        "kv": scratch("kv", (NP, 2 * F)), "messages": scratch("messages", (NP * RELS, F)),
        "gat1": scratch("gat1", (NP, F + 8)), "gat2": scratch("gat2", (NP, F + 1)),
        "gat3": scratch("gat3", (NP, F + 4)), "scan_x": scratch("scan_x", (NP, F)),
        "scan_y": scratch("scan_y", (NP, F)), "bc": scratch("bc", (32, P)),
    }
    count_edges(nc, io, dr)
    order_nodes(nc, io, dr)
    with ExitStack() as ctx:
        def sb(name, shape, dt=F32):
            return ctx.enter_context(nc.sbuf_tensor("k_" + name, shape, dt))
        kp = {
            "info": sb("info", [P, T, 4], I32), "x": sb("x", [P, T, F]), "a": sb("a", [P, T, F]),
            "b": sb("b", [P, T, F]), "er": sb("er", [P, T, 8]), "den": sb("den", [P, T, 4]),
            "top": sb("top", [P, T, 4]), "deg": sb("deg", [P, T]), "has_edges": sb("has", [P, T]),
            "inv_deg": sb("inv", [P, T]), "sched": sb("sched", [1, 5, 32], I32), "ident": sb("ident", [P, P]),
            "ones": sb("ones", [1, P]), "slot_no": sb("slotno", [P, S]),
            "counts": COUNTS,
        }
        fetch_nodes(nc, io, dr, kp)
        build_slots(nc, io, dr, kp)
        for name in ("conv", "messages", "rel", "gat1", "gat2", "gat3", "scan", "join"):
            if name == "messages":
                relation_messages(nc, io, dr, kp)
            elif name == "scan":
                state_scan(nc, io, dr, kp)
            elif name == "join":
                join(nc, io, dr, kp, result)
            else:
                edge_layer(nc, io, dr, kp, name)


COUNTS = {"conv": (12, 3, 4, 12, 0), "rel": (7, 1, 3, 4, 8), "gat1": (13, 4, 4, 4, 8),
          "gat2": (13, 4, 8, 4, 8), "gat3": (13, 4, 3, 0, 0)}

DIRECT = ["x", "src", "dst", "edge_type_32", "edge_weight1", "node_vec",
          "L0_gnn_Wq", "L0_gnn_bq", "L0_gnn_Wk", "L0_gnn_bk", "L0_gnn_Wv", "L0_gnn_bv", "L0_gnn_Wskip", "L0_gnn_bskip",
          "L0_gnn_gamma", "L0_gnn_beta", "L1_gnn_bases", "L1_gnn_w_comp", "L2_gnn_attn_l1", "L2_gnn_attn_r1",
          "L2_gnn_bias1", "L2_gnn_attn_l2", "L2_gnn_attn_r2", "L2_gnn_bias2", "L2_gnn_bb0", "L2_gnn_bb1",
          "L3_gnn_gat_a_src", "L3_gnn_gat_a_tgt", "L3_gnn_gat_b", "L3_gnn_ln_local_g", "L3_gnn_ln_local_b",
          "L3_gnn_ln_global_g", "L3_gnn_ln_global_b", "L3_gnn_ln2_g", "L3_gnn_ln2_b", "L3_gnn_conv_w",
          "L3_gnn_conv_b", "L3_gnn_dt_proj_b", "L3_gnn_A_log", "L3_gnn_D_param", "L3_gnn_ff1_b", "L3_gnn_ff2_b"]
TURNED = {"fc1": "L2_gnn_fc1_w", "fc2": "L2_gnn_fc2_w", "wb0": "L2_gnn_wb0", "gat": "L3_gnn_gat_w",
          "in_proj": "L3_gnn_in_proj_w", "x_proj": "L3_gnn_x_proj_w", "dt_proj": "L3_gnn_dt_proj_w",
          "out_proj": "L3_gnn_out_proj_w", "wl": "L3_gnn_wl", "wg": "L3_gnn_wg", "ff1": "L3_gnn_ff1_w",
          "ff2": "L3_gnn_ff2_w"}


def kernel(**inputs):
    import numpy as np
    import concourse.bacc as bacc
    from concourse.bass_utils import run_bass_kernel_spmd

    nc = bacc.Bacc("TRN2", target_bir_lowering=False, num_devices=1)
    arrays = {n: np.ascontiguousarray(inputs[n]) for n in DIRECT}
    arrays.update({n: np.ascontiguousarray(np.asarray(inputs[src]).T) for n, src in TURNED.items()})
    both = np.asarray(inputs["L2_gnn_wb1"]).T
    arrays["wb1a"], arrays["wb1b"] = np.ascontiguousarray(both[:F]), np.ascontiguousarray(both[F:])
    io = {n: nc.dram_tensor("in_" + n, a.shape, mybir.dt.from_np(a.dtype), kind="ExternalInput").ap()
          for n, a in arrays.items()}
    result = nc.dram_tensor("out_x", (N, F), F32, kind="ExternalOutput").ap()
    network(nc, io, result)
    r = run_bass_kernel_spmd(nc, [{"in_" + n: a for n, a in arrays.items()}], core_ids=[0])
    return r.results[0]["out_x"]
```
